# Optimizing a Trainium2 kernel written in Bass

```python
import numpy as np
import jax
import jax.numpy as jnp

def _softmax(x, axis=-1):
    return jax.nn.softmax(x, axis=axis)

def _gelu(x):
    return jax.nn.gelu(x, approximate=True)

def _silu(x):
    return jax.nn.silu(x)

def _sigmoid(x):
    return jax.nn.sigmoid(x)

def _layernorm(x, axis=-1, eps=1e-05):
    m = jnp.mean(x, axis=axis, keepdims=True)
    v = jnp.var(x, axis=axis, keepdims=True)
    return (x - m) / jnp.sqrt(v + eps)

def _scatter_add(tgt, idx, src, axis=0):
    return tgt.at[idx].add(src)

def _segment_sum(src, seg, n):
    return jax.ops.segment_sum(src, seg, n)
kernel_name = 'mk_xattn_ffn_d4_seqx_r8_e30cd0'

def setup_inputs(seed: int=0):
    np.random.seed(seed)
    _w = jnp.asarray

    def _rec_inputs():
        import jax
        import jax.numpy as jnp
        _rk = jax.random.key(seed)
        x = -0.0002928 + 1 * jax.random.normal(jax.random.fold_in(_rk, 1), (4, 256, 128), jnp.float32)
        _lenS = 256 - jax.random.randint(jax.random.fold_in(_rk, 7), (4,), 0, max(1, 256 // 4) + 1, jnp.int32)
        _lenS2 = 1601 - jax.random.randint(jax.random.fold_in(_rk, 8), (4,), 0, max(1, 1601 // 4) + 1, jnp.int32)
        _ctx_1024P = jax.random.normal(jax.random.fold_in(_rk, 11), (4, 16, 128), jnp.float32)
        _ctx_1024c = jax.random.dirichlet(jax.random.fold_in(_rk, 511), 0.3 * jnp.ones((16,), jnp.float32), (4, 1601))
        _ctx_1024t = jnp.einsum('bsk,bkd->bsd', _ctx_1024c, _ctx_1024P)
        _ctx_1024t = _ctx_1024t * jax.lax.rsqrt(jnp.mean(jnp.square(_ctx_1024t)) + 1e-12) * 0.953939
        ctx_1024 = -1.39393e-06 + 0.999914 * (_ctx_1024t + 0.3 * jax.random.normal(jax.random.fold_in(_rk, 611), (4, 1601, 128), jnp.float32))
        _validS = jnp.arange(256)[None, :] < _lenS[:, None]
        _validS2 = jnp.arange(1601)[None, :] < _lenS2[:, None]
        _causal = jnp.tril(jnp.ones((256, 256), dtype=bool))
        mask_SxS2_fk1 = jnp.where(jnp.broadcast_to(_validS2[0:1, :], (256, 1601)), 1.0, 0.0).astype(jnp.float32)
        mask_1x1xSxS2_ik0 = jnp.where(jnp.broadcast_to(_validS2[0:1, None, None, :], (1, 1, 256, 1601)), 0, 1).astype(jnp.int32)
        return (x, ctx_1024, mask_SxS2_fk1, mask_1x1xSxS2_ik0)
    x, ctx_1024, mask_SxS2_fk1, mask_1x1xSxS2_ik0 = _rec_inputs()

    def _L0_xattn_setup():
        import jax, jax.numpy as jnp
        import numpy as np
        D_MODEL = 128
        NUM_HEADS = 16
        D_K = D_MODEL // NUM_HEADS
        B, S = (2, 256)
        NEG = -1000000000.0

        def _split_heads(x):
            b, s, _ = x.shape
            return x.reshape(b, s, NUM_HEADS, D_K).transpose(0, 2, 1, 3)
        key = jax.random.key(seed)
        ks = jax.random.split(key, 12)
        sc = 1.0 / np.sqrt(D_MODEL)
        inp = {'Q': jax.random.normal(ks[0], (B, S, D_MODEL), jnp.float32), 'K': jax.random.normal(ks[1], (B, S, D_MODEL), jnp.float32), 'V': jax.random.normal(ks[2], (B, S, D_MODEL), jnp.float32), 'mask': jnp.triu(jnp.ones((S, S), jnp.float32), k=1), 'Wq': jax.random.normal(ks[3], (D_MODEL, D_MODEL), jnp.float32) * sc, 'bq': jnp.zeros((D_MODEL,), jnp.float32), 'Wk': jax.random.normal(ks[4], (D_MODEL, D_MODEL), jnp.float32) * sc, 'bk': jnp.zeros((D_MODEL,), jnp.float32), 'Wv': jax.random.normal(ks[5], (D_MODEL, D_MODEL), jnp.float32) * sc, 'bv': jnp.zeros((D_MODEL,), jnp.float32), 'Wo': jax.random.normal(ks[6], (D_MODEL, D_MODEL), jnp.float32) * sc, 'bo': jnp.zeros((D_MODEL,), jnp.float32)}
        return inp
    _L0_xattn_all = _L0_xattn_setup()
    _L0_xattn_in = {k: v for k, v in _L0_xattn_all.items() if k in ('Wq', 'bq', 'Wk', 'bk', 'Wv', 'bv', 'Wo', 'bo')}
    del _L0_xattn_all

    def _L0_ffn_setup():
        import jax, jax.numpy as jnp
        import numpy as np
        HIDDEN = 128
        INNER = 512

        def _weight_quant(w):
            scale = 1.0 / jnp.clip(jnp.mean(jnp.abs(w)), 1e-05)
            wq = jnp.clip(jnp.round(w * scale), -1.0, 1.0) / scale
            return w + jax.lax.stop_gradient(wq - w)

        def _act_quant(x):
            scale = 127.0 / jnp.clip(jnp.max(jnp.abs(x), axis=-1, keepdims=True), 1e-05)
            xq = jnp.clip(jnp.round(x * scale), -128.0, 127.0) / scale
            return x + jax.lax.stop_gradient(xq - x)

        def _bitlinear(x, w):
            return jnp.einsum('bsi,oi->bso', _act_quant(x), _weight_quant(w))
        key = jax.random.key(seed)
        k0, k1, k2, k3 = jax.random.split(key, 4)
        x = jax.random.normal(k0, (4, 256, HIDDEN), dtype=jnp.float32)
        w_gate = jax.random.normal(k1, (INNER, HIDDEN), dtype=jnp.float32) / np.sqrt(HIDDEN)
        w_up = jax.random.normal(k2, (INNER, HIDDEN), dtype=jnp.float32) / np.sqrt(HIDDEN)
        w_down = jax.random.normal(k3, (HIDDEN, INNER), dtype=jnp.float32) / np.sqrt(INNER)
        return {'x': x, 'w_gate': w_gate, 'w_up': w_up, 'w_down': w_down}
    _L0_ffn_all = _L0_ffn_setup()
    _L0_ffn_in = {k: v for k, v in _L0_ffn_all.items() if k in ('w_gate', 'w_up', 'w_down')}
    del _L0_ffn_all

    def _L1_xattn_setup():
        import jax, jax.numpy as jnp
        import numpy as np
        D_MODEL = 128
        B, S = (4, 256)
        key = jax.random.key(seed)
        ks = jax.random.split(key, 10)
        s = 1.0 / np.sqrt(D_MODEL)
        return {'k': jax.random.normal(ks[0], (B, S, D_MODEL), jnp.float32), 'v': jax.random.normal(ks[1], (B, S, D_MODEL), jnp.float32), 'q': jax.random.normal(ks[2], (B, S, D_MODEL), jnp.float32), 'Wk': jax.random.normal(ks[3], (D_MODEL, D_MODEL), jnp.float32) * s, 'Wv': jax.random.normal(ks[4], (D_MODEL, D_MODEL), jnp.float32) * s, 'bv': jnp.zeros((D_MODEL,), jnp.float32), 'Wq': jax.random.normal(ks[5], (D_MODEL, D_MODEL), jnp.float32) * s, 'bq': jnp.zeros((D_MODEL,), jnp.float32), 'Wo': jax.random.normal(ks[6], (D_MODEL, D_MODEL), jnp.float32) * s, 'bo': jnp.zeros((D_MODEL,), jnp.float32)}
    _L1_xattn_all = _L1_xattn_setup()
    _L1_xattn_in = {k: v for k, v in _L1_xattn_all.items() if k in ('Wk', 'Wv', 'bv', 'Wq', 'bq', 'Wo', 'bo')}
    del _L1_xattn_all

    def _L1_ffn_setup():
        import jax, jax.numpy as jnp
        import numpy as np
        B, N, D, H, E = (4, 128, 128, 16, 8)
        DK = D // H
        HID = 4 * D
        EPS = 1e-05

        def _layernorm(x, w, b):
            m = jnp.mean(x, axis=-1, keepdims=True)
            v = jnp.mean(jnp.square(x - m), axis=-1, keepdims=True)
            return (x - m) * jax.lax.rsqrt(v + EPS) * w + b

        def _msa(x, w_qkv, w_proj):
            b, n, d = x.shape
            qkv = (x @ w_qkv).reshape(b, n, 3, H, DK)
            q = qkv[:, :, 0].transpose(0, 2, 1, 3)
            k = qkv[:, :, 1].transpose(0, 2, 1, 3)
            v = qkv[:, :, 2].transpose(0, 2, 1, 3)
            attn = jnp.einsum('bhnd,bhmd->bhnm', q, k) * (1.0 / np.sqrt(DK))
            attn = jax.nn.softmax(attn, axis=-1)
            y = jnp.einsum('bhnm,bhmd->bhnd', attn, v)
            y = y.transpose(0, 2, 1, 3).reshape(b, n, d)
            return y @ w_proj

        def _moe_mlp(x, gate_w, gate_b, w1, w2):
            b, n, d = x.shape
            xf = x.reshape(b * n, d)
            logits = xf @ gate_w + gate_b
            one_hot = jax.nn.one_hot(jnp.argmax(logits, axis=-1), E, dtype=xf.dtype)
            h = jax.nn.gelu(jnp.einsum('td,edh->teh', xf, w1), approximate=True)
            y = jnp.einsum('teh,ehd->ted', h, w2)
            out = jnp.einsum('te,ted->td', one_hot, y)
            return out.reshape(b, n, d)
        key = jax.random.key(seed)
        ks = jax.random.split(key, 8)
        s = 0.02
        return {'x': jax.random.normal(ks[0], (B, N, D), jnp.float32), 'ln1_w': jnp.ones((D,), jnp.float32), 'ln1_b': jnp.zeros((D,), jnp.float32), 'w_qkv': jax.random.normal(ks[1], (D, 3 * D), jnp.float32) * s, 'w_proj': jax.random.normal(ks[2], (D, D), jnp.float32) * s, 'ln2_w': jnp.ones((D,), jnp.float32), 'ln2_b': jnp.zeros((D,), jnp.float32), 'gate_w': jax.random.normal(ks[3], (D, E), jnp.float32) * s, 'gate_b': jnp.zeros((E,), jnp.float32), 'w1': jax.random.normal(ks[4], (E, D, HID), jnp.float32) * s, 'w2': jax.random.normal(ks[5], (E, HID, D), jnp.float32) * s}
    _L1_ffn_all = _L1_ffn_setup()
    _L1_ffn_in = {k: v for k, v in _L1_ffn_all.items() if k in ('ln1_w', 'ln1_b', 'w_qkv', 'w_proj', 'ln2_w', 'ln2_b', 'gate_w', 'gate_b', 'w1', 'w2')}
    del _L1_ffn_all

    def _L2_xattn_setup():
        import jax, jax.numpy as jnp
        import numpy as np
        HIDDEN = 128
        HEADS = 16
        HEAD_DIM = 64
        key = jax.random.key(seed)
        ks = jax.random.split(key, 7)
        B, Q, K = (2, 256, 512)
        s = 1.0 / np.sqrt(HIDDEN)
        return {'query': jax.random.normal(ks[0], (B, Q, HIDDEN), dtype=jnp.float32), 'key': jax.random.normal(ks[1], (B, K, HIDDEN), dtype=jnp.float32), 'value': jax.random.normal(ks[2], (B, K, HIDDEN), dtype=jnp.float32), 'w_q': jax.random.normal(ks[3], (HIDDEN, HEADS * HEAD_DIM), dtype=jnp.float32) * s, 'w_k': jax.random.normal(ks[4], (HIDDEN, HEADS * HEAD_DIM), dtype=jnp.float32) * s, 'w_v': jax.random.normal(ks[5], (HIDDEN, HEADS * HEAD_DIM), dtype=jnp.float32) * s, 'w_o': jax.random.normal(ks[6], (HEADS * HEAD_DIM, HIDDEN), dtype=jnp.float32) * s}
    _L2_xattn_all = _L2_xattn_setup()
    _L2_xattn_in = {k: v for k, v in _L2_xattn_all.items() if k in ('w_q', 'w_k', 'w_v', 'w_o')}
    del _L2_xattn_all

    def _L2_ffn_setup():
        import jax, jax.numpy as jnp
        import numpy as np
        QMAX = 127.0

        def _ste_round(v):
            return v + jax.lax.stop_gradient(jnp.round(v) - v)

        def _act_fake_quant(x, clip_factor):
            scale = jax.nn.sigmoid(clip_factor) * jnp.max(jnp.abs(x)) / QMAX
            return jnp.clip(_ste_round(x / scale), -QMAX - 1.0, QMAX) * scale

        def _weight_fake_quant(w):
            scale = jnp.max(jnp.abs(w), axis=1, keepdims=True) / QMAX
            return jnp.clip(_ste_round(w / scale), -QMAX - 1.0, QMAX) * scale
        key = jax.random.key(seed)
        k1, k2, k3, k4 = jax.random.split(key, 4)
        B, S, H, I = (8, 1024, 128, 352)
        return {'x': jax.random.normal(k1, (B, S, H), dtype=jnp.float32), 'clip_x': jnp.full((1,), 4.0, dtype=jnp.float32), 'clip_down': jnp.full((1,), 4.0, dtype=jnp.float32), 'w_gate': jax.random.normal(k2, (I, H), dtype=jnp.float32) * 0.02, 'w_up': jax.random.normal(k3, (I, H), dtype=jnp.float32) * 0.02, 'w_down': jax.random.normal(k4, (H, I), dtype=jnp.float32) * 0.02}
    _L2_ffn_all = _L2_ffn_setup()
    _L2_ffn_in = {k: v for k, v in _L2_ffn_all.items() if k in ('clip_x', 'clip_down', 'w_gate', 'w_up', 'w_down')}
    del _L2_ffn_all

    def _L3_xattn_setup():
        import jax, jax.numpy as jnp
        import numpy as np
        EMBED_DIM = 128
        NUM_HEADS = 16
        HEAD_DIM = EMBED_DIM // NUM_HEADS
        B, S = (4, 256)

        def _split(x):
            b, s, _ = x.shape
            return x.reshape(b, s, NUM_HEADS, HEAD_DIM).transpose(0, 2, 1, 3)
        key = jax.random.key(seed)
        ks = jax.random.split(key, 12)
        s = 1.0 / np.sqrt(EMBED_DIM)
        inp = {'q': jax.random.normal(ks[0], (B, S, EMBED_DIM), jnp.float32), 'k': jax.random.normal(ks[1], (B, S, EMBED_DIM), jnp.float32), 'v': jax.random.normal(ks[2], (B, S, EMBED_DIM), jnp.float32), 'mask': jnp.tril(jnp.ones((S, S), jnp.int32))[None, None], 'Wq': jax.random.normal(ks[3], (EMBED_DIM, EMBED_DIM), jnp.float32) * s, 'bq': jax.random.normal(ks[4], (EMBED_DIM,), jnp.float32) * s, 'Wk': jax.random.normal(ks[5], (EMBED_DIM, EMBED_DIM), jnp.float32) * s, 'bk': jax.random.normal(ks[6], (EMBED_DIM,), jnp.float32) * s, 'Wv': jax.random.normal(ks[7], (EMBED_DIM, EMBED_DIM), jnp.float32) * s, 'bv': jax.random.normal(ks[8], (EMBED_DIM,), jnp.float32) * s, 'Wo': jax.random.normal(ks[9], (EMBED_DIM, EMBED_DIM), jnp.float32) * s, 'bo': jax.random.normal(ks[10], (EMBED_DIM,), jnp.float32) * s}
        return inp
    _L3_xattn_all = _L3_xattn_setup()
    _L3_xattn_in = {k: v for k, v in _L3_xattn_all.items() if k in ('Wq', 'bq', 'Wk', 'bk', 'Wv', 'bv', 'Wo', 'bo')}
    del _L3_xattn_all

    def _L3_ffn_setup():
        import jax, jax.numpy as jnp
        import numpy as np
        D_MODEL, D_FF, RANK = (128, 512, 32)
        B, S = (4, 512)
        key = jax.random.key(seed)
        ks = jax.random.split(key, 7)
        return {'x': jax.random.normal(ks[0], (B, S, D_MODEL), dtype=jnp.float32), 'U1': jax.random.normal(ks[1], (D_MODEL, RANK), dtype=jnp.float32) * 0.02, 'V1': jax.random.normal(ks[2], (RANK, D_FF), dtype=jnp.float32) * 0.02, 'b1': jnp.zeros((D_FF,), dtype=jnp.float32), 'U2': jax.random.normal(ks[3], (D_FF, RANK), dtype=jnp.float32) * 0.02, 'V2': jax.random.normal(ks[4], (RANK, D_MODEL), dtype=jnp.float32) * 0.02, 'b2': jnp.zeros((D_MODEL,), dtype=jnp.float32)}
    _L3_ffn_all = _L3_ffn_setup()
    _L3_ffn_in = {k: v for k, v in _L3_ffn_all.items() if k in ('U1', 'V1', 'b1', 'U2', 'V2', 'b2')}
    del _L3_ffn_all
    return {'x': x, 'ctx_1024': ctx_1024, 'mask_SxS2_fk1': mask_SxS2_fk1, 'mask_1x1xSxS2_ik0': mask_1x1xSxS2_ik0, 'L0_xattn_Wq': _L0_xattn_in['Wq'], 'L0_xattn_bq': _L0_xattn_in['bq'], 'L0_xattn_Wk': _L0_xattn_in['Wk'], 'L0_xattn_bk': _L0_xattn_in['bk'], 'L0_xattn_Wv': _L0_xattn_in['Wv'], 'L0_xattn_bv': _L0_xattn_in['bv'], 'L0_xattn_Wo': _L0_xattn_in['Wo'], 'L0_xattn_bo': _L0_xattn_in['bo'], 'L0_ffn_w_gate': _L0_ffn_in['w_gate'], 'L0_ffn_w_up': _L0_ffn_in['w_up'], 'L0_ffn_w_down': _L0_ffn_in['w_down'], 'L1_xattn_Wk': _L1_xattn_in['Wk'], 'L1_xattn_Wv': _L1_xattn_in['Wv'], 'L1_xattn_bv': _L1_xattn_in['bv'], 'L1_xattn_Wq': _L1_xattn_in['Wq'], 'L1_xattn_bq': _L1_xattn_in['bq'], 'L1_xattn_Wo': _L1_xattn_in['Wo'], 'L1_xattn_bo': _L1_xattn_in['bo'], 'L1_ffn_ln1_w': _L1_ffn_in['ln1_w'], 'L1_ffn_ln1_b': _L1_ffn_in['ln1_b'], 'L1_ffn_w_qkv': _L1_ffn_in['w_qkv'], 'L1_ffn_w_proj': _L1_ffn_in['w_proj'], 'L1_ffn_ln2_w': _L1_ffn_in['ln2_w'], 'L1_ffn_ln2_b': _L1_ffn_in['ln2_b'], 'L1_ffn_gate_w': _L1_ffn_in['gate_w'], 'L1_ffn_gate_b': _L1_ffn_in['gate_b'], 'L1_ffn_w1': _L1_ffn_in['w1'], 'L1_ffn_w2': _L1_ffn_in['w2'], 'L2_xattn_w_q': _L2_xattn_in['w_q'], 'L2_xattn_w_k': _L2_xattn_in['w_k'], 'L2_xattn_w_v': _L2_xattn_in['w_v'], 'L2_xattn_w_o': _L2_xattn_in['w_o'], 'L2_ffn_clip_x': _L2_ffn_in['clip_x'], 'L2_ffn_clip_down': _L2_ffn_in['clip_down'], 'L2_ffn_w_gate': _L2_ffn_in['w_gate'], 'L2_ffn_w_up': _L2_ffn_in['w_up'], 'L2_ffn_w_down': _L2_ffn_in['w_down'], 'L3_xattn_Wq': _L3_xattn_in['Wq'], 'L3_xattn_bq': _L3_xattn_in['bq'], 'L3_xattn_Wk': _L3_xattn_in['Wk'], 'L3_xattn_bk': _L3_xattn_in['bk'], 'L3_xattn_Wv': _L3_xattn_in['Wv'], 'L3_xattn_bv': _L3_xattn_in['bv'], 'L3_xattn_Wo': _L3_xattn_in['Wo'], 'L3_xattn_bo': _L3_xattn_in['bo'], 'L3_ffn_U1': _L3_ffn_in['U1'], 'L3_ffn_V1': _L3_ffn_in['V1'], 'L3_ffn_b1': _L3_ffn_in['b1'], 'L3_ffn_U2': _L3_ffn_in['U2'], 'L3_ffn_V2': _L3_ffn_in['V2'], 'L3_ffn_b2': _L3_ffn_in['b2']}

def reference(x, ctx_1024, mask_SxS2_fk1, mask_1x1xSxS2_ik0, L0_xattn_Wq, L0_xattn_bq, L0_xattn_Wk, L0_xattn_bk, L0_xattn_Wv, L0_xattn_bv, L0_xattn_Wo, L0_xattn_bo, L0_ffn_w_gate, L0_ffn_w_up, L0_ffn_w_down, L1_xattn_Wk, L1_xattn_Wv, L1_xattn_bv, L1_xattn_Wq, L1_xattn_bq, L1_xattn_Wo, L1_xattn_bo, L1_ffn_ln1_w, L1_ffn_ln1_b, L1_ffn_w_qkv, L1_ffn_w_proj, L1_ffn_ln2_w, L1_ffn_ln2_b, L1_ffn_gate_w, L1_ffn_gate_b, L1_ffn_w1, L1_ffn_w2, L2_xattn_w_q, L2_xattn_w_k, L2_xattn_w_v, L2_xattn_w_o, L2_ffn_clip_x, L2_ffn_clip_down, L2_ffn_w_gate, L2_ffn_w_up, L2_ffn_w_down, L3_xattn_Wq, L3_xattn_bq, L3_xattn_Wk, L3_xattn_bk, L3_xattn_Wv, L3_xattn_bv, L3_xattn_Wo, L3_xattn_bo, L3_ffn_U1, L3_ffn_V1, L3_ffn_b1, L3_ffn_U2, L3_ffn_V2, L3_ffn_b2):
    import jax
    import jax.numpy as jnp

    def _L0_xattn_ref(Q, K, V, mask, Wq, bq, Wk, bk, Wv, bv, Wo, bo):
        import jax, jax.numpy as jnp
        import numpy as np
        D_MODEL = 128
        NUM_HEADS = 16
        D_K = D_MODEL // NUM_HEADS
        B, S = (2, 256)
        NEG = -1000000000.0

        def _split_heads(x):
            b, s, _ = x.shape
            return x.reshape(b, s, NUM_HEADS, D_K).transpose(0, 2, 1, 3)
        q = _split_heads(Q @ Wq.T + bq)
        k = _split_heads(K @ Wk.T + bk)
        v = _split_heads(V @ Wv.T + bv)
        scores = jnp.einsum('bhqd,bhkd->bhqk', q, k) / np.sqrt(D_K)
        scores = scores + mask * NEG
        probs = jax.nn.softmax(scores, axis=-1)
        attn = jnp.einsum('bhqk,bhkd->bhqd', probs, v)
        attn = attn.transpose(0, 2, 1, 3).reshape(Q.shape[0], Q.shape[1], D_MODEL)
        return attn @ Wo.T + bo

    def _L0_ffn_ref(x, w_gate, w_up, w_down):
        import jax, jax.numpy as jnp
        import numpy as np
        HIDDEN = 128
        INNER = 512

        def _weight_quant(w):
            scale = 1.0 / jnp.clip(jnp.mean(jnp.abs(w)), 1e-05)
            wq = jnp.clip(jnp.round(w * scale), -1.0, 1.0) / scale
            return w + jax.lax.stop_gradient(wq - w)

        def _act_quant(x):
            scale = 127.0 / jnp.clip(jnp.max(jnp.abs(x), axis=-1, keepdims=True), 1e-05)
            xq = jnp.clip(jnp.round(x * scale), -128.0, 127.0) / scale
            return x + jax.lax.stop_gradient(xq - x)

        def _bitlinear(x, w):
            return jnp.einsum('bsi,oi->bso', _act_quant(x), _weight_quant(w))
        gate = jax.nn.silu(_bitlinear(x, w_gate))
        up = _bitlinear(x, w_up)
        return _bitlinear(gate * up, w_down)

    def _L1_xattn_ref(k, v, q, Wk, Wv, bv, Wq, bq, Wo, bo):
        import jax, jax.numpy as jnp
        import numpy as np
        D_MODEL = 128
        B, S = (4, 256)
        kp = jnp.einsum('bsd,ed->bse', k, Wk)
        vp = jnp.einsum('bsd,ed->bse', v, Wv) + bv
        qp = jnp.einsum('bsd,ed->bse', q, Wq) + bq
        scale = 1.0 / jnp.sqrt(jnp.float32(kp.shape[-1]))
        scores = jnp.einsum('bqd,bkd->bqk', qp, kp) * scale
        probs = jax.nn.softmax(scores, axis=-1)
        ctx = jnp.einsum('bqk,bkd->bqd', probs, vp)
        return jnp.einsum('bqd,ed->bqe', ctx, Wo) + bo

    def _L1_ffn_ref(x, ln1_w, ln1_b, w_qkv, w_proj, ln2_w, ln2_b, gate_w, gate_b, w1, w2):
        import jax, jax.numpy as jnp
        import numpy as np
        B, N, D, H, E = (4, 128, 128, 16, 8)
        DK = D // H
        HID = 4 * D
        EPS = 1e-05

        def _layernorm(x, w, b):
            m = jnp.mean(x, axis=-1, keepdims=True)
            v = jnp.mean(jnp.square(x - m), axis=-1, keepdims=True)
            return (x - m) * jax.lax.rsqrt(v + EPS) * w + b

        def _msa(x, w_qkv, w_proj):
            b, n, d = x.shape
            qkv = (x @ w_qkv).reshape(b, n, 3, H, DK)
            q = qkv[:, :, 0].transpose(0, 2, 1, 3)
            k = qkv[:, :, 1].transpose(0, 2, 1, 3)
            v = qkv[:, :, 2].transpose(0, 2, 1, 3)
            attn = jnp.einsum('bhnd,bhmd->bhnm', q, k) * (1.0 / np.sqrt(DK))
            attn = jax.nn.softmax(attn, axis=-1)
            y = jnp.einsum('bhnm,bhmd->bhnd', attn, v)
            y = y.transpose(0, 2, 1, 3).reshape(b, n, d)
            return y @ w_proj

        def _moe_mlp(x, gate_w, gate_b, w1, w2):
            b, n, d = x.shape
            xf = x.reshape(b * n, d)
            logits = xf @ gate_w + gate_b
            one_hot = jax.nn.one_hot(jnp.argmax(logits, axis=-1), E, dtype=xf.dtype)
            h = jax.nn.gelu(jnp.einsum('td,edh->teh', xf, w1), approximate=True)
            y = jnp.einsum('teh,ehd->ted', h, w2)
            out = jnp.einsum('te,ted->td', one_hot, y)
            return out.reshape(b, n, d)
        x = x + _msa(_layernorm(x, ln1_w, ln1_b), w_qkv, w_proj)
        x = x + _moe_mlp(_layernorm(x, ln2_w, ln2_b), gate_w, gate_b, w1, w2)
        return x

    def _L2_xattn_ref(query, key, value, w_q, w_k, w_v, w_o):
        import jax, jax.numpy as jnp
        import numpy as np
        HIDDEN = 128
        HEADS = 16
        HEAD_DIM = 64
        B, Q, _ = query.shape
        Kl = key.shape[1]
        scale = HEAD_DIM ** (-0.5)
        q = (query @ w_q).reshape(B, Q, HEADS, HEAD_DIM).transpose(0, 2, 1, 3)
        k = (key @ w_k).reshape(B, Kl, HEADS, HEAD_DIM).transpose(0, 2, 1, 3)
        v = (value @ w_v).reshape(B, Kl, HEADS, HEAD_DIM).transpose(0, 2, 1, 3)
        scores = jnp.einsum('bhqd,bhkd->bhqk', q, k) * scale
        attn = jax.nn.softmax(scores, axis=-1)
        out = jnp.einsum('bhqk,bhkd->bhqd', attn, v)
        out = out.transpose(0, 2, 1, 3).reshape(B, Q, HEADS * HEAD_DIM)
        return out @ w_o

    def _L2_ffn_ref(x, clip_x, clip_down, w_gate, w_up, w_down):
        import jax, jax.numpy as jnp
        import numpy as np
        QMAX = 127.0

        def _ste_round(v):
            return v + jax.lax.stop_gradient(jnp.round(v) - v)

        def _act_fake_quant(x, clip_factor):
            scale = jax.nn.sigmoid(clip_factor) * jnp.max(jnp.abs(x)) / QMAX
            return jnp.clip(_ste_round(x / scale), -QMAX - 1.0, QMAX) * scale

        def _weight_fake_quant(w):
            scale = jnp.max(jnp.abs(w), axis=1, keepdims=True) / QMAX
            return jnp.clip(_ste_round(w / scale), -QMAX - 1.0, QMAX) * scale
        xq = _act_fake_quant(x, clip_x[0])
        gate = jnp.einsum('bsh,ih->bsi', xq, _weight_fake_quant(w_gate))
        up = jnp.einsum('bsh,ih->bsi', xq, _weight_fake_quant(w_up))
        h = _act_fake_quant(jax.nn.silu(gate) * up, clip_down[0])
        return jnp.einsum('bsi,hi->bsh', h, _weight_fake_quant(w_down))

    def _L3_xattn_ref(q, k, v, mask, Wq, bq, Wk, bk, Wv, bv, Wo, bo):
        import jax, jax.numpy as jnp
        import numpy as np
        EMBED_DIM = 128
        NUM_HEADS = 16
        HEAD_DIM = EMBED_DIM // NUM_HEADS
        B, S = (4, 256)

        def _split(x):
            b, s, _ = x.shape
            return x.reshape(b, s, NUM_HEADS, HEAD_DIM).transpose(0, 2, 1, 3)
        Q = _split(q @ Wq.T + bq)
        K = _split(k @ Wk.T + bk)
        V = _split(v @ Wv.T + bv)
        scores = jnp.einsum('bhqd,bhkd->bhqk', Q, K) / np.sqrt(HEAD_DIM).astype(np.float32)
        scores = jnp.where(mask == 0, jnp.float32(-1000000000.0), scores)
        attn = jax.nn.softmax(scores, axis=-1)
        out = jnp.einsum('bhqk,bhkd->bhqd', attn, V)
        out = out.transpose(0, 2, 1, 3).reshape(q.shape[0], q.shape[1], EMBED_DIM)
        return out @ Wo.T + bo

    def _L3_ffn_ref(x, U1, V1, b1, U2, V2, b2):
        import jax, jax.numpy as jnp
        import numpy as np
        D_MODEL, D_FF, RANK = (128, 512, 32)
        B, S = (4, 512)
        P = jnp.einsum('bsd,dr->bsr', x, U1)
        H = jax.nn.gelu(jnp.einsum('bsr,rf->bsf', P, V1) + b1)
        Q = jnp.einsum('bsf,fr->bsr', H, U2)
        return jnp.einsum('bsr,rd->bsd', Q, V2) + b2
    x = x + _L0_xattn_ref(_layernorm(x, axis=-1), ctx_1024, ctx_1024, mask_SxS2_fk1, L0_xattn_Wq, L0_xattn_bq, L0_xattn_Wk, L0_xattn_bk, L0_xattn_Wv, L0_xattn_bv, L0_xattn_Wo, L0_xattn_bo)
    x = x + _L0_ffn_ref(_layernorm(x, axis=-1), L0_ffn_w_gate, L0_ffn_w_up, L0_ffn_w_down)
    x = x + _L1_xattn_ref(ctx_1024, ctx_1024, _layernorm(x, axis=-1), L1_xattn_Wk, L1_xattn_Wv, L1_xattn_bv, L1_xattn_Wq, L1_xattn_bq, L1_xattn_Wo, L1_xattn_bo)
    x = x + _L1_ffn_ref(_layernorm(x, axis=-1), L1_ffn_ln1_w, L1_ffn_ln1_b, L1_ffn_w_qkv, L1_ffn_w_proj, L1_ffn_ln2_w, L1_ffn_ln2_b, L1_ffn_gate_w, L1_ffn_gate_b, L1_ffn_w1, L1_ffn_w2)
    x = x + _L2_xattn_ref(_layernorm(x, axis=-1), ctx_1024, ctx_1024, L2_xattn_w_q, L2_xattn_w_k, L2_xattn_w_v, L2_xattn_w_o)
    x = x + _L2_ffn_ref(_layernorm(x, axis=-1), L2_ffn_clip_x, L2_ffn_clip_down, L2_ffn_w_gate, L2_ffn_w_up, L2_ffn_w_down)
    x = x + _L3_xattn_ref(_layernorm(x, axis=-1), ctx_1024, ctx_1024, mask_1x1xSxS2_ik0, L3_xattn_Wq, L3_xattn_bq, L3_xattn_Wk, L3_xattn_bk, L3_xattn_Wv, L3_xattn_bv, L3_xattn_Wo, L3_xattn_bo)
    x = x + _L3_ffn_ref(_layernorm(x, axis=-1), L3_ffn_U1, L3_ffn_V1, L3_ffn_b1, L3_ffn_U2, L3_ffn_V2, L3_ffn_b2)
    return x

_drawn_inputs = setup_inputs


def setup_inputs(seed=0):
    import zlib

    import numpy as np

    out = dict(_drawn_inputs(seed))
    spreads = {'L0_xattn_bq': (0.0, 0.456),
     'L0_xattn_bk': (0.0, 2.0),
     'L0_xattn_bv': (0.0, 0.1),
     'L0_xattn_bo': (0.0, 0.1),
     'L1_xattn_bv': (0.0, 0.1),
     'L1_xattn_bq': (0.0, 0.454),
     'L1_xattn_bo': (0.0, 0.1),
     'L1_ffn_ln1_w': (1.0, 0.6),
     'L1_ffn_ln1_b': (0.0, 0.8),
     'L1_ffn_ln2_w': (1.0, 0.6),
     'L1_ffn_ln2_b': (0.0, 0.8),
     'L1_ffn_gate_b': (0.0, 0.6),
     'L3_ffn_b1': (0.0, 0.8),
     'L3_ffn_b2': (0.0, 0.746)}
    factors = {'L1_ffn_w_qkv': 5.08,
     'L1_ffn_w_proj': 5.03,
     'L1_ffn_gate_w': 3.089,
     'L1_ffn_w1': 2.799,
     'L1_ffn_w2': 2.807,
     'L2_ffn_w_gate': 8.0,
     'L2_ffn_w_up': 8.0,
     'L2_ffn_w_down': 8.0,
     'L3_xattn_bq': 7.919,
     'L3_xattn_bk': 64.0,
     'L3_ffn_U1': 8.0,
     'L3_ffn_V1': 8.0,
     'L3_ffn_U2': 8.0,
     'L3_ffn_V2': 8.0,
     'L3_xattn_bv': 4.781,
     'L3_xattn_bo': 4.797}
    for name, (base, spread) in spreads.items():
        noise = np.random.default_rng([zlib.crc32(name.encode()), seed]).standard_normal(out[name].shape)
        drawn = base * np.exp(spread * noise) if base else spread * noise
        out[name] = jnp.asarray(drawn.astype(out[name].dtype))
    for name, factor in factors.items():
        out[name] = (out[name] * factor).astype(out[name].dtype)
    return out
```

```python
from contextlib import ExitStack

import numpy as np

import concourse.bass as bass
from concourse import mybir

F32 = mybir.dt.float32
BF16 = mybir.dt.bfloat16
I32 = mybir.dt.int32
ALU = mybir.AluOpType
ACT = mybir.ActivationFunctionType
X = mybir.AxisListType.X

P = 128
D = 128
B, S, SC = 4, 256, 1601
TT = B * S // P
KT = (SC + P - 1) // P
SCP = KT * P
HEADS = 16
ROUND = 12582912.0
LOWEST = -3.0e38
MASKED = -(2.0 ** 100)
LN_EPS = 1e-5
FF0 = 512
FF2 = 352
FF2_CHUNKS = [(0, 128), (128, 128), (256, 96)]
EXPERTS, HID = 8, 512
FF3, RANK = 512, 32


def pipelined(eng, total, unroll, lag, step, peel=1):
    for v in range(min(peel, total // unroll)):
        for k in range(unroll):
            step(v, k)
    if total > unroll * peel:
        with eng.Fori(peel, total // unroll) as v:
            for k in range(unroll):
                step(v, k)
    for i in range(total, total + lag):
        step(i // unroll, i % unroll)


class Link:

    def __init__(self, eng, sem, per_step=0):
        self.eng, self.sem, self.per_step = eng, sem, per_step
        self.base, self.n = 0, 0

    def at(self, t):
        self.base, self.n = t * self.per_step, 0

    def __call__(self, ins):
        self.n += 1
        ins.then_inc(self.sem, 1)
        self.eng.wait_ge(self.sem, self.base + self.n)


class Core:

    def __init__(self, nc, ctx, inp):
        self.nc, self.ctx, self.inp = nc, ctx, inp
        self.sems = []
        self.x = self.sb(ctx, "x", [P, TT, D], F32)
        self.xn = self.sb(ctx, "xn", [P, TT, D], F32)
        self.xnT = self.sb(ctx, "xnT", [P, B * S], F32)
        self.ctxT = self.sb(ctx, "ctxT", [P, B, SCP], F32)
        self.ident = self.sb(ctx, "ident", [P, P], F32)
        self.identb = self.sb(ctx, "identb", [P, P], BF16)
        self.ones = self.sb(ctx, "ones", [P, P], F32)
        self.eps = self.sb(ctx, "eps", [P, 1], F32)
        self.bank = [ctx.enter_context(nc.psum_tensor(f"bank{i}", [P, 512], F32)) for i in range(8)]

    def sb(self, ctx, name, shape, dt):
        return ctx.enter_context(self.nc.sbuf_tensor(name, shape, dt))

    def sem(self, name):
        self.sems.append(self.nc.alloc_semaphore(name=name))
        return self.sems[-1]

    def end_layer(self):
        self.nc.clear_and_free_semaphores(self.sems)
        self.nc.all_engine_barrier()
        self.sems = []


def start_stage(core):
    nc = core.nc
    loaded, made = core.sem("start_loaded"), core.sem("start_made")
    with nc.Block() as block:
        @block.sync
        def _(sp):
            sp.dma_start(core.x[:, :, :], core.inp["x"].rearrange("(t p) d -> p t d", p=P)).then_inc(loaded, 16)
            sp.dma_start(core.ident[:, :], core.inp["ident"]).then_inc(loaded, 16)
            for b in range(B):
                sp.dma_start(core.ctxT[:, b, :], core.inp["ctxT"][:, b, :]).then_inc(loaded, 16)
            sp.wait_ge(loaded, 16 * (2 + B))

        @block.vector
        def _(dve):
            dve.memset(core.ones[:, :], 1.0)
            dve.memset(core.eps[:, :], LN_EPS)
            dve.wait_ge(loaded, 16 * (2 + B))
            dve.tensor_copy(core.identb[:, :], core.ident[:, :]).then_inc(made, 1)
            dve.wait_ge(made, 1)


def layernorm_stage(core, name, src, dst, dstT=None, affine=None, loads=()):
    nc = core.nc
    loaded, affine_in = core.sem(name + "_loaded"), core.sem(name + "_affine_in")
    chain, dev_ready, dev_done = core.sem(name + "_chain"), core.sem(name + "_var"), core.sem(name + "_std")
    normed, turned, copied = core.sem(name + "_normed"), core.sem(name + "_turned"), core.sem(name + "_copied")
    with ExitStack() as ctx:
        stats = core.sb(ctx, name + "_stats", [P, TT, 6], F32)
        mv = core.sb(ctx, name + "_mv", [P, TT, 2], F32)
        var = core.sb(ctx, name + "_v", [P, TT], F32)
        std = core.sb(ctx, name + "_std", [P, TT], F32)
        rec = core.sb(ctx, name + "_rec", [P, TT], F32)
        wb = core.sb(ctx, name + "_wb", [P, 2, D], F32) if affine else None
        block = ctx.enter_context(nc.Block())

        @block.sync
        def _(sp):
            n = 0
            if affine:
                for i in range(2):
                    sp.dma_start(wb[:, i, :], affine[i].partition_broadcast(P)).then_inc(affine_in, 16)
            for tile, dram in loads:
                sp.dma_start(tile, dram).then_inc(loaded, 16)
                n += 1
            if n:
                sp.wait_ge(loaded, 16 * n)

        @block.scalar
        def _(act):
            act.wait_ge(dev_ready, 1)
            act.activation(std[:, :], var[:, :], ACT.Sqrt).then_inc(dev_done, 1)
            if dstT is not None:
                act.wait_ge(turned, 1)
                act.activation(dstT[:, 0:512], core.bank[0][:, :], ACT.Copy).then_inc(copied, 1)

        @block.tensor
        def _(pe):
            if dstT is not None:
                for t in range(TT):
                    pe.wait_ge(normed, t + 1)
                    ins = pe.transpose(core.bank[t // 4][:, (t % 4) * P:(t % 4 + 1) * P], dst[:, t, :], core.ident[:, :])
                    if t % 4 == 3:
                        ins.then_inc(turned, 1)

        @block.vector
        def _(dve):
            link = Link(dve, chain)
            for t in range(TT):
                ins = dve.bn_stats(stats[:, t, :], src[:, t, :])
            link(ins)
            for t in range(TT):
                ins = dve.bn_aggr(mv[:, t, :], stats[:, t, :])
            link(ins)
            dve.tensor_scalar(var[:, :], mv[:, :, 1], LN_EPS, None, ALU.add).then_inc(dev_ready, 1)
            dve.wait_ge(dev_done, 1)
            link(dve.reciprocal(rec[:, :], std[:, :]))
            dve.wait_ge(dev_ready, 1)
            link(dve.tensor_tensor(rec[:, :], rec[:, :], var[:, :], ALU.mult))
            link(dve.tensor_tensor(std[:, :], std[:, :], rec[:, :], ALU.add))
            link(dve.tensor_scalar(std[:, :], std[:, :], 0.5, None, ALU.mult))
            link(dve.reciprocal(rec[:, :], std[:, :]))
            if affine:
                dve.wait_ge(affine_in, 32)
            for t in range(TT):
                ins = dve.tensor_scalar(dst[:, t, :], src[:, t, :], mv[:, t, 0:1], rec[:, t:t + 1],
                                        ALU.subtract, ALU.mult)
                if affine:
                    link(ins)
                    link(dve.tensor_tensor(dst[:, t, :], dst[:, t, :], wb[:, 0, :], ALU.mult))
                    ins = dve.tensor_tensor(dst[:, t, :], dst[:, t, :], wb[:, 1, :], ALU.add)
                ins.then_inc(normed, 1)
            dve.wait_ge(normed, TT)
            if dstT is not None:
                dve.wait_ge(turned, 2)
                dve.tensor_copy(dstT[:, 512:1024], core.bank[1][:, :]).then_inc(copied, 1)


def split_project_stage(core, name, w, bias, scale, from_ctx, k_parts, q_parts, v_rows):
    nc = core.nc
    cols = SCP if from_ctx else B * S
    nb = B if from_ctx else 1
    kts = cols // P
    ck = cols // 4 if from_ctx else 512
    n_ck = cols // ck
    groups = [(g, min(4, kts - g)) for g in range(0, kts, 4)]
    ng = len(groups)
    q_ready, q_evac = core.sem(name + "_q_ready"), core.sem(name + "_q_evac")
    k_ready, k_evac = core.sem(name + "_k_ready"), core.sem(name + "_k_evac")
    v_ready, v_evac = core.sem(name + "_v_ready"), core.sem(name + "_v_evac")
    ctx_in = [core.sem(f"{name}_ctx_in{i}") for i in range(2)]
    part1, rest, part2, part3 = (core.sem(name + s) for s in ("_part1", "_rest", "_part2", "_part3"))
    qpart1, qrest, qpart2, qpart3 = (core.sem(name + s) for s in ("_qpart1", "_qrest", "_qpart2", "_qpart3"))
    q_stored = core.sem(name + "_q_stored")
    k_stored = [core.sem(f"{name}_k_stored{i}") for i in range(2)]
    v_stored = [core.sem(f"{name}_v_stored{i}") for i in range(2)]
    with ExitStack() as ctx:
        ctxb = core.sb(ctx, name + "_ctxb", [P, 2, cols], F32) if from_ctx else None
        qf = core.sb(ctx, name + "_qf", [P, B * S], F32)
        qp = core.sb(ctx, name + "_qp", [P, 3, B * S], BF16)
        kf = core.sb(ctx, name + "_kf", [P, 2, cols], F32)
        kp = core.sb(ctx, name + "_kp", [P, 2, 3, cols], BF16)
        vb = core.sb(ctx, name + "_vb", [P, 2, HEADS, kts * 8], F32)
        block = ctx.enter_context(nc.Block())
        kbank, vbank, qbank = core.bank[0:2], core.bank[2:4], core.bank[4:6]

        @block.sync
        def _(sp):
            if from_ctx:
                def load(v, k):
                    if isinstance(v, int) and 2 * v + k >= nb:
                        return
                    if not isinstance(v, int) or v > 0:
                        sp.wait_ge(v_ready, ng * (2 * v + k - 1))
                    sp.dma_start(ctxb[:, k, :], core.inp["ctxT"][:, 2 * v + k, :]).then_inc(ctx_in[k], 16)
                pipelined(sp, nb, 2, 0, load)

        @block.gpsimd
        def _(pool):
            pool.wait_ge(qpart3, 1)
            pool.dma_start(q_parts.rearrange("t p c -> p t c"), qp[:, :, :]).then_inc(q_stored, 16)

            def store(v, k):
                b = 2 * v + k
                pool.wait_ge(part3, b + 1)
                pool.dma_start(k_parts[:, :, b, :].rearrange("t p c -> p t c"), kp[:, k, :, :]).then_inc(k_stored[k], 16)
                pool.wait_ge(v_evac, ng * (b + 1))
                pool.dma_start(v_rows[b, :, :, :], vb[:, k, :, :]).then_inc(v_stored[k], 16)
            if nb == 1:
                store(0, 0)
            else:
                pipelined(pool, nb, 2, 0, store)
            pool.wait_ge(q_stored, 16)
            for k in range(min(nb, 2)):
                pool.wait_ge(k_stored[k], 16 * max(nb // 2, 1))
                pool.wait_ge(v_stored[k], 16 * max(nb // 2, 1))

        @block.tensor
        def _(pe):
            for c in range(2):
                pe.matmul(qbank[c][:, :], w[:, 0, :], core.xnT[:, c * 512:(c + 1) * 512],
                          start=True, stop=True).then_inc(q_ready, 1)

            def step(v, k):
                b = 2 * v + k
                first = isinstance(v, int) and b == 0
                src = ctxb[:, k, :] if from_ctx else core.xnT[:, :]
                if from_ctx:
                    pe.wait_ge(ctx_in[k], 16 * (v + 1))
                for c in range(n_ck):
                    if not (first and c < 2):
                        pe.wait_ge(k_evac, n_ck * b + c - 1)
                    pe.matmul(kbank[c % 2][:, 0:ck], w[:, 1, :], src[:, c * ck:(c + 1) * ck],
                              start=True, stop=True).then_inc(k_ready, 1)
                for g, (kt, m) in enumerate(groups):
                    if not (first and g < 2):
                        pe.wait_ge(v_evac, ng * b + g - 1)
                    for j in range(m):
                        ins = pe.matmul(vbank[g % 2][:, j * P:(j + 1) * P], src[:, (kt + j) * P:(kt + j + 1) * P],
                                        w[:, 2, :], start=True, stop=True)
                    ins.then_inc(v_ready, 1)
            if nb == 1:
                step(0, 0)
            else:
                pipelined(pe, nb, 2, 0, step)

        @block.scalar
        def _(act):
            act.wait_ge(q_evac, 2)
            act.activation(qp[:, 0, :], qf[:, :], ACT.Copy).then_inc(qpart1, 1)
            act.wait_ge(qrest, 1)
            act.activation(qp[:, 1, :], qf[:, :], ACT.Copy).then_inc(qpart2, 1)

            def step(v, k):
                b = 2 * v + k
                first = isinstance(v, int) and v == 0
                if not first:
                    act.wait_ge(part3, b - 1)
                for c in range(n_ck):
                    act.wait_ge(k_ready, n_ck * b + c + 1)
                    act.activation(kf[:, k, c * ck:(c + 1) * ck], kbank[c % 2][:, 0:ck], ACT.Identity,
                                   bias=bias[:, 1:2]).then_inc(k_evac, 1)
                act.wait_ge(k_evac, n_ck * (b + 1))
                if not first:
                    act.wait_ge(k_stored[k], 16 * v)
                act.activation(kp[:, k, 0, :], kf[:, k, :], ACT.Copy).then_inc(part1, 1)
                act.wait_ge(rest, b + 1)
                act.activation(kp[:, k, 1, :], kf[:, k, :], ACT.Copy).then_inc(part2, 1)
            if nb == 1:
                step(0, 0)
            else:
                pipelined(act, nb, 2, 0, step)

        @block.vector
        def _(dve):
            for c in range(2):
                dve.wait_ge(q_ready, c + 1)
                dve.tensor_scalar(qf[:, c * 512:(c + 1) * 512], qbank[c][:, :], bias[:, 0:1], scale,
                                  ALU.add, ALU.mult).then_inc(q_evac, 1)
            dve.wait_ge(qpart1, 1)
            dve.wait_ge(q_evac, 2)
            dve.tensor_tensor(qf[:, :], qf[:, :], qp[:, 0, :], ALU.subtract).then_inc(qrest, 1)
            dve.wait_ge(qpart2, 1)
            dve.wait_ge(qrest, 1)
            dve.tensor_tensor(qp[:, 2, :], qf[:, :], qp[:, 1, :], ALU.subtract).then_inc(qpart3, 1)

            def step(v, k):
                b = 2 * v + k
                first = isinstance(v, int) and v == 0
                for g, (kt, m) in enumerate(groups):
                    dve.wait_ge(v_ready, ng * b + g + 1)
                    if g == 0 and not first:
                        dve.wait_ge(v_stored[k], 16 * v)
                    out = vb[:, k, :, kt * 8:(kt + m) * 8].rearrange("p h (t d) -> p t h d", d=8)
                    src = vbank[g % 2][:, 0:m * P].rearrange("p (t h d) -> p t h d", t=m, h=HEADS)
                    for j in range(m):
                        ins = dve.tensor_copy(out[:, j], src[:, j])
                    ins.then_inc(v_evac, 1)
                dve.wait_ge(part1, b + 1)
                dve.tensor_tensor(kf[:, k, :], kf[:, k, :], kp[:, k, 0, :], ALU.subtract).then_inc(rest, 1)
                dve.wait_ge(part2, b + 1)
                dve.wait_ge(rest, b + 1)
                dve.tensor_tensor(kp[:, k, 2, :], kf[:, k, :], kp[:, k, 1, :], ALU.subtract).then_inc(part3, 1)
            if nb == 1:
                step(0, 0)
            else:
                pipelined(dve, nb, 2, 0, step)


def attention_stage(core, name, acc, wo, heads, dh, nk, load_operands, dmas, load_values, scores_rhs, lhs, vtile, mask):
    nc = core.nc
    units, kts = B * heads, (nk + P - 1) // P
    tiles = 2 * units
    chunks = [(c, min(512, nk - c)) for c in range(0, nk, 512)]
    nch = len(chunks)
    groups = [(g, min(4, kts - g)) for g in range(0, kts, 4)]
    ng = len(groups)
    col_tile = max(dh, 32)
    lanes = min(P // col_tile, kts)
    loaded = [core.sem(f"{name}_loaded{i}") for i in range(2)]
    names = ("scores_ready", "scores_read", "max_part", "max_ready", "exp_done", "turned", "pv_done", "u_out", "wo_done",
             "recip_done", "acc_done", "setup")
    (scores_ready, scores_read, max_part, max_ready, exp_done, turned, pv_done, u_out, wo_done, recip_done,
     acc_done, setup) = (core.sem(f"{name}_{s}") for s in names)
    turned_out = [core.sem(f"{name}_turned_out{i}") for i in range(2)]
    v_loaded = [core.sem(f"{name}_v_loaded{i}") for i in range(2)]
    passed = core.sem(name + "_passed")
    s_bank, t_bank, u_bank, o_bank = core.bank[0:4], core.bank[4:6], core.bank[6], core.bank[7]
    LAST = 4
    with ExitStack() as ctx:
        sc = core.sb(ctx, name + "_sc", [P, 2, nk], F32)
        pr = core.sb(ctx, name + "_pr", [P, 2, kts * P], F32)
        prT = core.sb(ctx, name + "_prT", [P, 2, kts, P], F32)
        mx = core.sb(ctx, name + "_mx", [P, 2, nch], F32)
        nmx = core.sb(ctx, name + "_nmx", [P, 2], F32)
        tot = core.sb(ctx, name + "_tot", [P, 4], F32)
        rtot = core.sb(ctx, name + "_rtot", [P, 4], F32)
        u_sb = core.sb(ctx, name + "_u", [P, 2, P], F32)
        block = ctx.enter_context(nc.Block())

        def live(v, k, lag):
            return not isinstance(v, int) or 0 <= 4 * v + k - lag < tiles

        def first(v, k, lag, n):
            return isinstance(v, int) and 4 * v + k - lag < n

        def where(v, k, lag):
            u = 2 * v + (k - lag) // 2
            return 4 * v + k - lag, u, (u // heads if heads > 1 else u), (u % heads if heads > 1 else 0)

        @block.sync
        def _(sp):
            def place(u):
                return (u // heads, u % heads) if heads > 1 else (u, 0)

            def step(v, k):
                u = 2 * v + k
                if not isinstance(v, int) or u < units:
                    if not isinstance(v, int) or v > 0:
                        sp.wait_ge(scores_ready, nch * (2 * u - 2))
                    load_operands(sp, *place(u), k, loaded[k])
                if not isinstance(v, int) or u > 0:
                    if not isinstance(v, int) or u > 2:
                        sp.wait_ge(pv_done, 2 * u - 4)
                    load_values(sp, *place(u - 1), 1 - k, v_loaded[1 - k])
            pipelined(sp, units, 2, 1, step, peel=2)

        @block.tensor
        def _(pe):
            def step(v, k):
                if live(v, k, 0):
                    t, u, b, h = where(v, k, 0)
                    if k % 2 == 0:
                        pe.wait_ge(loaded[k // 2], 16 * dmas * (v + 1))
                    for c, (at, w) in enumerate(chunks):
                        if not first(v, k, 0, 1):
                            pe.wait_ge(scores_read, nch * (t - 1) + c + 1)
                        pe.matmul(s_bank[c][:, 0:w], lhs(k // 2, k % 2), scores_rhs(k // 2, b, at, w),
                                  start=True, stop=True).then_inc(scores_ready, 1)
                if live(v, k, 2):
                    t, _, _, _ = where(v, k, 2)
                    pe.wait_ge(setup, 1)
                    pe.wait_ge(exp_done, t + 1)
                    for g, (kt, m) in enumerate(groups):
                        n = ng * (k - 2) + g
                        if not (isinstance(v, int) and 4 * ng * v + n < 2):
                            pe.wait_ge(turned_out[n % 2], 2 * ng * v + n // 2)
                        for j in range(m):
                            ins = pe.transpose(t_bank[n % 2][:, j * P:(j + 1) * P],
                                               pr[:, k % 2, (kt + j) * P:(kt + j + 1) * P], core.ident[:, :])
                        ins.then_inc(turned, 1)
                if live(v, k, 3):
                    t, _, _, _ = where(v, k, 3)
                    for i in range(2 if ng > 1 else 1):
                        n = ng * (k - 3) + ng - 1 - i
                        pe.wait_ge(turned_out[n % 2], 2 * ng * v + n // 2 + 1)
                    if not first(v, k, 3, 1):
                        pe.wait_ge(u_out, t)
                    c = (k - 3) // 2
                    pe.wait_ge(v_loaded[c % 2], 16 * (v + c // 2 + 1))
                    for kt in range(kts):
                        j = kt % lanes
                        ins = pe.matmul(u_bank[j * col_tile:j * col_tile + dh, 0:P],
                                        vtile(((k - 3) // 2) % 2, kt), prT[:, (k - 3) % 2, kt, :],
                                        start=(kt < lanes), stop=(kt >= kts - lanes))
                    ins.then_inc(pv_done, 1)
                if live(v, k, 4):
                    t, u, b, h = where(v, k, 4)
                    pe.wait_ge(u_out, t + 1)
                    if not first(v, k, 4, 1):
                        pe.wait_ge(acc_done, t + 2)
                    pe.matmul(o_bank[:, 0:D], u_sb[:, k % 2, :], wo[:, h, :], start=True, stop=True).then_inc(wo_done, 1)
            pipelined(pe, tiles, 4, LAST, step)

        @block.scalar
        def _(act):
            def copy_out(v, k):
                t, _, _, _ = where(v, k, 2)
                for g, (kt, m) in enumerate(groups):
                    n = ng * (k - 2) + g
                    if g == 1:
                        continue
                    act.wait_ge(turned, ng * t + g + 1)
                    if g == 0 and not first(v, k, 2, 2):
                        act.wait_ge(pv_done, t - 1)
                    act.activation(prT[:, k % 2, kt:kt + m, :], t_bank[n % 2][:, 0:m * P].rearrange("p (t q) -> p t q", t=m),
                                   ACT.Copy).then_inc(turned_out[n % 2], 1)

            def step(v, k):
                if live(v, k, 2):
                    copy_out(v, k)
                if live(v, k, 0):
                    t, _, _, _ = where(v, k, 0)
                    act.wait_ge(max_ready, t + 1)
                    if not first(v, k, 0, 2):
                        act.wait_ge(turned, ng * (t - 1))
                    if not first(v, k, 0, 4):
                        act.wait_ge(recip_done, t - 3)
                    act.activation(pr[:, k % 2, 0:nk], sc[:, k % 2, :], ACT.Exp, bias=nmx[:, k % 2:k % 2 + 1],
                                   scale=1.0, accum_out=tot[:, k:k + 1]).then_inc(exp_done, 1)
            pipelined(act, tiles, 4, LAST, step)

        @block.vector
        def _(dve):
            if kts * P > nk:
                dve.memset(pr[:, :, nk:], 0.0)
            dve.memset(u_bank[:, 0:P], 0.0).then_inc(setup, 1)
            dve.memset(nmx[:, :], 0.0).then_inc(acc_done, 2)

            def maxima(v, k, cs):
                t, _, _, _ = where(v, k, 0)
                for c in cs:
                    at, w = chunks[c]
                    dve.wait_ge(scores_ready, nch * t + c + 1)
                    if c == 0 and not first(v, k, 0, 2):
                        dve.wait_ge(exp_done, t - 1)
                    dve.sem_inc(passed, 1)
                    dve.tensor_tensor_reduce(sc[:, k % 2, at:at + w], s_bank[c][:, 0:w], mask(k % 2, at, w), 1.0,
                                             LOWEST, ALU.add, ALU.max, mx[:, k % 2, c:c + 1]).then_inc(scores_read, 1)

            def step(v, k):
                if live(v, k, 0):
                    maxima(v, k, range(min(2, nch)))
                if live(v, k, 2) and ng > 1:
                    t, _, _, _ = where(v, k, 2)
                    kt, m = groups[1]
                    n = ng * (k - 2) + 1
                    dve.wait_ge(turned, ng * t + 2)
                    if not first(v, k, 2, 2):
                        dve.wait_ge(pv_done, t - 1)
                    dve.tensor_copy(prT[:, k % 2, kt:kt + m, :],
                                    t_bank[n % 2][:, 0:m * P].rearrange("p (t q) -> p t q", t=m)).then_inc(turned_out[n % 2], 1)
                if live(v, k, 0):
                    t, _, _, _ = where(v, k, 0)
                    maxima(v, k, range(2, nch))
                    dve.wait_ge(scores_read, nch * (t + 1))
                    dve.tensor_reduce(nmx[:, k % 2:k % 2 + 1], mx[:, k % 2, :], X, ALU.max, negate=True).then_inc(max_ready, 1)
                if live(v, k, 2):
                    t, _, _, _ = where(v, k, 2)
                    dve.wait_ge(exp_done, t + 1)
                    kk = (k - 2) % 4
                    dve.reciprocal(rtot[:, kk:kk + 1], tot[:, kk:kk + 1]).then_inc(recip_done, 1)
                if live(v, k, 3):
                    t, _, _, _ = where(v, k, 3)
                    dve.wait_ge(pv_done, t + 1)
                    dve.tensor_copy(u_sb[:, (k - 3) % 2, :], u_bank[:, 0:P]).then_inc(u_out, 1)
                if live(v, k, 4):
                    t, u, b, h = where(v, k, 4)
                    dve.wait_ge(wo_done, t + 1)
                    dve.wait_ge(acc_done, t + 1)
                    dve.wait_ge(recip_done, t + 1)
                    tile = acc[:, 2 * b + k % 2, :]
                    dve.scalar_tensor_tensor(tile, o_bank[:, 0:D], rtot[:, k:k + 1], tile, ALU.mult,
                                             ALU.add).then_inc(acc_done, 1)
            pipelined(dve, tiles, 4, LAST, step)


def bias_stage(core, name, acc, bv, wo_t, bo):
    nc = core.nc
    spread, mixed, added = core.sem(name + "_spread"), core.sem(name + "_mixed"), core.sem(name + "_added")
    with ExitStack() as ctx:
        bvb = core.sb(ctx, name + "_bvb", [P, P], F32)
        row = core.sb(ctx, name + "_row", [P, D], F32)
        block = ctx.enter_context(nc.Block())

        @block.tensor
        def _(pe):
            pe.wait_ge(spread, 1)
            pe.matmul(core.bank[0][:, 0:D], bvb[:, :], wo_t, start=True, stop=True).then_inc(mixed, 1)

        @block.vector
        def _(dve):
            dve.tensor_scalar(bvb[:, :], core.ones[:, :], bv, None, ALU.mult).then_inc(spread, 1)
            dve.wait_ge(mixed, 1)
            dve.tensor_tensor(row[:, :], core.bank[0][:, 0:D], bo, ALU.add).then_inc(added, 1)
            dve.wait_ge(added, 1)
            dve.tensor_tensor(acc[:, :, :], acc[:, :, :], row[:, :].unsqueeze(1).broadcast_to([P, TT, D]),
                              ALU.add).then_inc(added, 1)
            dve.wait_ge(added, 2)


def wide_project_stage(core, name, heads, dh, wq_blocks, wk_blocks, bq, scale, wv, qk_parts, v_rows):
    nc = core.nc
    blocks = heads * dh // P
    per = heads // blocks
    width = heads * dh
    halves = [(c, min(512, width - c)) for c in range(0, width, 512)]
    nh = len(halves)
    names = ("q_ready", "q_evac", "qk_ready", "qk_evac", "v_ready", "v_evac")
    q_ready, q_evac, qk_ready, qk_evac, v_ready, v_evac = (core.sem(f"{name}_{s}") for s in names)
    w_in = [core.sem(f"{name}_w_in{i}") for i in range(2)]
    ctx_in = [core.sem(f"{name}_ctx_in{i}") for i in range(2)]
    qk_stored = [core.sem(f"{name}_qk_stored{i}") for i in range(2)]
    v_stored = [core.sem(f"{name}_v_stored{i}") for i in range(2)]
    with ExitStack() as ctx:
        wqb = core.sb(ctx, name + "_wqb", [P, 2, P], F32)
        wkb = core.sb(ctx, name + "_wkb", [P, 2, per, P], F32)
        qb = core.sb(ctx, name + "_qb", [P, 2, B * S], F32)
        qk = core.sb(ctx, name + "_qk", [P, 2, per, B * S], F32)
        ctxb = core.sb(ctx, name + "_ctxb", [P, 2, SCP], F32)
        vb = core.sb(ctx, name + "_vb", [P, 2, heads, KT * dh], F32)
        block = ctx.enter_context(nc.Block())
        qbank, qkbank, vbank = core.bank[0:2], core.bank[2:4], core.bank[4:6]

        def over_blocks(eng, step):
            if blocks == 1:
                step(0, 0)
            else:
                pipelined(eng, blocks, 2, 0, step)

        @block.sync
        def _(sp):
            def load_weights(v, k):
                m = 2 * v + k
                if not isinstance(v, int) or v > 0:
                    sp.wait_ge(qk_ready, 2 * per * (m - 1))
                sp.dma_start(wqb[:, k, :], wq_blocks[m]).then_inc(w_in[k], 16)
                sp.dma_start(wkb[:, k, :, :], wk_blocks[m]).then_inc(w_in[k], 16)
            over_blocks(sp, load_weights)

            def load_ctx(v, k):
                b = 2 * v + k
                if not isinstance(v, int) or v > 0:
                    sp.wait_ge(v_ready, KT * nh * (b - 1))
                sp.dma_start(ctxb[:, k, :], core.inp["ctxT"][:, b, :]).then_inc(ctx_in[k], 16)
            pipelined(sp, B, 2, 0, load_ctx)

        @block.gpsimd
        def _(pool):
            def store_qk(v, k):
                m = 2 * v + k
                pool.wait_ge(qk_evac, 2 * per * (m + 1))
                pool.dma_start(qk_parts[m], qk[:, k, :, :]).then_inc(qk_stored[k], 16)
            over_blocks(pool, store_qk)

            def store_v(v, k):
                b = 2 * v + k
                pool.wait_ge(v_evac, KT * nh * (b + 1))
                pool.dma_start(v_rows[b], vb[:, k, :, :]).then_inc(v_stored[k], 16)
            pipelined(pool, B, 2, 0, store_v)
            for k in range(min(blocks, 2)):
                pool.wait_ge(qk_stored[k], 16 * max(blocks // 2, 1))
            for k in range(2):
                pool.wait_ge(v_stored[k], 16 * B // 2)

        @block.tensor
        def _(pe):
            def queries(v, k):
                m = 2 * v + k
                first = isinstance(v, int) and m == 0
                pe.wait_ge(w_in[k], 32 * (v + 1))
                for c in range(2):
                    if not first:
                        pe.wait_ge(q_evac, 2 * m + c - 1)
                    pe.matmul(qbank[c][:, :], wqb[:, k, :], core.xnT[:, c * 512:(c + 1) * 512],
                              start=True, stop=True).then_inc(q_ready, 1)
                for j in range(per):
                    for c in range(2):
                        n = 2 * j + c
                        if not (first and n < 2):
                            pe.wait_ge(qk_evac, 2 * per * m + n - 1)
                        if j == 0:
                            pe.wait_ge(q_evac, 2 * m + c + 1)
                        pe.matmul(qkbank[c][:, :], wkb[:, k, j, :], qb[:, k, c * 512:(c + 1) * 512],
                                  start=True, stop=True).then_inc(qk_ready, 1)
            over_blocks(pe, queries)

            def values(v, k):
                b = 2 * v + k
                first = isinstance(v, int) and b == 0
                pe.wait_ge(ctx_in[k], 16 * (v + 1))
                for kt in range(KT):
                    for c, (at, w) in enumerate(halves):
                        n = kt * nh + c
                        if not (first and n < 2):
                            pe.wait_ge(v_evac, KT * nh * b + n - 1)
                        pe.matmul(vbank[(KT * nh * k + n) % 2][:, 0:w], ctxb[:, k, kt * P:(kt + 1) * P],
                                  wv[:, at:at + w], start=True, stop=True).then_inc(v_ready, 1)
            pipelined(pe, B, 2, 0, values)

        @block.scalar
        def _(act):
            def queries(v, k):
                m = 2 * v + k
                if not isinstance(v, int) or v > 0:
                    act.wait_ge(qk_stored[k], 16 * v)
                for j in range(per):
                    for c in range(2):
                        act.wait_ge(qk_ready, 2 * per * m + 2 * j + c + 1)
                        act.activation(qk[:, k, j, c * 512:(c + 1) * 512], qkbank[c][:, :], ACT.Copy).then_inc(qk_evac, 1)
            over_blocks(act, queries)

        @block.vector
        def _(dve):
            def queries(v, k):
                m = 2 * v + k
                if not isinstance(v, int) or v > 0:
                    dve.wait_ge(qk_ready, 2 * per * (m - 1))
                for c in range(2):
                    dve.wait_ge(q_ready, 2 * m + c + 1)
                    dve.tensor_scalar(qb[:, k, c * 512:(c + 1) * 512], qbank[c][:, :], bq, scale,
                                      ALU.add, ALU.mult).then_inc(q_evac, 1)
            over_blocks(dve, queries)

            def values(v, k):
                b = 2 * v + k
                if not isinstance(v, int) or v > 0:
                    dve.wait_ge(v_stored[k], 16 * v)
                for kt in range(KT):
                    for c, (at, w) in enumerate(halves):
                        n = kt * nh + c
                        dve.wait_ge(v_ready, KT * nh * b + n + 1)
                        dve.tensor_copy(vb[:, k, at // dh:(at + w) // dh, kt * dh:(kt + 1) * dh],
                                        vbank[(KT * nh * k + n) % 2][:, 0:w].rearrange("p (h d) -> p h d", d=dh)
                                        ).then_inc(v_evac, 1)
            pipelined(dve, B, 2, 0, values)


def ffn0_stage(core, w):
    nc = core.nc
    wc, xc, hc, fc, gc = (core.sem("ffn0_" + s) for s in ("w_chain", "x_chain", "h_chain", "f_chain", "g_chain"))
    names = ("sums_ready", "x_quantized", "x_turned", "x_ready", "gu_ready", "silu_done", "h_quantized", "h_turned",
             "h_ready", "down_ready", "added")
    (sums_ready, x_quantized, x_turned, x_ready, gu_ready, silu_done, h_quantized, h_turned, h_ready, down_ready,
     added) = (core.sem("ffn0_" + s) for s in names)
    with ExitStack() as ctx:
        part = core.sb(ctx, "ffn0_part", [P, 3], F32)
        mean = core.sb(ctx, "ffn0_mean", [P, 3], F32)
        inv = core.sb(ctx, "ffn0_inv", [P, 3], F32)
        wr = core.sb(ctx, "ffn0_wr", [P, 3, FF0], F32)
        wq = core.sb(ctx, "ffn0_wq", [P, 3, FF0], BF16)
        am = core.sb(ctx, "ffn0_am", [P, TT], F32)
        sx = core.sb(ctx, "ffn0_sx", [P, TT], F32)
        fgu = core.sb(ctx, "ffn0_fgu", [P, 2, TT], F32)
        xr = core.sb(ctx, "ffn0_xr", [P, TT, D], F32)
        xq = core.sb(ctx, "ffn0_xq", [P, TT, D], BF16)
        xqT = core.sb(ctx, "ffn0_xqT", [P, B * S], BF16)
        gs = core.sb(ctx, "ffn0_gs", [P, 2, FF0], F32)
        hs = core.sb(ctx, "ffn0_hs", [P, 2, FF0], F32)
        ham = core.sb(ctx, "ffn0_ham", [P, 2], F32)
        hsc = core.sb(ctx, "ffn0_hsc", [P, 2], F32)
        hf = core.sb(ctx, "ffn0_hf", [P, 2], F32)
        hq = core.sb(ctx, "ffn0_hq", [P, 2, FF0], BF16)
        hT = core.sb(ctx, "ffn0_hT", [P, 2, FF0], BF16)
        block = ctx.enter_context(nc.Block())
        g_bank, u_bank, t_bank, d_bank = core.bank[0:2], core.bank[2:4], core.bank[4:6], core.bank[6:8]
        tb = [t_bank[i][:, :].bitcast(BF16) for i in range(2)]

        def live(v, k, lag):
            return not isinstance(v, int) or 0 <= 2 * v + k - lag < TT

        def early(v, k, lag, n):
            return isinstance(v, int) and 2 * v + k - lag < n

        @block.tensor
        def _(pe):
            pe.wait_ge(wc, 1)
            pe.matmul(g_bank[0][:, 0:3], core.ones[:, :], part[:, :], start=True, stop=True).then_inc(sums_ready, 1)
            pe.wait_ge(x_quantized, 1)
            for t in range(TT):
                ins = pe.transpose(tb[t // 4][:, t % 4 * P:(t % 4 + 1) * P], xq[:, t, :], core.identb[:, :])
            ins.then_inc(x_turned, 1)
            pe.wait_ge(x_ready, 2)

            def step(v, k):
                t = 2 * v + k
                if live(v, k, 0):
                    if not early(v, k, 0, 2):
                        pe.wait_ge(h_quantized, t - 1)
                    pe.matmul(g_bank[k][:, :], xqT[:, bass.ts(t, P)], wq[:, 0, :], start=True, stop=True)
                    pe.matmul(u_bank[k][:, :], xqT[:, bass.ts(t, P)], wq[:, 1, :], start=True, stop=True).then_inc(gu_ready, 1)
                if live(v, k, 1):
                    j = 1 - k
                    pe.wait_ge(h_quantized, t)
                    if not early(v, k, 1, 2):
                        pe.wait_ge(h_ready, t - 2)
                    for c in range(4):
                        ins = pe.transpose(tb[j][:, c * P:(c + 1) * P], hq[:, j, c * P:(c + 1) * P], core.identb[:, :])
                    ins.then_inc(h_turned, 1)
                    pe.wait_ge(h_ready, t)
                    if not early(v, k, 1, 2):
                        pe.wait_ge(added, t - 2)
                    for c in range(4):
                        ins = pe.matmul(d_bank[j][:, 0:D], hT[:, j, c * P:(c + 1) * P], wq[:, 2, c * P:(c + 1) * P],
                                        start=(c == 0), stop=(c == 3))
                    ins.then_inc(down_ready, 1)
            pipelined(pe, TT, 2, 1, step, peel=2)

        @block.scalar
        def _(act):
            act.wait_ge(x_turned, 1)
            act.activation(xqT[:, 0:512], tb[0][:, 0:512], ACT.Copy).then_inc(x_ready, 1)
            act.wait_ge(fc, 3)

            def step(v, k):
                t = 2 * v + k
                if live(v, k, 0):
                    act.wait_ge(gu_ready, t + 1)
                    if not early(v, k, 0, 2):
                        act.wait_ge(h_quantized, t - 1)
                    act.activation(gs[:, k, :], g_bank[k][:, :], ACT.Silu, scale=fgu[:, 0, bass.ts(t, 1)]).then_inc(silu_done, 1)
                if live(v, k, 1):
                    j = 1 - k
                    act.wait_ge(h_turned, t)
                    if not early(v, k, 1, 2):
                        act.wait_ge(down_ready, t - 2)
                    act.activation(hT[:, j, :], tb[j][:, 0:FF0], ACT.Copy).then_inc(h_ready, 1)
            pipelined(act, TT, 2, 1, step, peel=2)

        @block.vector
        def _(dve):
            wl, xl, fl = Link(dve, wc), Link(dve, xc), Link(dve, fc)
            wl(dve.tensor_reduce(part[:, :], w[:, :, :], X, ALU.add, apply_absolute_value=True))
            xl(dve.tensor_reduce(am[:, :], core.xn[:, :, :], X, ALU.max, apply_absolute_value=True))
            xl(dve.tensor_scalar(am[:, :], am[:, :], 1e-5, None, ALU.max))
            xl(dve.reciprocal(sx[:, :], am[:, :]))
            xl(dve.tensor_scalar(sx[:, :], sx[:, :], 127.0, None, ALU.mult))
            for t in range(TT):
                ins = dve.tensor_scalar(xr[:, t, :], core.xn[:, t, :], sx[:, t:t + 1], ROUND, ALU.mult, ALU.add)
            xl(ins)
            xl(dve.tensor_scalar(xr[:, :, :], xr[:, :, :], ROUND, 127.0, ALU.subtract, ALU.min))
            dve.tensor_scalar(xq[:, :, :], xr[:, :, :], -128.0, None, ALU.max).then_inc(x_quantized, 1)
            dve.wait_ge(sums_ready, 1)
            wl(dve.tensor_scalar(mean[:, :], g_bank[0][:, 0:3], 1.0 / (FF0 * D), 1e-5, ALU.mult, ALU.max))
            wl(dve.reciprocal(inv[:, :], mean[:, :]))
            for i in range(3):
                ins = dve.tensor_scalar(wr[:, i, :], w[:, i, :], inv[:, i:i + 1], ROUND, ALU.mult, ALU.add)
            wl(ins)
            wl(dve.tensor_scalar(wr[:, :, :], wr[:, :, :], ROUND, 1.0, ALU.subtract, ALU.min))
            wl(dve.tensor_scalar(wq[:, :, :], wr[:, :, :], -1.0, None, ALU.max))
            fl(dve.tensor_scalar(am[:, :], am[:, :], 1.0 / 127.0, None, ALU.mult))
            dve.tensor_scalar(fgu[:, 0, :], am[:, :], mean[:, 0:1], None, ALU.mult)
            fl(dve.tensor_scalar(fgu[:, 1, :], am[:, :], mean[:, 1:2], None, ALU.mult))
            fl(dve.tensor_scalar(mean[:, 2:3], mean[:, 2:3], 1.0 / 127.0, None, ALU.mult))
            dve.wait_ge(x_turned, 1)
            dve.tensor_copy(xqT[:, 512:1024], tb[1][:, 0:512]).then_inc(x_ready, 1)
            hl = Link(dve, hc, 6)

            def step(v, k):
                t = 2 * v + k
                if live(v, k, 0):
                    hl.at(t)
                    dve.wait_ge(silu_done, t + 1)
                    hl(dve.scalar_tensor_tensor(hs[:, k, :], u_bank[k][:, :], fgu[:, 1, bass.ts(t, 1)], gs[:, k, :],
                                                ALU.mult, ALU.mult))
                    hl(dve.tensor_reduce(ham[:, k:k + 1], hs[:, k, :], X, ALU.max, apply_absolute_value=True))
                    hl(dve.tensor_scalar(ham[:, k:k + 1], ham[:, k:k + 1], 1e-5, None, ALU.max))
                    hl(dve.reciprocal(hsc[:, k:k + 1], ham[:, k:k + 1]))
                    if not early(v, k, 0, 2):
                        dve.wait_ge(added, t - 1)
                    dve.tensor_scalar(hf[:, k:k + 1], ham[:, k:k + 1], mean[:, 2:3], None, ALU.mult)
                    hl(dve.tensor_scalar(hsc[:, k:k + 1], hsc[:, k:k + 1], 127.0, None, ALU.mult))
                    hl(dve.tensor_scalar(hs[:, k, :], hs[:, k, :], hsc[:, k:k + 1], ROUND, ALU.mult, ALU.add))
                    if not early(v, k, 0, 2):
                        dve.wait_ge(h_turned, t - 1)
                    dve.tensor_scalar(hq[:, k, :], hs[:, k, :], ROUND, 127.0, ALU.subtract, ALU.min).then_inc(h_quantized, 1)
                if live(v, k, 1):
                    j = 1 - k
                    dve.wait_ge(down_ready, t)
                    tile = core.x[:, t - 1, :]
                    dve.scalar_tensor_tensor(tile, d_bank[j][:, 0:D], hf[:, j:j + 1], tile, ALU.mult, ALU.add).then_inc(added, 1)
            pipelined(dve, TT, 2, 1, step, peel=2)


def moe_stage(core, y, zT, w1, w2, gw, gb, rank):
    nc = core.nc
    gc = core.sem("moe_chain")
    names = ("logits_ready", "up_ready", "gelu_done", "down_ready", "added")
    logits_ready, up_ready, gelu_done, down_ready, added = (core.sem("moe_" + s) for s in names)
    w_in = [core.sem(f"moe_w_in{i}") for i in range(2)]
    steps = 2 * EXPERTS
    with ExitStack() as ctx:
        w1b = core.sb(ctx, "moe_w1b", [P, 2, HID], F32)
        w2b = core.sb(ctx, "moe_w2b", [P, 2, 4, D], F32)
        hid = core.sb(ctx, "moe_hid", [P, 2, 4, 512], F32)
        lg = core.sb(ctx, "moe_lg", [P, TT, EXPERTS], F32)
        best = core.sb(ctx, "moe_best", [P, TT], F32)
        pick = core.sb(ctx, "moe_pick", [P, TT, EXPERTS], F32)
        block = ctx.enter_context(nc.Block())
        up_bank, down_bank, g_bank = core.bank[0:4], core.bank[4:6], core.bank[6]

        def live(v, k, lag):
            return not isinstance(v, int) or 0 <= 4 * v + k - lag < steps

        def early(v, k, lag, n):
            return isinstance(v, int) and 4 * v + k - lag < n

        @block.sync
        def _(sp):
            def step(v, k):
                e = 2 * v + k
                if not isinstance(v, int) or v > 0:
                    sp.wait_ge(down_ready, 2 * (e - 1))
                sp.dma_start(w1b[:, k, :], w1[e]).then_inc(w_in[k], 16)
                sp.dma_start(w2b[:, k, :, :], w2[e]).then_inc(w_in[k], 16)
            pipelined(sp, EXPERTS, 2, 0, step)

        @block.tensor
        def _(pe):
            for t in range(TT):
                ins = pe.matmul(g_bank[:, t * EXPERTS:(t + 1) * EXPERTS], zT[:, t * P:(t + 1) * P], gw,
                                start=True, stop=True)
            ins.then_inc(logits_ready, 1)

            def step(v, k):
                i = 4 * v + k
                if live(v, k, 0):
                    if k % 2 == 0:
                        pe.wait_ge(w_in[k // 2], 32 * (v + 1))
                    for c in range(4):
                        if not early(v, k, 0, 1):
                            pe.wait_ge(gelu_done, 4 * (i - 1) + c + 1)
                        pe.matmul(up_bank[c][:, :], w1b[:, k // 2, c * P:(c + 1) * P],
                                  zT[:, (k % 2) * 512:(k % 2 + 1) * 512], start=True, stop=True).then_inc(up_ready, 1)
                if live(v, k, 1):
                    j = (k - 1) % 4
                    pe.wait_ge(gelu_done, 4 * i)
                    if not early(v, k, 1, 2):
                        pe.wait_ge(added, 4 * (i - 2))
                    for q in range(4):
                        for c in range(4):
                            ins = pe.matmul(down_bank[j % 2][:, q * D:(q + 1) * D], hid[:, j % 2, c, q * P:(q + 1) * P],
                                            w2b[:, j // 2, c, :], start=(c == 0), stop=(c == 3))
                    ins.then_inc(down_ready, 1)
            pipelined(pe, steps, 4, 1, step)

        @block.scalar
        def _(act):
            def step(v, k):
                i = 4 * v + k
                for c in range(4):
                    act.wait_ge(up_ready, 4 * i + c + 1)
                    if c == 0 and not early(v, k, 0, 2):
                        act.wait_ge(down_ready, i - 1)
                    act.activation(hid[:, k % 2, c, :], up_bank[c][:, :], ACT.Gelu_apprx_tanh).then_inc(gelu_done, 1)
            pipelined(act, steps, 4, 0, step)

        @block.vector
        def _(dve):
            link = Link(dve, gc)
            wide = lambda a: a.unsqueeze(1).broadcast_to([P, TT, EXPERTS])
            each = lambda a: a.unsqueeze(2).broadcast_to([P, TT, EXPERTS])
            dve.wait_ge(logits_ready, 1)
            link(dve.tensor_tensor(lg[:, :, :], g_bank[:, 0:TT * EXPERTS].rearrange("p (t e) -> p t e", e=EXPERTS),
                                   wide(gb), ALU.add))
            link(dve.tensor_reduce(best[:, :], lg[:, :, :], X, ALU.max))
            link(dve.tensor_tensor(pick[:, :, :], lg[:, :, :], each(best[:, :]), ALU.is_equal))
            link(dve.tensor_tensor(pick[:, :, :], pick[:, :, :], wide(rank), ALU.mult))
            link(dve.tensor_reduce(best[:, :], pick[:, :, :], X, ALU.max))
            link(dve.tensor_tensor(lg[:, :, :], pick[:, :, :], each(best[:, :]), ALU.is_equal))

            def step(v, k):
                if live(v, k, 1):
                    i = 4 * v + k
                    j = (k - 1) % 4
                    e = 2 * v + (k - 1) // 2
                    dve.wait_ge(down_ready, i)
                    for q in range(4):
                        t = 4 * (j % 2) + q
                        tile = y[:, t, :]
                        if not early(v, k, 1, 2):
                            dve.wait_ge(added, 4 * (i - 3) + q + 1)
                        dve.scalar_tensor_tensor(tile, down_bank[j % 2][:, q * D:(q + 1) * D], lg[:, t, bass.ts(e, 1)],
                                                 tile, ALU.mult, ALU.add).then_inc(added, 1)
            pipelined(dve, steps, 4, 1, step)
            dve.wait_ge(added, 4 * steps)
            link(dve.tensor_tensor(core.x[:, :, :], core.x[:, :, :], y[:, :, :], ALU.add))


def ffn2_stage(core, w_gu, w_down, clips):
    nc = core.nc
    names = ("chain", "w_quantized", "w_turned", "w_ready", "col_ready", "col_turned", "top_ready", "top_spread",
             "exp_done", "gu_ready", "silu_done", "gu_read", "down_ready", "scaled", "out_turned", "w_copied", "xq_ready")
    (chain, w_quantized, w_turned, w_ready, col_ready, col_turned, top_ready, top_spread, exp_done, gu_ready,
     silu_done, gu_read, down_ready, scaled, out_turned, w_copied, xq_ready) = (core.sem("ffn2_" + s) for s in names)
    top_done = core.sem("ffn2_top_done")
    N = B * S
    NC = len(FF2_CHUNKS)
    with ExitStack() as ctx:
        sb = lambda n, shape, dt: core.sb(ctx, "ffn2_" + n, shape, dt)
        am = sb("am", [P, 2 * NC + 1], F32)
        inv = sb("inv", [P, 2 * NC + 1], F32)
        wr = sb("wr", [P, 2 * NC, D], F32)
        wqn = sb("wqn", [P, 2 * NC, D], BF16)
        wdn = sb("wdn", [P, NC * P], F32)
        wdq = sb("wdq", [P, NC * P], BF16)
        wgu = sb("wgu", [P, 2 * NC, P], BF16)
        wd = sb("wd", [P, NC, P], BF16)
        xr = sb("xr", [P, N], F32)
        xq = sb("xq", [P, N], BF16)
        sig = sb("sig", [P, 2], F32)
        col = sb("col", [P, 1], F32)
        top = sb("top", [1, 1], F32)
        sx = sb("sx", [P, 2], F32)
        rx = sb("rx", [P, 2], F32)
        fs = sb("fs", [P, 2 * NC + 1], F32)
        gs = sb("gs", [P, 2, 512], F32)
        h = sb("h", [P, NC, N], F32)
        hq = sb("hq", [P, NC, N], BF16)
        oT = sb("oT", [P, N], F32)
        block = ctx.enter_context(nc.Block())
        bank = core.bank
        tb = bank[0][:, :].bitcast(BF16)
        tb2 = bank[1][:, :].bitcast(BF16)
        work = [(c, i) for i in range(NC) for c in range(2)]

        def pad(i):
            return FF2_CHUNKS[i][1]

        @block.tensor
        def _(pe):
            pe.wait_ge(w_quantized, 2)
            for i in range(2 * NC):
                pe.transpose(tb[:, i * P:(i + 1) * P], wqn[:, i, :], core.identb[:, :])
            for i in range(NC):
                ins = pe.transpose(tb2[:, i * P:(i + 1) * P], wdq[:, i * P:(i + 1) * P], core.identb[:, :])
            ins.then_inc(w_turned, 1)
            for r in range(2):
                pe.wait_ge(col_ready, r + 1)
                pe.transpose(bank[7][0:1, 0:P], col[:, :], core.ident[:, :]).then_inc(col_turned, 1)
                pe.wait_ge(top_ready, r + 1)
                pe.matmul(bank[7][:, 128:129], core.ones[0:1, :], top[:, :], start=True, stop=True).then_inc(top_spread, 1)
                if r == 0:
                    pe.wait_ge(xq_ready, 1)
                    pe.wait_ge(w_ready, 1)
                    for n, (c, i) in enumerate(work):
                        if n >= 2:
                            pe.wait_ge(gu_read, n - 1)
                        rhs = xq[:, c * 512:(c + 1) * 512]
                        pe.matmul(bank[2 + n % 2][0:pad(i), :], wgu[:, i, 0:pad(i)], rhs, start=True, stop=True)
                        pe.matmul(bank[4 + n % 2][0:pad(i), :], wgu[:, NC + i, 0:pad(i)], rhs,
                                  start=True, stop=True).then_inc(gu_ready, 1)
            pe.wait_ge(xq_ready, 2)
            pe.wait_ge(gu_read, 2 * NC)
            for c in range(2):
                for i in range(NC):
                    ins = pe.matmul(bank[2 + c][:, :], wd[:, i, :], hq[:, i, c * 512:(c + 1) * 512],
                                    start=(i == 0), stop=(i == NC - 1))
                ins.then_inc(down_ready, 1)
            for c in range(2):
                pe.wait_ge(scaled, c + 1)
                for t in range(4):
                    ins = pe.transpose(bank[4 + c][:, t * P:(t + 1) * P], oT[:, (4 * c + t) * P:(4 * c + t + 1) * P],
                                       core.ident[:, :])
                ins.then_inc(out_turned, 1)

        @block.scalar
        def _(act):
            act.activation(sig[:, :], clips, ACT.Exp, scale=-1.0).then_inc(exp_done, 1)
            act.wait_ge(w_turned, 1)
            act.activation(wgu[:, :, :], tb[:, 0:2 * NC * P].rearrange("p (i q) -> p i q", q=P), ACT.Copy).then_inc(w_copied, 1)
            act.activation(wd[:, :, :], tb2[:, 0:NC * P].rearrange("p (i q) -> p i q", q=P), ACT.Copy).then_inc(w_copied, 1)
            act.wait_ge(w_copied, 2)
            act.activation(gs[0:1, 0, 0:1], core.ones[0:1, 0:1], ACT.Silu).then_inc(w_ready, 1)
            act.wait_ge(w_ready, 1)
            for n, (c, i) in enumerate(work):
                act.wait_ge(gu_ready, n + 1)
                if n == 0:
                    act.wait_ge(top_done, 1)
                if n >= 2:
                    act.wait_ge(gu_read, n - 1)
                act.activation(gs[0:pad(i), n % 2, :], bank[2 + n % 2][0:pad(i), :], ACT.Silu,
                               scale=fs[0:pad(i), i:i + 1]).then_inc(silu_done, 1)

        @block.vector
        def _(dve):
            link = Link(dve, chain)
            link(dve.tensor_reduce(am[:, 0:2 * NC], w_gu, X, ALU.max, apply_absolute_value=True))
            link(dve.tensor_reduce(am[:, 2 * NC:], w_down, X, ALU.max, apply_absolute_value=True))
            link(dve.tensor_scalar(am[:, :], am[:, :], 1.0 / 127.0, None, ALU.mult))
            link(dve.reciprocal(inv[:, :], am[:, :]))
            for i in range(2 * NC):
                dve.tensor_scalar(wr[:, i, :], w_gu[:, i, :], inv[:, i:i + 1], ROUND, ALU.mult, ALU.add)
            link(dve.tensor_scalar(wdn[:, 0:FF2], w_down, inv[:, 2 * NC:], ROUND, ALU.mult, ALU.add))
            dve.tensor_scalar(wqn[:, :, :], wr[:, :, :], ROUND, 127.0, ALU.subtract, ALU.min).then_inc(w_quantized, 1)
            dve.memset(wdq[:, FF2:], 0.0)
            dve.memset(h[96:P, NC - 1, :], 0.0)
            dve.tensor_scalar(wdq[:, 0:FF2], wdn[:, 0:FF2], ROUND, 127.0, ALU.subtract, ALU.min).then_inc(w_quantized, 1)
            dve.wait_ge(exp_done, 1)
            link(dve.tensor_scalar(sig[:, :], sig[:, :], 1.0, None, ALU.add))
            link(dve.reciprocal(sig[:, :], sig[:, :]))

            def scale_of(r, data):
                dve.tensor_reduce(col[:, :], data, X if r == 0 else mybir.AxisListType.XY, ALU.max,
                                  apply_absolute_value=True).then_inc(col_ready, 1)
                dve.wait_ge(col_turned, r + 1)
                dve.tensor_reduce(top[:, :], bank[7][0:1, 0:P], X, ALU.max).then_inc(top_ready, 1)
                dve.wait_ge(top_spread, r + 1)
                link(dve.tensor_scalar(sx[:, r:r + 1], bank[7][:, 128:129], sig[:, r:r + 1], 1.0 / 127.0, ALU.mult, ALU.mult))
                link(dve.reciprocal(rx[:, r:r + 1], sx[:, r:r + 1]))

            scale_of(0, core.xnT[:, :])
            dve.tensor_scalar(fs[:, :], am[:, :], sx[:, 0:1], None, ALU.mult).then_inc(top_done, 1)
            link(dve.tensor_scalar(xr[:, :], core.xnT[:, :], rx[:, 0:1], ROUND, ALU.mult, ALU.add))
            link(dve.tensor_scalar(xr[:, :], xr[:, :], ROUND, 127.0, ALU.subtract, ALU.min))
            dve.tensor_scalar(xq[:, :], xr[:, :], -128.0, None, ALU.max).then_inc(xq_ready, 1)
            dve.wait_ge(top_done, 1)
            for n, (c, i) in enumerate(work):
                dve.wait_ge(silu_done, n + 1)
                dve.scalar_tensor_tensor(h[0:pad(i), i, c * 512:(c + 1) * 512], bank[4 + n % 2][0:pad(i), :],
                                         fs[0:pad(i), NC + i:NC + i + 1], gs[0:pad(i), n % 2, :],
                                         ALU.mult, ALU.mult).then_inc(gu_read, 1)
            dve.wait_ge(gu_read, 2 * NC)
            scale_of(1, h[:, :, :])
            link(dve.tensor_scalar(h[:, :, :], h[:, :, :], rx[:, 1:2], ROUND, ALU.mult, ALU.add))
            link(dve.tensor_scalar(h[:, :, :], h[:, :, :], ROUND, 127.0, ALU.subtract, ALU.min))
            dve.tensor_scalar(hq[:, :, :], h[:, :, :], -128.0, None, ALU.max).then_inc(xq_ready, 1)
            link(dve.tensor_scalar(fs[:, 2 * NC:], am[:, 2 * NC:], sx[:, 1:2], None, ALU.mult))
            for c in range(2):
                dve.wait_ge(down_ready, c + 1)
                dve.tensor_scalar(oT[:, c * 512:(c + 1) * 512], bank[2 + c][:, :], fs[:, 2 * NC:], None,
                                  ALU.mult).then_inc(scaled, 1)
            for c in range(2):
                dve.wait_ge(out_turned, c + 1)
                link(dve.tensor_tensor(core.x[:, 4 * c:4 * c + 4, :], core.x[:, 4 * c:4 * c + 4, :],
                                       bank[4 + c][:, :].rearrange("p (t d) -> p t d", d=D), ALU.add))


def ffn3_stage(core, u1, v1, b1, u2, v2, b2):
    nc = core.nc
    names = ("p_ready", "p_out", "h_ready", "gelu_done", "q_ready", "q_out", "o_ready", "biased", "added", "stored")
    p_ready, p_out, h_ready, gelu_done, q_ready, q_out, o_ready, biased, added, stored = (core.sem("ffn3_" + s) for s in names)
    NC = FF3 // P
    with ExitStack() as ctx:
        pT = core.sb(ctx, "ffn3_pT", [RANK, B * S], F32)
        hT = core.sb(ctx, "ffn3_hT", [P, 2, NC, 512], F32)
        qT = core.sb(ctx, "ffn3_qT", [RANK, B * S], F32)
        block = ctx.enter_context(nc.Block())
        bank = core.bank
        half = lambda c: slice(c * 512, (c + 1) * 512)

        @block.tensor
        def _(pe):
            for c in range(2):
                pe.matmul(bank[c][0:RANK, :], u1, core.xnT[:, half(c)], start=True, stop=True).then_inc(p_ready, 1)
            for c in range(2):
                pe.wait_ge(p_out, c + 1)
                for i in range(NC):
                    if c:
                        pe.wait_ge(gelu_done, i + 1)
                    pe.matmul(bank[2 + i][:, :], v1[:, i * P:(i + 1) * P], pT[:, half(c)],
                              start=True, stop=True).then_inc(h_ready, 1)
            for c in range(2):
                pe.wait_ge(gelu_done, NC * (c + 1))
                for i in range(NC):
                    ins = pe.matmul(bank[c][0:RANK, :], u2[:, i, :], hT[:, c, i, :], start=(i == 0), stop=(i == NC - 1))
                ins.then_inc(q_ready, 1)
            for c in range(2):
                pe.wait_ge(q_out, c + 1)
                for t in range(4):
                    ins = pe.matmul(bank[6 + c][:, t * D:(t + 1) * D], qT[:, (4 * c + t) * P:(4 * c + t + 1) * P], v2,
                                    start=True, stop=True)
                ins.then_inc(o_ready, 1)

        @block.scalar
        def _(act):
            for c in range(2):
                for i in range(NC):
                    act.wait_ge(h_ready, NC * c + i + 1)
                    act.activation(hT[:, c, i, :], bank[2 + i][:, :], ACT.Gelu_apprx_tanh, bias=b1[:, i:i + 1]).then_inc(gelu_done, 1)

        @block.vector
        def _(dve):
            for c in range(2):
                dve.wait_ge(p_ready, c + 1)
                dve.tensor_copy(pT[:, half(c)], bank[c][0:RANK, :]).then_inc(p_out, 1)
            dve.tensor_tensor(core.x[:, :, :], core.x[:, :, :], b2.unsqueeze(1).broadcast_to([P, TT, D]), ALU.add).then_inc(biased, 1)
            for c in range(2):
                dve.wait_ge(q_ready, c + 1)
                dve.tensor_copy(qT[:, half(c)], bank[c][0:RANK, :]).then_inc(q_out, 1)
            dve.wait_ge(biased, 1)
            for c in range(2):
                dve.wait_ge(o_ready, c + 1)
                dve.tensor_tensor(core.x[:, 4 * c:4 * c + 4, :], core.x[:, 4 * c:4 * c + 4, :],
                                  bank[6 + c][:, :].rearrange("p (t d) -> p t d", d=D), ALU.add).then_inc(added, 1)

        @block.sync
        def _(sp):
            out = core.inp["out"].rearrange("(t p) d -> p t d", p=P)
            for c in range(2):
                sp.wait_ge(added, c + 1)
                sp.dma_start(out[:, 4 * c:4 * c + 4, :], core.x[:, 4 * c:4 * c + 4, :]).then_inc(stored, 16)
            sp.wait_ge(stored, 32)


def small_head_layer(core, name, acc, q_src_affine, mask_tile, from_ctx, qkv_w, worep, qk_bias, v_bias, wo_t, bo):
    nc = core.nc
    nb, cols = (B, SCP) if from_ctx else (1, B * S)
    nk = SC if from_ctx else S
    kts = (nk + P - 1) // P
    k_parts = nc.dram_tensor(name + "_k_parts", (3, P, nb, cols), BF16, kind="Internal").ap()
    q_parts = nc.dram_tensor(name + "_q_parts", (3, P, B * S), BF16, kind="Internal").ap()
    v_rows = nc.dram_tensor(name + "_v_rows", (nb, P, HEADS, cols // P * 8), F32, kind="Internal").ap()
    split_project_stage(core, name + "_proj", qkv_w, qk_bias, 8.0 ** -0.5, from_ctx, k_parts, q_parts, v_rows)
    if v_bias is not None:
        bias_stage(core, name + "_bias", acc, v_bias, wo_t, bo)
    STACK = 72
    with ExitStack() as ctx:
        ks = core.sb(ctx, name + "_ks", [P, 2, nk], BF16)
        qs = core.sb(ctx, name + "_qs", [P, 2, S], BF16)
        vs = core.sb(ctx, name + "_vs", [P, 2, kts, 8], F32)
        clear = core.sem(name + "_cleared")
        with nc.Block() as block:
            @block.vector
            def _(dve):
                dve.memset(ks[:, :, :], 0.0).then_inc(clear, 1)
                dve.memset(qs[:, :, :], 0.0).then_inc(clear, 1)
                dve.wait_ge(clear, 2)

        def load(sp, b, h, k, sem):
            keys = (k_parts[:, bass.ds(h * 8, 8), b, 0:nk] if from_ctx else
                    k_parts[:, bass.ds(h * 8, 8), 0, bass.ds(b * S, S)])
            queries = q_parts[:, bass.ds(h * 8, 8), bass.ds(b * S, S)]
            for i in range(3):
                sp.dma_start(ks[24 * i:24 * i + 24, k, :], keys[i].unsqueeze(0).broadcast_to([3, 8, nk])).then_inc(sem, 16)
                sp.dma_start(qs[24 * i:24 * i + 24, k, :], queries).then_inc(sem, 16)

        def load_values(sp, b, h, k, sem):
            values = (v_rows[b, :, h, :] if from_ctx else v_rows[0, :, h, bass.ds(b * kts * 8, kts * 8)])
            sp.dma_start(vs[:, k, :, :], values.rearrange("p (t d) -> p t d", d=8)).then_inc(sem, 16)

        attention_stage(core, name + "_attn", acc, worep, HEADS, 8, nk, load, 6, load_values,
                        lambda k, b, at, w: ks[:, k, at:at + w],
                        lambda k, qt: qs[:, k, qt * P:(qt + 1) * P],
                        lambda k, kt: vs[:, k, kt, :], mask_tile)


def wide_head_layer(core, name, acc, heads, dh, wq_blocks, wk_blocks, bq, wv, worep, zeros):
    nc = core.nc
    blocks = heads * dh // P
    per = heads // blocks
    qk = nc.dram_tensor(name + "_qk", (blocks, P, per, B * S), F32, kind="Internal").ap()
    v_rows = nc.dram_tensor(name + "_v_rows", (B, P, heads, KT * dh), F32, kind="Internal").ap()
    wide_project_stage(core, name + "_proj", heads, dh, wq_blocks, wk_blocks, bq, float(dh) ** -0.5, wv, qk, v_rows)
    with ExitStack() as ctx:
        qs = core.sb(ctx, name + "_qs", [P, 2, S], F32)
        vs = core.sb(ctx, name + "_vs", [P, 2, KT, dh], F32)

        def load(sp, b, h, k, sem):
            m, j = (h // per, h % per) if per > 1 else (h, 0)
            sp.dma_start(qs[:, k, :], qk[m, :, j, bass.ds(b * S, S)]).then_inc(sem, 16)

        def load_values(sp, b, h, k, sem):
            sp.dma_start(vs[:, k, :, :], v_rows[b, :, h, :].rearrange("p (t d) -> p t d", d=dh)).then_inc(sem, 16)

        attention_stage(core, name + "_attn", acc, worep, heads, dh, SC, load, 1, load_values,
                        lambda k, b, at, w: core.ctxT[:, b, at:at + w],
                        lambda k, qt: qs[:, k, qt * P:(qt + 1) * P],
                        lambda k, kt: vs[:, k, kt, :], zeros)


def zero_mask_stage(core, name, tile):
    done = core.sem(name)
    with core.nc.Block() as block:
        @block.vector
        def _(dve):
            dve.memset(tile, 0.0).then_inc(done, 1)
            dve.wait_ge(done, 1)


LIMIT = 8


def build(nc, inp):
    with ExitStack() as top:
        core = Core(nc, top, inp)
        start_stage(core)

        def finish():
            done = core.sem("early_out")
            with nc.Block() as block:
                @block.sync
                def _(sp):
                    sp.dma_start(inp["out"].rearrange("(t p) d -> p t d", p=P), core.x[:, :, :]).then_inc(done, 16)
                    sp.wait_ge(done, 16)

        with ExitStack() as ctx:
            sb = lambda n, shape, dt=F32: core.sb(ctx, n, shape, dt)
            w, worep, wot = sb("a0_w", [P, 3, D]), sb("a0_worep", [P, HEADS, D]), sb("a0_wot", [P, D])
            cols, bo = sb("a0_cols", [P, 3]), sb("a0_bo", [P, D])
            mask = sb("a0_mask", [P, 2, SC])
            layernorm_stage(core, "ln0a", core.x, core.xn, core.xnT, loads=[
                (w[:, :, :], inp["a0_w"]), (worep[:, :, :], inp["a0_worep"]), (wot[:, :], inp["a0_wot"]),
                (cols[:, :], inp["a0_cols"]), (bo[:, :], inp["a0_bo"].partition_broadcast(P)),
                (mask[:, :, :], inp["mask0"].rearrange("(t p) k -> p t k", p=P))])
            scaled = core.sem("a0_mask_scaled")
            with nc.Block() as block:
                @block.vector
                def _(dve):
                    dve.tensor_scalar(mask[:, :, :], mask[:, :, :], -1e9, None, ALU.mult).then_inc(scaled, 1)
                    dve.wait_ge(scaled, 1)
            small_head_layer(core, "a0", core.x, None, lambda qt, at, n: mask[:, qt, at:at + n], True,
                             w, worep, cols, cols[:, 2:3], wot[:, :], bo[:, :])
        core.end_layer()
        if LIMIT == 1:
            return finish()
        with ExitStack() as ctx:
            w = core.sb(ctx, "f0_w", [P, 3, FF0], F32)
            layernorm_stage(core, "ln0f", core.x, core.xn, loads=[(w[:, :, :], inp["f0_w"])])
            ffn0_stage(core, w)
        core.end_layer()
        if LIMIT == 2:
            return finish()
        with ExitStack() as ctx:
            sb = lambda n, shape, dt=F32: core.sb(ctx, n, shape, dt)
            wv, wot, cols, bo = sb("a1_wv", [P, D]), sb("a1_wot", [P, 1, D]), sb("a1_cols", [P, 2]), sb("a1_bo", [P, D])
            zeros = sb("a1_zeros", [P, 512])
            layernorm_stage(core, "ln1a", core.x, core.xn, core.xnT, loads=[
                (wv[:, :], inp["a1_wv"]), (wot[:, 0, :], inp["a1_wot"]), (cols[:, :], inp["a1_cols"]),
                (bo[:, :], inp["a1_bo"].partition_broadcast(P))])
            zero_mask_stage(core, "a1_zeroed", zeros[:, :])
            bias_stage(core, "a1_bias", core.x, cols[:, 1:2], wot[:, 0, :], bo[:, :])
            wide_head_layer(core, "a1", core.x, 1, D, [inp["a1_wq"]], [inp["a1_wk"].unsqueeze(1)],
                            cols[:, 0:1], wv, wot, lambda qt, at, n: zeros[:, 0:n])
        core.end_layer()
        if LIMIT == 3:
            return finish()
        with ExitStack() as ctx:
            sb = lambda n, shape, dt=F32: core.sb(ctx, n, shape, dt)
            y = sb("f1_y", [P, TT, D])
            layernorm_stage(core, "ln1f", core.x, y)
            with ExitStack() as inner:
                sbi = lambda n, shape, dt=F32: core.sb(inner, n, shape, dt)
                w, worep, zeros = sbi("m1_w", [P, 3, D]), sbi("m1_worep", [P, HEADS, D]), sbi("m1_zeros", [P, 512])
                layernorm_stage(core, "ln1s", y, core.xn, core.xnT, affine=(inp["ln1_w"], inp["ln1_b"]), loads=[
                    (w[:, :, :], inp["m1_w"]), (worep[:, :, :], inp["m1_worep"])])
                zero_mask_stage(core, "m1_zeroed", zeros[:, :])
                small_head_layer(core, "m1", y, None, lambda qt, at, n: zeros[:, 0:n], False,
                                 w, worep, zeros, None, None, None)
            gw, gb, rank = sb("e1_gw", [P, EXPERTS]), sb("e1_gb", [P, EXPERTS]), sb("e1_rank", [P, EXPERTS])
            layernorm_stage(core, "ln1e", y, core.xn, core.xnT, affine=(inp["ln2_w"], inp["ln2_b"]), loads=[
                (gw[:, :], inp["e1_gw"]), (gb[:, :], inp["e1_gb"].partition_broadcast(P)),
                (rank[:, :], inp["rank"].partition_broadcast(P))])
            moe_stage(core, y, core.xnT, inp["e1_w1"], inp["e1_w2"], gw[:, :], gb[:, :], rank[:, :])
        core.end_layer()
        if LIMIT == 4:
            return finish()
        with ExitStack() as ctx:
            sb = lambda n, shape, dt=F32: core.sb(ctx, n, shape, dt)
            wv, worep, zeros = sb("a2_wv", [P, 1024]), sb("a2_worep", [P, HEADS, D]), sb("a2_zeros", [P, 512])
            layernorm_stage(core, "ln2a", core.x, core.xn, core.xnT, loads=[
                (wv[:, :], inp["a2_wv"]), (worep[:, :, :], inp["a2_worep"])])
            zero_mask_stage(core, "a2_zeroed", zeros[:, :])
            wide_head_layer(core, "a2", core.x, HEADS, 64, inp["a2_wq"], inp["a2_wk"], zeros[:, 0:1], wv, worep,
                            lambda qt, at, n: zeros[:, 0:n])
        core.end_layer()
        if LIMIT == 5:
            return finish()
        with ExitStack() as ctx:
            sb = lambda n, shape, dt=F32: core.sb(ctx, n, shape, dt)
            wgu, wdn, clips = sb("f2_wgu", [P, 6, D]), sb("f2_wdn", [P, FF2]), sb("f2_clips", [P, 2])
            layernorm_stage(core, "ln2f", core.x, core.xn, core.xnT, loads=[
                (wgu[:, :, :], inp["f2_wgu"]), (wdn[:, :], inp["f2_wdn"]),
                (clips[:, 0:1], inp["f2_clip_x"].partition_broadcast(P)),
                (clips[:, 1:2], inp["f2_clip_down"].partition_broadcast(P))])
            ffn2_stage(core, wgu[:, :, :], wdn[:, :], clips[:, :])
        core.end_layer()
        if LIMIT == 6:
            return finish()
        with ExitStack() as ctx:
            sb = lambda n, shape, dt=F32: core.sb(ctx, n, shape, dt)
            w, worep, wot = sb("a3_w", [P, 3, D]), sb("a3_worep", [P, HEADS, D]), sb("a3_wot", [P, D])
            cols, bo = sb("a3_cols", [P, 3]), sb("a3_bo", [P, D])
            mask = sb("a3_mask", [P, 2, SC])
            with ExitStack() as inner:
                seen = core.sb(inner, "a3_seen", [P, 2, SC], I32)
                layernorm_stage(core, "ln3a", core.x, core.xn, core.xnT, loads=[
                    (w[:, :, :], inp["a3_w"]), (worep[:, :, :], inp["a3_worep"]), (wot[:, :], inp["a3_wot"]),
                    (cols[:, :], inp["a3_cols"]), (bo[:, :], inp["a3_bo"].partition_broadcast(P)),
                    (seen[:, :, :], inp["mask3"].rearrange("(t p) k -> p t k", p=P))])
                scaled3 = core.sem("a3_mask_scaled")
                with nc.Block() as block:
                    @block.vector
                    def _(dve):
                        dve.tensor_scalar(mask[:, :, :], seen[:, :, :], 0.0, MASKED, ALU.is_equal,
                                          ALU.mult).then_inc(scaled3, 1)
                        dve.wait_ge(scaled3, 1)
            small_head_layer(core, "a3", core.x, None, lambda qt, at, n: mask[:, qt, at:at + n], True,
                             w, worep, cols, cols[:, 2:3], wot[:, :], bo[:, :])
        core.end_layer()
        if LIMIT == 7:
            return finish()
        with ExitStack() as ctx:
            sb = lambda n, shape, dt=F32: core.sb(ctx, n, shape, dt)
            u1, v1, b1 = sb("f3_u1", [P, RANK]), sb("f3_v1", [RANK, FF3]), sb("f3_b1", [P, FF3 // P])
            u2, v2, b2 = sb("f3_u2", [P, FF3 // P, RANK]), sb("f3_v2", [RANK, D]), sb("f3_b2", [P, D])
            layernorm_stage(core, "ln3f", core.x, core.xn, core.xnT, loads=[
                (u1[:, :], inp["f3_u1"]), (v1[:, :], inp["f3_v1"]), (b1[:, :], inp["f3_b1"]),
                (u2[:, :, :], inp["f3_u2"]), (v2[:, :], inp["f3_v2"]), (b2[:, :], inp["f3_b2"].partition_broadcast(P))])
            ffn3_stage(core, u1[:, :], v1[:, :], b1, u2, v2[:, :], b2[:, :])


def lay_out(inputs):
    g = {k: np.asarray(v) for k, v in inputs.items()}
    a = {"x": g["x"].reshape(B * S, D), "ident": np.eye(P, dtype=np.float32)}
    ctxT = np.zeros((P, B, SCP), np.float32)
    ctxT[:, :, :SC] = g["ctx_1024"].transpose(2, 0, 1)
    a["ctxT"] = ctxT
    a["mask0"] = g["mask_SxS2_fk1"]
    a["mask3"] = g["mask_1x1xSxS2_ik0"].reshape(S, SC)
    a["rank"] = np.arange(EXPERTS, 0, -1).astype(np.float32)

    def replicate(wo_rows, dh):
        H = wo_rows.shape[0] // dh
        tile = max(dh, 32)
        out = np.zeros((P, H, D), np.float32)
        for j in range(P // tile):
            out[j * tile:j * tile + dh] = wo_rows.reshape(H, dh, D).transpose(1, 0, 2)
        return out

    for n, pre in (("a0", "L0_xattn_"), ("a3", "L3_xattn_")):
        a[n + "_w"] = np.stack([g[pre + k].T for k in ("Wq", "Wk", "Wv")], 1)
        a[n + "_worep"] = replicate(g[pre + "Wo"].T, 8)
        a[n + "_wot"] = g[pre + "Wo"].T
        a[n + "_cols"] = np.stack([g[pre + k] for k in ("bq", "bk", "bv")], 1)
        a[n + "_bo"] = g[pre + "bo"]
    a["f0_w"] = np.stack([g["L0_ffn_w_gate"].T, g["L0_ffn_w_up"].T,
                          g["L0_ffn_w_down"].T.reshape(4, P, D).transpose(1, 0, 2).reshape(P, FF0)], 1)
    a["a1_wq"], a["a1_wk"], a["a1_wv"] = g["L1_xattn_Wq"].T, g["L1_xattn_Wk"], g["L1_xattn_Wv"].T
    a["a1_wot"], a["a1_bo"] = g["L1_xattn_Wo"].T, g["L1_xattn_bo"]
    a["a1_cols"] = np.stack([g["L1_xattn_bq"], g["L1_xattn_bv"]], 1)
    a["m1_w"] = g["L1_ffn_w_qkv"].reshape(D, 3, D)
    a["m1_worep"] = replicate(g["L1_ffn_w_proj"], 8)
    for k in ("ln1_w", "ln1_b", "ln2_w", "ln2_b"):
        a[k] = g["L1_ffn_" + k]
    a["e1_gw"], a["e1_gb"] = g["L1_ffn_gate_w"], g["L1_ffn_gate_b"]
    a["e1_w1"] = g["L1_ffn_w1"]
    a["e1_w2"] = g["L1_ffn_w2"].reshape(EXPERTS, 4, P, D).transpose(0, 2, 1, 3)
    a["a2_wq"] = g["L2_xattn_w_q"].reshape(D, 8, P).transpose(1, 0, 2)
    wk = np.zeros((8, P, 2, P), np.float32)
    rows = g["L2_xattn_w_k"].T.reshape(8, 2, 64, D)
    for j in range(2):
        wk[:, 64 * j:64 * (j + 1), j] = rows[:, j]
    a["a2_wk"] = wk
    a["a2_wv"] = g["L2_xattn_w_v"]
    a["a2_worep"] = replicate(g["L2_xattn_w_o"], 64)
    gu = np.ones((2, 3 * P, D), np.float32)
    gu[0, :FF2], gu[1, :FF2] = g["L2_ffn_w_gate"], g["L2_ffn_w_up"]
    a["f2_wgu"] = gu.reshape(6, P, D).transpose(1, 0, 2)
    a["f2_wdn"] = g["L2_ffn_w_down"]
    a["f2_clip_x"], a["f2_clip_down"] = g["L2_ffn_clip_x"], g["L2_ffn_clip_down"]
    a["f3_u1"], a["f3_v1"] = g["L3_ffn_U1"], g["L3_ffn_V1"]
    a["f3_b1"] = g["L3_ffn_b1"].reshape(4, P).T
    a["f3_u2"] = g["L3_ffn_U2"].reshape(4, P, RANK).transpose(1, 0, 2)
    a["f3_v2"], a["f3_b2"] = g["L3_ffn_V2"], g["L3_ffn_b2"]
    return {k: np.ascontiguousarray(v) for k, v in a.items()}


def kernel(**inputs):
    import concourse.bacc as bacc
    from concourse.bass_utils import run_bass_kernel_spmd

    nc = bacc.Bacc("TRN2", target_bir_lowering=False, num_devices=1)
    arrays = lay_out(inputs)
    inp = {n: nc.dram_tensor("in_" + n, a.shape, mybir.dt.from_np(a.dtype), kind="ExternalInput").ap()
           for n, a in arrays.items()}
    inp["out"] = nc.dram_tensor("out_x", (B * S, D), F32, kind="ExternalOutput").ap()
    build(nc, inp)
    r = run_bass_kernel_spmd(nc, [{"in_" + n: a for n, a in arrays.items()}], core_ids=[0])
    return r.results[0]["out_x"].reshape(B, S, D)
```

```python
from contextlib import ExitStack

import numpy as np

import concourse.bass as bass
from concourse import mybir

F32 = mybir.dt.float32
BF16 = mybir.dt.bfloat16
I32 = mybir.dt.int32
ALU = mybir.AluOpType
ACT = mybir.ActivationFunctionType
X = mybir.AxisListType.X

P = 128
D = 128
B, S, SC = 4, 256, 1601
TT = B * S // P
KT = (SC + P - 1) // P
SCP = KT * P
HEADS = 16
ROUND = 12582912.0
LOWEST = -3.0e38
MASKED = -(2.0 ** 100)
LN_EPS = 1e-5
FF0 = 512
FF2 = 352
FF2_CHUNKS = [(0, 128), (128, 128), (256, 96)]
EXPERTS, HID = 8, 512
VCOLS = 9
TWO_ONES = float(np.array([0x3F803F80], np.uint32).view(np.float32)[0])
MAX_ROW = 96
FF3, RANK = 512, 32


def pipelined(eng, total, unroll, lag, step, peel=1):
    for v in range(min(peel, total // unroll)):
        for k in range(unroll):
            step(v, k)
    if total > unroll * peel:
        with eng.Fori(peel, total // unroll) as v:
            for k in range(unroll):
                step(v, k)
    for i in range(total, total + lag):
        step(i // unroll, i % unroll)


class Link:

    def __init__(self, eng, sem, per_step=0):
        self.eng, self.sem, self.per_step = eng, sem, per_step
        self.base, self.n = 0, 0

    def at(self, t):
        self.base, self.n = t * self.per_step, 0

    def __call__(self, ins):
        self.n += 1
        ins.then_inc(self.sem, 1)
        self.eng.wait_ge(self.sem, self.base + self.n)


class Core:

    def __init__(self, nc, ctx, inp):
        self.nc, self.ctx, self.inp = nc, ctx, inp
        self.sems = []
        self.x = self.sb(ctx, "x", [P, TT, D], F32)
        self.xn = self.sb(ctx, "xn", [P, TT, D], F32)
        self.xnT = self.sb(ctx, "xnT", [P, B * S], F32)
        self.ctxT = self.sb(ctx, "ctxT", [P, B, SCP], F32)
        self.ident = self.sb(ctx, "ident", [P, P], F32)
        self.identb = self.sb(ctx, "identb", [P, P], BF16)
        self.ones = self.sb(ctx, "ones", [P, P], F32)
        self.eps = self.sb(ctx, "eps", [P, 1], F32)
        self.bank = [ctx.enter_context(nc.psum_tensor(f"bank{i}", [P, 512], F32)) for i in range(4)]
        self.wide = [ctx.enter_context(nc.psum_tensor(f"wide{i}", [P, 1024], F32)) for i in range(2)]
        self.bank += [w[:, 512 * i:512 * (i + 1)] for w in self.wide for i in range(2)]

    def sb(self, ctx, name, shape, dt):
        return ctx.enter_context(self.nc.sbuf_tensor(name, shape, dt))

    def sem(self, name):
        self.sems.append(self.nc.alloc_semaphore(name=name))
        return self.sems[-1]

    def end_layer(self):
        self.nc.clear_and_free_semaphores(self.sems)
        self.nc.all_engine_barrier()
        self.sems = []


def start_stage(core):
    nc = core.nc
    loaded, made = core.sem("start_loaded"), core.sem("start_made")
    with nc.Block() as block:
        @block.sync
        def _(sp):
            sp.dma_start(core.x[:, :, :], core.inp["x"].rearrange("(t p) d -> p t d", p=P)).then_inc(loaded, 16)
            sp.dma_start(core.ident[:, :], core.inp["ident"]).then_inc(loaded, 16)
            sp.wait_ge(loaded, 16 * 2)

        @block.vector
        def _(dve):
            dve.memset(core.ones[:, :], 1.0)
            dve.memset(core.eps[:, :], LN_EPS)
            dve.wait_ge(loaded, 16 * 2)
            dve.tensor_copy(core.identb[:, :], core.ident[:, :]).then_inc(made, 1)
            dve.wait_ge(made, 1)


def layernorm_stage(core, name, src, dst, dstT=None, affine=None, loads=()):
    nc = core.nc
    loaded, affine_in = core.sem(name + "_loaded"), core.sem(name + "_affine_in")
    chain, dev_ready, dev_done = core.sem(name + "_chain"), core.sem(name + "_var"), core.sem(name + "_std")
    normed, turned, copied = core.sem(name + "_normed"), core.sem(name + "_turned"), core.sem(name + "_copied")
    with ExitStack() as ctx:
        stats = core.sb(ctx, name + "_stats", [P, TT, 6], F32)
        mv = core.sb(ctx, name + "_mv", [P, TT, 2], F32)
        var = core.sb(ctx, name + "_v", [P, TT], F32)
        std = core.sb(ctx, name + "_std", [P, TT], F32)
        rec = core.sb(ctx, name + "_rec", [P, TT], F32)
        wb = core.sb(ctx, name + "_wb", [P, 2, D], F32) if affine else None
        block = ctx.enter_context(nc.Block())

        @block.sync
        def _(sp):
            n = 0
            if affine:
                for i in range(2):
                    sp.dma_start(wb[:, i, :], affine[i].partition_broadcast(P)).then_inc(affine_in, 16)
            for tile, dram in loads:
                sp.dma_start(tile, dram).then_inc(loaded, 16)
                n += 1
            if n:
                sp.wait_ge(loaded, 16 * n)

        @block.scalar
        def _(act):
            act.wait_ge(dev_ready, 1)
            act.activation(std[:, :], var[:, :], ACT.Sqrt).then_inc(dev_done, 1)
            if dstT is not None:
                act.wait_ge(turned, 1)
                act.activation(dstT[:, 0:512], core.bank[0][:, :], ACT.Copy).then_inc(copied, 1)

        @block.tensor
        def _(pe):
            if dstT is not None:
                for t in range(TT):
                    pe.wait_ge(normed, t + 1)
                    ins = pe.transpose(core.bank[t // 4][:, (t % 4) * P:(t % 4 + 1) * P], dst[:, t, :], core.ident[:, :])
                    if t % 4 == 3:
                        ins.then_inc(turned, 1)

        @block.vector
        def _(dve):
            link = Link(dve, chain)
            for t in range(TT):
                ins = dve.bn_stats(stats[:, t, :], src[:, t, :])
            link(ins)
            for t in range(TT):
                ins = dve.bn_aggr(mv[:, t, :], stats[:, t, :])
            link(ins)
            dve.tensor_scalar(var[:, :], mv[:, :, 1], LN_EPS, None, ALU.add).then_inc(dev_ready, 1)
            dve.wait_ge(dev_done, 1)
            link(dve.reciprocal(rec[:, :], std[:, :]))
            dve.wait_ge(dev_ready, 1)
            link(dve.tensor_tensor(rec[:, :], rec[:, :], var[:, :], ALU.mult))
            link(dve.tensor_tensor(std[:, :], std[:, :], rec[:, :], ALU.add))
            link(dve.tensor_scalar(std[:, :], std[:, :], 0.5, None, ALU.mult))
            link(dve.reciprocal(rec[:, :], std[:, :]))
            if affine:
                dve.wait_ge(affine_in, 32)
            for t in range(TT):
                ins = dve.tensor_scalar(dst[:, t, :], src[:, t, :], mv[:, t, 0:1], rec[:, t:t + 1],
                                        ALU.subtract, ALU.mult)
                if affine:
                    link(ins)
                    link(dve.tensor_tensor(dst[:, t, :], dst[:, t, :], wb[:, 0, :], ALU.mult))
                    ins = dve.tensor_tensor(dst[:, t, :], dst[:, t, :], wb[:, 1, :], ALU.add)
                ins.then_inc(normed, 1)
            dve.wait_ge(normed, TT)
            if dstT is not None:
                dve.wait_ge(turned, 2)
                dve.tensor_copy(dstT[:, 512:1024], core.bank[1][:, :]).then_inc(copied, 1)


def split_project_stage(core, name, w, bias, scale, from_ctx, k_parts, q_stack, v_rows, clear, late_loads):
    nc = core.nc
    cols = SCP if from_ctx else B * S
    nb = B if from_ctx else 1
    kts = cols // P
    ck = cols // 4 if from_ctx else 512
    n_ck = cols // ck
    groups = [(g, min(4, kts - g)) for g in range(0, kts, 4)]
    ng = len(groups)
    q_ready, q_evac = core.sem(name + "_q_ready"), core.sem(name + "_q_evac")
    k_ready, k_evac = core.sem(name + "_k_ready"), core.sem(name + "_k_evac")
    v_ready, v_evac = core.sem(name + "_v_ready"), core.sem(name + "_v_evac")
    ctx_in = [core.sem(f"{name}_ctx_in{i}") for i in range(2)]
    part1, rest, part2, part3 = (core.sem(name + s) for s in ("_part1", "_rest", "_part2", "_part3"))
    qpart1, qrest, qpart2, qpart3 = (core.sem(name + s) for s in ("_qpart1", "_qrest", "_qpart2", "_qpart3"))
    q_stored, ones_in = core.sem(name + "_q_stored"), core.sem(name + "_ones_in")
    cleared, late = core.sem(name + "_cleared"), core.sem(name + "_late")
    k_stored = [core.sem(f"{name}_k_stored{i}") for i in range(2)]
    v_stored = [core.sem(f"{name}_v_stored{i}") for i in range(2)]
    with ExitStack() as ctx:
        ctxb = core.sb(ctx, name + "_ctxb", [P, 2, cols], F32) if from_ctx else None
        qf = core.sb(ctx, name + "_qf", [P, B * S], F32)
        qp = core.sb(ctx, name + "_qp", [P, 3, B * S], BF16)
        kf = core.sb(ctx, name + "_kf", [P, 2, cols], F32)
        kp = core.sb(ctx, name + "_kp", [P, 2, 3, cols], BF16)
        vb = core.sb(ctx, name + "_vb", [P, 2, HEADS, kts * VCOLS], F32)
        block = ctx.enter_context(nc.Block())
        kbank, vbank, qbank = core.bank[0:2], core.bank[2:4], core.bank[4:6]

        @block.sync
        def _(sp):
            if from_ctx:
                def load(v, k):
                    if isinstance(v, int) and 2 * v + k >= nb:
                        return
                    if not isinstance(v, int) or v > 0:
                        sp.wait_ge(v_ready, ng * (2 * v + k - 1))
                    sp.dma_start(ctxb[:, k, :], core.inp["ctxT"][:, 2 * v + k, :]).then_inc(ctx_in[k], 16)
                pipelined(sp, nb, 2, 0, load)
            for tile, dram in late_loads:
                sp.dma_start(tile, dram).then_inc(late, 16)
            if late_loads:
                sp.wait_ge(late, 16 * len(late_loads))

        @block.gpsimd
        def _(pool):
            clear(pool, cleared)
            pool.wait_ge(qpart3, 1)
            for j in range(3):
                for i in range(3):
                    pool.dma_start(q_stack[:, j, i, :, :], qp[:, j, :]).then_inc(q_stored, 16)

            def store(v, k):
                b = 2 * v + k
                pool.wait_ge(part3, b + 1)
                for i in range(3):
                    pool.dma_start(k_parts[b, :, i, :, :], kp[:, k, i, :]).then_inc(k_stored[k], 16)
                pool.wait_ge(v_evac, ng * (b + 1))
                pool.wait_ge(ones_in, 1)
                pool.dma_start(v_rows[b, :, :, :], vb[:, k, :, :]).then_inc(v_stored[k], 16)
            if nb == 1:
                store(0, 0)
            else:
                pipelined(pool, nb, 2, 0, store)
            pool.wait_ge(q_stored, 16 * 9)
            for k in range(min(nb, 2)):
                pool.wait_ge(k_stored[k], 48 * max(nb // 2, 1))
                pool.wait_ge(v_stored[k], 16 * max(nb // 2, 1))

        @block.tensor
        def _(pe):
            for c in range(2):
                pe.matmul(qbank[c][:, :], w[:, 0, :], core.xnT[:, c * 512:(c + 1) * 512],
                          start=True, stop=True).then_inc(q_ready, 1)

            def step(v, k):
                b = 2 * v + k
                first = isinstance(v, int) and b == 0
                src = ctxb[:, k, :] if from_ctx else core.xnT[:, :]
                if from_ctx:
                    pe.wait_ge(ctx_in[k], 16 * (v + 1))
                for c in range(n_ck):
                    if not (first and c < 2):
                        pe.wait_ge(k_evac, n_ck * b + c - 1)
                    pe.matmul(kbank[c % 2][:, 0:ck], w[:, 1, :], src[:, c * ck:(c + 1) * ck],
                              start=True, stop=True).then_inc(k_ready, 1)
                for g, (kt, m) in enumerate(groups):
                    if not (first and g < 2):
                        pe.wait_ge(v_evac, ng * b + g - 1)
                    for j in range(m):
                        ins = pe.matmul(vbank[g % 2][:, j * P:(j + 1) * P], src[:, (kt + j) * P:(kt + j + 1) * P],
                                        w[:, 2, :], start=True, stop=True)
                    ins.then_inc(v_ready, 1)
            if nb == 1:
                step(0, 0)
            else:
                pipelined(pe, nb, 2, 0, step)

        @block.scalar
        def _(act):
            act.wait_ge(q_evac, 2)
            act.activation(qp[:, 0, :], qf[:, :], ACT.Copy).then_inc(qpart1, 1)
            act.wait_ge(qrest, 1)
            act.activation(qp[:, 1, :], qf[:, :], ACT.Copy).then_inc(qpart2, 1)

            def step(v, k):
                b = 2 * v + k
                first = isinstance(v, int) and v == 0
                if not first:
                    act.wait_ge(part3, b - 1)
                for c in range(n_ck):
                    act.wait_ge(k_ready, n_ck * b + c + 1)
                    act.activation(kf[:, k, c * ck:(c + 1) * ck], kbank[c % 2][:, 0:ck], ACT.Identity,
                                   bias=bias[:, 1:2]).then_inc(k_evac, 1)
                act.wait_ge(k_evac, n_ck * (b + 1))
                if not first:
                    act.wait_ge(k_stored[k], 48 * v)
                act.activation(kp[:, k, 0, :], kf[:, k, :], ACT.Copy).then_inc(part1, 1)
                act.wait_ge(rest, b + 1)
                act.activation(kp[:, k, 1, :], kf[:, k, :], ACT.Copy).then_inc(part2, 1)
            if nb == 1:
                step(0, 0)
            else:
                pipelined(act, nb, 2, 0, step)

        @block.vector
        def _(dve):
            for c in range(2):
                dve.wait_ge(q_ready, c + 1)
                dve.tensor_scalar(qf[:, c * 512:(c + 1) * 512], qbank[c][:, :], bias[:, 0:1], scale,
                                  ALU.add, ALU.mult).then_inc(q_evac, 1)
            dve.memset(vb[:, :, :, :].rearrange("p k h (t d) -> p (k h t) d", d=VCOLS)[:, :, 8:9], 1.0).then_inc(ones_in, 1)
            dve.wait_ge(qpart1, 1)
            dve.wait_ge(q_evac, 2)
            dve.tensor_tensor(qf[:, :], qf[:, :], qp[:, 0, :], ALU.subtract).then_inc(qrest, 1)
            dve.wait_ge(qpart2, 1)
            dve.wait_ge(qrest, 1)
            dve.tensor_tensor(qp[:, 2, :], qf[:, :], qp[:, 1, :], ALU.subtract).then_inc(qpart3, 1)

            def step(v, k):
                b = 2 * v + k
                first = isinstance(v, int) and v == 0
                dve.wait_ge(part1, b + 1)
                dve.tensor_tensor(kf[:, k, :], kf[:, k, :], kp[:, k, 0, :], ALU.subtract).then_inc(rest, 1)
                for g, (kt, m) in enumerate(groups):
                    dve.wait_ge(v_ready, ng * b + g + 1)
                    if g == 0 and not first:
                        dve.wait_ge(v_stored[k], 16 * v)
                    out = vb[:, k, :, kt * VCOLS:(kt + m) * VCOLS].rearrange("p h (t d) -> p t h d", d=VCOLS)[:, :, :, 0:8]
                    src = vbank[g % 2][:, 0:m * P].rearrange("p (t h d) -> p t h d", t=m, h=HEADS)
                    for j in range(m):
                        ins = dve.tensor_copy(out[:, j], src[:, j])
                    ins.then_inc(v_evac, 1)
                dve.wait_ge(part2, b + 1)
                dve.wait_ge(rest, b + 1)
                dve.tensor_tensor(kp[:, k, 2, :], kf[:, k, :], kp[:, k, 1, :], ALU.subtract).then_inc(part3, 1)
            if nb == 1:
                step(0, 0)
            else:
                pipelined(dve, nb, 2, 0, step)


def attention_stage(core, name, acc, wo, heads, dh, nk, load_operands, dmas, load_values, scores_rhs, lhs, vtile, mask):
    nc = core.nc
    units, kts = B * heads, (nk + P - 1) // P
    tiles = 2 * units
    UN = 8
    RING = UN // 2
    EXP, TURN, RECIP, PV, OUT, ACC = 1, 3, 3, 4, 5, 6
    chunks = [(c, min(512, nk - c)) for c in range(0, nk, 512)]
    nch = len(chunks)
    groups = [(g, min(4, kts - g)) for g in range(0, kts, 4)]
    ng = len(groups)
    col_tile = max(dh, 32)
    lanes = min(P // col_tile, kts)
    loaded = [core.sem(f"{name}_loaded{i}") for i in range(RING)]
    v_loaded = [core.sem(f"{name}_v_loaded{i}") for i in range(RING)]
    names = ("scores_ready", "scores_read", "max_ready", "exp_done", "turned", "pv_done", "u_out", "wo_done",
             "recip_done", "acc_done", "setup", "passed")
    (scores_ready, scores_read, max_ready, exp_done, turned, pv_done, u_out, wo_done, recip_done,
     acc_done, setup, passed) = (core.sem(f"{name}_{s}") for s in names)
    turned_out = [core.sem(f"{name}_turned_out{i}") for i in range(2)]
    s_bank, t_bank, u_bank, o_bank = core.bank[0:4], core.bank[4:6], core.bank[6], core.bank[7]
    with ExitStack() as ctx:
        sc = core.sb(ctx, name + "_sc", [P, 4, nk], F32)
        pr = core.sb(ctx, name + "_pr", [P, 4, kts * P], F32)
        prT = core.sb(ctx, name + "_prT", [P, 2, kts, P], F32)
        mx = core.sb(ctx, name + "_mx", [P, 2, nch], F32)
        nmx = core.sb(ctx, name + "_nmx", [P, 4], F32)
        tot = core.sb(ctx, name + "_tot", [P, 4], F32)
        rtot = core.sb(ctx, name + "_rtot", [P, 4], F32)
        u_sb = core.sb(ctx, name + "_u", [P, 2, P], F32)
        block = ctx.enter_context(nc.Block())

        def live(v, k, lag):
            return not isinstance(v, int) or 0 <= UN * v + k - lag < tiles

        def first(v, k, lag, n):
            return isinstance(v, int) and UN * v + k - lag < n

        def place(u):
            return (u // heads, u % heads) if heads > 1 else (u, 0)

        def turns(v, k, g):
            n = ng * (k - TURN) + g
            return n % 2, UN // 2 * ng * v + n // 2

        @block.sync
        def _(sp):
            def step(v, k):
                u = RING * v + k
                if not isinstance(v, int) or v > 0:
                    sp.wait_ge(scores_ready, nch * (2 * u - 6))
                load_operands(sp, *place(u), k, loaded[k])
                if not isinstance(v, int) or v > 0:
                    sp.wait_ge(pv_done, 2 * u - 6)
                load_values(sp, *place(u), k, v_loaded[k])
            pipelined(sp, units, RING, 0, step)

        @block.tensor
        def _(pe):
            def score_chunk(v, k, c):
                t = UN * v + k
                b, _ = place(RING * v + k // 2)
                if k % 2 == 0 and c == 0:
                    pe.wait_ge(loaded[k // 2], 16 * dmas * (v + 1))
                if not first(v, k, 0, 1):
                    pe.wait_ge(scores_read, nch * (t - 1) + c + 1)
                at, w = chunks[c]
                pe.matmul(s_bank[c][:, 0:w], lhs(k // 2, k % 2), scores_rhs(k // 2, b, at, w),
                          start=True, stop=True).then_inc(scores_ready, 1)

            def turn_group(v, k, g):
                t = UN * v + k - TURN
                kt, m = groups[g]
                bank, before = turns(v, k, g)
                if g == 0:
                    pe.wait_ge(setup, 1)
                    pe.wait_ge(exp_done, t + 1)
                if not (isinstance(v, int) and before == 0):
                    pe.wait_ge(turned_out[bank], before)
                for j in range(m):
                    ins = pe.transpose(t_bank[bank][:, j * P:(j + 1) * P],
                                       pr[:, (k - TURN) % 4, (kt + j) * P:(kt + j + 1) * P], core.ident[:, :])
                ins.then_inc(turned, 1)

            def value_group(v, k, g):
                t, c = UN * v + k - PV, (k - PV) // 2
                bank, before = turns(v, k - PV + TURN, g)
                pe.wait_ge(turned_out[bank], before + 1)
                if g == 0:
                    pe.wait_ge(v_loaded[c % RING], 16 * (v + c // RING + 1))
                    if not first(v, k, PV, 1):
                        pe.wait_ge(u_out, t)
                first_kt, m = groups[g]
                for kt in range(first_kt, first_kt + m):
                    j = kt % lanes
                    ins = pe.matmul(u_bank[j * col_tile:j * col_tile + dh, 0:P], vtile(c % RING, kt),
                                    prT[:, (k - PV) % 2, kt, :], start=(kt < lanes), stop=(kt >= kts - lanes))
                if g == ng - 1:
                    ins.then_inc(pv_done, 1)

            def step(v, k):
                for g in range(ng):
                    if live(v, k, TURN):
                        turn_group(v, k, g)
                    if live(v, k, 0):
                        score_chunk(v, k, g)
                    if live(v, k, PV) and g > 0:
                        value_group(v, k, g - 1)
                        if g == ng - 1:
                            value_group(v, k, g)
                    if g == 1 and live(v, k, OUT):
                        t = UN * v + k - OUT
                        _, h = place(RING * v + (k - OUT) // 2)
                        pe.wait_ge(u_out, t + 1)
                        if not first(v, k, OUT, 1):
                            pe.wait_ge(acc_done, t + 2)
                        pe.matmul(o_bank[:, 0:D], u_sb[:, (k - OUT) % 2, :], wo[:, h, :], start=True, stop=True).then_inc(wo_done, 1)
            pipelined(pe, tiles, UN, ACC, step)

        def copy_group(eng, copy, v, k, g):
            t = UN * v + k - TURN
            kt, m = groups[g]
            bank, _ = turns(v, k, g)
            eng.wait_ge(turned, ng * t + g + 1)
            if g < 2 and not first(v, k, TURN, 2):
                eng.wait_ge(pv_done, t - 1)
            copy(prT[:, (k - TURN) % 2, kt:kt + m, :],
                 t_bank[bank][:, 0:m * P].rearrange("p (t q) -> p t q", t=m)).then_inc(turned_out[bank], 1)

        @block.scalar
        def _(act):
            copy = lambda out, src: act.activation(out, src, ACT.Copy)

            def step(v, k):
                if live(v, k, TURN):
                    copy_group(act, copy, v, k, 0)
                if live(v, k, EXP):
                    t = UN * v + k - EXP
                    slot = (k - EXP) % 4
                    act.wait_ge(max_ready, t + 1)
                    if not first(v, k, EXP, 4):
                        act.wait_ge(turned, ng * (t - 3))
                        act.wait_ge(recip_done, t - 3)
                    act.activation(pr[:, slot, 0:nk], sc[:, slot, :], ACT.Exp, bias=nmx[:, slot:slot + 1],
                                   scale=1.0, accum_out=tot[:, slot:slot + 1]).then_inc(exp_done, 1)
                if live(v, k, TURN):
                    for g in range(2, ng):
                        copy_group(act, copy, v, k, g)
            pipelined(act, tiles, UN, ACC, step)

        @block.vector
        def _(dve):
            if kts * P > nk:
                dve.memset(pr[:, :, nk:], 0.0)
            dve.memset(u_bank[:, 0:P], 0.0).then_inc(setup, 1)
            dve.memset(nmx[:, :], 0.0).then_inc(acc_done, 2)

            def maxima(v, k, cs):
                t = UN * v + k
                for c in cs:
                    at, w = chunks[c]
                    dve.wait_ge(scores_ready, nch * t + c + 1)
                    if c == 0 and not first(v, k, 0, 4):
                        dve.wait_ge(exp_done, t - 3)
                    dve.sem_inc(passed, 1)
                    dve.tensor_tensor_reduce(sc[:, k % 4, at:at + w], s_bank[c][:, 0:w], mask(k % 2, at, w), 1.0,
                                             LOWEST, ALU.add, ALU.max, mx[:, k % 2, c:c + 1]).then_inc(scores_read, 1)

            def step(v, k):
                if live(v, k, ACC):
                    t = UN * v + k - ACC
                    b, _ = place(RING * v + (k - ACC) // 2)
                    dve.wait_ge(wo_done, t + 1)
                    dve.wait_ge(acc_done, t + 1)
                    dve.wait_ge(recip_done, t + 1)
                    tile = acc[:, 2 * b + k % 2, :]
                    slot = (k - ACC) % 4
                    dve.scalar_tensor_tensor(tile, o_bank[:, 0:D], rtot[:, slot:slot + 1], tile, ALU.mult,
                                             ALU.add).then_inc(acc_done, 1)
                if live(v, k, OUT):
                    t = UN * v + k - OUT
                    dve.wait_ge(pv_done, t + 1)
                    dve.tensor_copy(u_sb[:, (k - OUT) % 2, :], u_bank[:, 0:P]).then_inc(u_out, 1)
                if live(v, k, 0):
                    maxima(v, k, range(0, 1))
                if live(v, k, TURN):
                    copy_group(dve, dve.tensor_copy, v, k, 1)
                if live(v, k, 0):
                    maxima(v, k, range(1, nch))
                    dve.wait_ge(scores_read, nch * (UN * v + k + 1))
                    dve.tensor_reduce(nmx[:, k % 4:k % 4 + 1], mx[:, k % 2, :], X, ALU.max, negate=True).then_inc(max_ready, 1)
                if live(v, k, RECIP):
                    slot = (k - RECIP) % 4
                    dve.wait_ge(exp_done, UN * v + k - RECIP + 1)
                    dve.reciprocal(rtot[:, slot:slot + 1], tot[:, slot:slot + 1]).then_inc(recip_done, 1)
            pipelined(dve, tiles, UN, ACC, step)


def turned_attention_stage(core, name, acc, wo, nk, ring, share, lags, load_operands, dmas, load_values, ks, qs, qx, vs, mask,
                           maskT):
    nc = core.nc
    ROWS, EXP, PV, OUT, ACC = lags
    peel = 2 if ACC + 1 >= ring else 1
    units, kts = B * HEADS, (nk + P - 1) // P
    if mask:
        w = (nk + 3) // 4
        pieces = [[(qt, c, min(w, nk - c))] for qt in range(2) for c in range(0, nk, w)]
    else:
        pieces = [[(0, 0, nk), (1, 0, nk)]]
    npc = len(pieces)
    groups = [(g, min(4, kts - g)) for g in range(0, kts, 4)]
    ng = len(groups)
    lanes = min(4, kts)
    per = npc // ng
    o_at, r_at = min(1, ng - 1), min(2, ng - 1)
    loaded = [core.sem(f"{name}_loaded{i}") for i in range(ring // share)]
    v_loaded = [core.sem(f"{name}_v_loaded{i}") for i in range(ring // share)]
    names = ("scores_ready", "scores_read", "max_ready", "cut", "cut_done", "rows_ready", "rows_in", "turned_ready",
             "exp_done", "pv_done", "u_out", "wo_done", "recip_done", "acc_done", "setup", "passed")
    (scores_ready, scores_read, max_ready, cut, cut_done, rows_ready, rows_in, turned_ready, exp_done, pv_done,
     u_out, wo_done, recip_done, acc_done, setup, passed) = (core.sem(f"{name}_{s}") for s in names)
    s_bank, o_bank = core.bank[0:2], core.bank[3]
    shared = ng > 1
    r_bank = o_bank if shared else core.bank[5]
    u_banks = [core.bank[2]] if shared else [core.bank[2], core.bank[7]]
    nu = len(u_banks)
    with ExitStack() as ctx:
        junk = core.sb(ctx, name + "_junk", [P, 2, nk], F32) if mask else None
        prT = core.sb(ctx, name + "_prT", [P, 2, kts, S], F32)
        mx = core.sb(ctx, name + "_mx", [P, 2, 2, npc // 2], F32) if mask else None
        nmx = core.sb(ctx, name + "_nmx", [P, 2, 2], F32)
        rest = core.sb(ctx, name + "_rest", [P, 2], F32)
        zero = core.sb(ctx, name + "_zero", [P, 2], F32)
        parts = core.sb(ctx, name + "_parts", [P, 2, 2, 3], BF16)
        rtot = core.sb(ctx, name + "_rtot", [P, 2, 2], F32)
        u_sb = core.sb(ctx, name + "_u", [P, 2, S], F32)
        block = ctx.enter_context(nc.Block())

        def live(v, k, lag):
            return not isinstance(v, int) or 0 <= ring * v + k - lag < units

        def first(v, k, lag, n):
            return isinstance(v, int) and ring * v + k - lag < n

        def place(v, k, lag):
            u = ring * v + k - lag
            if share == 1:
                return u // HEADS, u % HEADS
            return (k - lag) % B, ring // B * v + (k - lag) // B

        @block.sync
        def _(sp):
            def step(v, k):
                u = ring * v + share * k
                if not isinstance(v, int) or v > 0:
                    sp.wait_ge(turned_ready, ng * (u - ring + share))
                load_operands(sp, *place(v, share * k, 0), k, loaded[k])
                if not isinstance(v, int) or v > 0:
                    sp.wait_ge(pv_done, u - ring + share)
                load_values(sp, *place(v, share * k, 0), k, v_loaded[k])
            pipelined(sp, units // share, ring // share, 0, step)

        @block.tensor
        def _(pe):
            def score_piece(v, k, n):
                if not live(v, k, 0):
                    return
                t = npc * (ring * v + k) + n
                bank = (npc * k + n) % 2
                if n == 0:
                    pe.wait_ge(loaded[k // share], 16 * dmas * (v + 1))
                if not (isinstance(v, int) and t < 2):
                    pe.wait_ge(scores_read if mask else max_ready, t - 1)
                for qt, at, w in pieces[n]:
                    col = qt * nk if len(pieces[n]) > 1 else 0
                    ins = pe.matmul(s_bank[bank][:, col:col + w], qs(k, qt), ks(k, at, w),
                                    start=True, stop=True)
                ins.then_inc(scores_ready, 1)

            def turned_group(v, k, g):
                u, c = ring * v + k - EXP, (k - EXP) % ring
                bank = core.wide[(ng * (k - EXP) + g) % 2]
                kt, m = groups[g]
                if g == 0:
                    pe.wait_ge(rows_in, u + 1)
                if not (isinstance(v, int) and ng * u + g < 2):
                    pe.wait_ge(exp_done, ng * u + g - 1)
                for j in range(m):
                    at, keys = (kt + j) * P, min(P, nk - (kt + j) * P)
                    out = bank[0:keys, j * S:(j + 1) * S]
                    if mask:
                        pe.matmul(out, core.identb[:, 0:keys], maskT(kt + j), start=True, stop=False)
                    ins = pe.matmul(out, ks(c, at, keys), qx(c), start=not mask, stop=True)
                ins.then_inc(turned_ready, 1)

            def value_group(v, k, g):
                u, c = ring * v + k - PV, (k - PV) % ring
                kt, m = groups[g]
                if g == 0:
                    pe.wait_ge(setup, 1 + nu)
                    pe.wait_ge(v_loaded[c // share], 16 * (v + (k - PV) // ring + 1))
                    if not first(v, k, PV, nu):
                        pe.wait_ge(u_out, u - nu + 1)
                pe.wait_ge(exp_done, ng * u + g + 1)
                for i in range(kt, kt + m):
                    j = i % lanes
                    ins = pe.matmul(u_banks[(k - PV) % nu][j * 32:j * 32 + VCOLS, 0:S], vs(c, i), prT[:, (k - PV) % 2, i, :],
                                    start=(i < lanes), stop=(i >= kts - lanes))
                if g == ng - 1:
                    ins.then_inc(pv_done, 1)

            def step(v, k):
                for g in range(ng):
                    score_piece(v, k, per * g)
                    if live(v, k, EXP):
                        turned_group(v, k, g)
                    for n in range(1, per):
                        score_piece(v, k, per * g + n)
                    if live(v, k, PV):
                        value_group(v, k, g)
                    if g == o_at and live(v, k, OUT):
                        u, (_, h) = ring * v + k - OUT, place(v, k, OUT)
                        pe.wait_ge(u_out, u + 1)
                        if shared and (live(v, k, ROWS + 1)):
                            pe.wait_ge(rows_in, ring * v + k - ROWS)
                        pe.wait_ge(acc_done, 2 * u + 2)
                        for qt in range(2):
                            ins = pe.matmul(o_bank[:, qt * (D + 1):(qt + 1) * (D + 1)], u_sb[:, (k - OUT) % 2, qt * P:(qt + 1) * P],
                                            wo[:, h, :], start=True, stop=True)
                        ins.then_inc(wo_done, 1)
                    if g == r_at and live(v, k, ROWS):
                        u = ring * v + k - ROWS
                        pe.wait_ge(cut_done, u + 1)
                        if shared and live(v, k, OUT):
                            pe.wait_ge(acc_done, 2 * (ring * v + k - OUT) + 4)
                        if not first(v, k, ROWS, 1):
                            pe.wait_ge(rows_in, u)
                        for qt in range(2):
                            ins = pe.matmul(r_bank[MAX_ROW:MAX_ROW + 3, qt * P:(qt + 1) * P], parts[:, (k - ROWS) % 2, qt, :],
                                            core.identb[:, :], start=True, stop=True)
                        ins.then_inc(rows_ready, 1)
            pipelined(pe, units, ring, ACC, step, peel)

        @block.scalar
        def _(act):
            def step(v, k):
                if live(v, k, OUT):
                    u = ring * v + k - OUT
                    act.wait_ge(pv_done, u + 1)
                    if not first(v, k, OUT, 2):
                        act.wait_ge(wo_done, u - 1)
                    act.activation(u_sb[:, (k - OUT) % 2, :], u_banks[(k - OUT) % nu][:, 0:S], ACT.Copy).then_inc(u_out, 1)
                for g, (kt, m) in enumerate(groups):
                    if live(v, k, EXP):
                        u = ring * v + k - EXP
                        if g == 0 and first(v, k, EXP, 1):
                            act.wait_ge(setup, 1 + nu)
                        if g == 0 and not first(v, k, EXP, 2):
                            act.wait_ge(pv_done, u - 1)
                        act.wait_ge(turned_ready, ng * u + g + 1)
                        keys = min(P, nk - kt * P)
                        bank = core.wide[(ng * (k - EXP) + g) % 2]
                        act.activation(prT[0:keys, (k - EXP) % 2, kt:kt + m, :],
                                       bank[0:keys, 0:m * S].rearrange("p (t q) -> p t q", q=S), ACT.Exp).then_inc(exp_done, 1)
                    if g == r_at and live(v, k, ROWS):
                        u, c = ring * v + k - ROWS, (k - ROWS) % ring
                        act.wait_ge(rows_ready, u + 1)
                        act.wait_ge(loaded[c // share], 16 * dmas * (v + (k - ROWS) // ring + 1))
                        act.activation(qx(c)[MAX_ROW:MAX_ROW + 3], r_bank[MAX_ROW:MAX_ROW + 3, 0:S], ACT.Copy).then_inc(rows_in, 1)
            pipelined(act, units, ring, ACC, step, peel)

        @block.gpsimd
        def _(pool):
            def step(v, k):
                u, c = ring * v + k, k % 2
                chain = lambda ins, n: (ins.then_inc(cut, 1), pool.wait_ge(cut, 3 * u + n))
                pool.wait_ge(max_ready, u + 1)
                if not first(v, k, 0, 2):
                    pool.wait_ge(rows_ready, u - 1)
                chain(pool.tensor_tensor(parts[:, c, :, 0], nmx[:, c, :], zero[:, :], ALU.add), 1)
                chain(pool.tensor_tensor(rest[:, :], nmx[:, c, :], parts[:, c, :, 0], ALU.subtract), 2)
                chain(pool.tensor_tensor(parts[:, c, :, 1], rest[:, :], zero[:, :], ALU.add), 3)
                pool.tensor_tensor(parts[:, c, :, 2], rest[:, :], parts[:, c, :, 1], ALU.subtract).then_inc(cut_done, 1)
            pool.memset(zero[:, :], 0.0).then_inc(setup, 1)
            pool.wait_ge(setup, 1 + nu)
            pipelined(pool, units, ring, 0, step)

        @block.vector
        def _(dve):
            if kts * P > nk:
                dve.memset(prT[:, :, kts - 1, :], 0.0)
            for bank in u_banks:
                dve.memset(bank[:, 0:S], 0.0).then_inc(setup, 1)
            dve.sem_inc(acc_done, 2)

            def maximum(v, k, n):
                u = ring * v + k
                t, bank = npc * u + n, (npc * k + n) % 2
                dve.wait_ge(scores_ready, t + 1)
                if n == 0 and mask and not first(v, k, 0, 2):
                    dve.wait_ge(max_ready, u - 1)
                if mask:
                    (qt, at, w), = pieces[n]
                    dve.sem_inc(passed, 1)
                    dve.tensor_tensor_reduce(junk[:, qt, at:at + w], s_bank[bank][:, 0:w], mask(qt, at, w), 1.0, LOWEST,
                                             ALU.add, ALU.max, mx[:, k % 2, qt, n % (npc // 2):n % (npc // 2) + 1]).then_inc(scores_read, 1)
                if n == npc - 1:
                    if mask:
                        dve.wait_ge(scores_read, npc * (u + 1))
                    if not first(v, k, 0, 2):
                        dve.wait_ge(cut_done, u - 1)
                    if mask:
                        dve.tensor_reduce(nmx[:, k % 2, :], mx[:, k % 2, :, :], X, ALU.max, negate=True).then_inc(max_ready, 1)
                    else:
                        dve.tensor_reduce(nmx[:, k % 2, :], s_bank[bank][:, 0:2 * nk].rearrange("p (t c) -> p t c", t=2), X,
                                          ALU.max, negate=True).then_inc(max_ready, 1)

            def add_up(v, k):
                u, slot = ring * v + k - ACC, (k - ACC) % 2
                b, _ = place(v, k, ACC)
                dve.wait_ge(wo_done, u + 1)
                dve.wait_ge(acc_done, 2 * u + 2)
                outs = o_bank[:, 0:2 * (D + 1)].rearrange("p (t c) -> p t c", t=2)
                dve.reciprocal(rtot[:, slot, :], outs[:, :, D]).then_inc(recip_done, 1)
                dve.wait_ge(recip_done, u + 1)
                for qt in range(2):
                    tile = acc[:, 2 * b + qt, :]
                    dve.scalar_tensor_tensor(tile, outs[:, qt, 0:D], rtot[:, slot, qt:qt + 1], tile,
                                             ALU.mult, ALU.add).then_inc(acc_done, 1)

            def step(v, k):
                if ACC > OUT and live(v, k, ACC):
                    add_up(v, k)
                for g in range(ng):
                    if live(v, k, 0):
                        for n in range(per * g, per * (g + 1)):
                            maximum(v, k, n)
                    if g == o_at and ACC == OUT and live(v, k, ACC):
                        add_up(v, k)
            pipelined(dve, units, ring, ACC, step, peel)


def bias_stage(core, name, acc, bv, wo_t, bo):
    nc = core.nc
    spread, mixed, added = core.sem(name + "_spread"), core.sem(name + "_mixed"), core.sem(name + "_added")
    with ExitStack() as ctx:
        bvb = core.sb(ctx, name + "_bvb", [P, P], F32)
        row = core.sb(ctx, name + "_row", [P, D], F32)
        block = ctx.enter_context(nc.Block())

        @block.tensor
        def _(pe):
            pe.wait_ge(spread, 1)
            pe.matmul(core.bank[0][:, 0:D], bvb[:, :], wo_t, start=True, stop=True).then_inc(mixed, 1)

        @block.vector
        def _(dve):
            dve.tensor_scalar(bvb[:, :], core.ones[:, :], bv, None, ALU.mult).then_inc(spread, 1)
            dve.wait_ge(mixed, 1)
            dve.tensor_tensor(row[:, :], core.bank[0][:, 0:D], bo, ALU.add).then_inc(added, 1)
            dve.wait_ge(added, 1)
            dve.tensor_tensor(acc[:, :, :], acc[:, :, :], row[:, :].unsqueeze(1).broadcast_to([P, TT, D]),
                              ALU.add).then_inc(added, 1)
            dve.wait_ge(added, 2)


def wide_project_stage(core, name, heads, dh, wq_blocks, wk_blocks, bq, scale, wv, qk_parts, v_rows):
    nc = core.nc
    blocks = heads * dh // P
    per = heads // blocks
    width = heads * dh
    halves = [(c, min(512, width - c)) for c in range(0, width, 512)]
    nh = len(halves)
    names = ("q_ready", "q_evac", "qk_ready", "qk_evac", "v_ready", "v_evac")
    q_ready, q_evac, qk_ready, qk_evac, v_ready, v_evac = (core.sem(f"{name}_{s}") for s in names)
    w_in = [core.sem(f"{name}_w_in{i}") for i in range(2)]
    ctx_in = [core.sem(f"{name}_ctx_in{i}") for i in range(2)]
    qk_stored = [core.sem(f"{name}_qk_stored{i}") for i in range(2)]
    v_stored = [core.sem(f"{name}_v_stored{i}") for i in range(2)]
    with ExitStack() as ctx:
        wqb = core.sb(ctx, name + "_wqb", [P, 2, P], F32)
        wkb = core.sb(ctx, name + "_wkb", [P, 2, per, P], F32)
        qb = core.sb(ctx, name + "_qb", [P, 2, B * S], F32)
        qk = core.sb(ctx, name + "_qk", [P, 2, per, B * S], F32)
        ctxb = core.sb(ctx, name + "_ctxb", [P, 2, SCP], F32)
        vb = core.sb(ctx, name + "_vb", [P, 2, heads, KT * dh], F32)
        block = ctx.enter_context(nc.Block())
        qbank, qkbank, vbank = core.bank[0:2], core.bank[2:4], core.bank[4:6]

        def over_blocks(eng, step):
            if blocks == 1:
                step(0, 0)
            else:
                pipelined(eng, blocks, 2, 0, step)

        @block.sync
        def _(sp):
            def load_weights(v, k):
                m = 2 * v + k
                if not isinstance(v, int) or v > 0:
                    sp.wait_ge(qk_ready, 2 * per * (m - 1))
                sp.dma_start(wqb[:, k, :], wq_blocks[m]).then_inc(w_in[k], 16)
                sp.dma_start(wkb[:, k, :, :], wk_blocks[m]).then_inc(w_in[k], 16)
            over_blocks(sp, load_weights)

            def load_ctx(v, k):
                b = 2 * v + k
                if not isinstance(v, int) or v > 0:
                    sp.wait_ge(v_ready, KT * nh * (b - 1))
                sp.dma_start(ctxb[:, k, :], core.inp["ctxT"][:, b, :]).then_inc(ctx_in[k], 16)
            pipelined(sp, B, 2, 0, load_ctx)

        @block.gpsimd
        def _(pool):
            def store_qk(v, k):
                m = 2 * v + k
                pool.wait_ge(qk_evac, 2 * per * (m + 1))
                pool.dma_start(qk_parts[m], qk[:, k, :, :]).then_inc(qk_stored[k], 16)
            over_blocks(pool, store_qk)

            def store_v(v, k):
                b = 2 * v + k
                pool.wait_ge(v_evac, KT * nh * (b + 1))
                pool.dma_start(v_rows[b], vb[:, k, :, :]).then_inc(v_stored[k], 16)
            pipelined(pool, B, 2, 0, store_v)
            for k in range(min(blocks, 2)):
                pool.wait_ge(qk_stored[k], 16 * max(blocks // 2, 1))
            for k in range(2):
                pool.wait_ge(v_stored[k], 16 * B // 2)

        @block.tensor
        def _(pe):
            def queries(v, k):
                m = 2 * v + k
                first = isinstance(v, int) and m == 0
                pe.wait_ge(w_in[k], 32 * (v + 1))
                for c in range(2):
                    if not first:
                        pe.wait_ge(q_evac, 2 * m + c - 1)
                    pe.matmul(qbank[c][:, :], wqb[:, k, :], core.xnT[:, c * 512:(c + 1) * 512],
                              start=True, stop=True).then_inc(q_ready, 1)
                for j in range(per):
                    for c in range(2):
                        n = 2 * j + c
                        if not (first and n < 2):
                            pe.wait_ge(qk_evac, 2 * per * m + n - 1)
                        if j == 0:
                            pe.wait_ge(q_evac, 2 * m + c + 1)
                        pe.matmul(qkbank[c][:, :], wkb[:, k, j, :], qb[:, k, c * 512:(c + 1) * 512],
                                  start=True, stop=True).then_inc(qk_ready, 1)
            over_blocks(pe, queries)

            def values(v, k):
                b = 2 * v + k
                first = isinstance(v, int) and b == 0
                pe.wait_ge(ctx_in[k], 16 * (v + 1))
                for kt in range(KT):
                    for c, (at, w) in enumerate(halves):
                        n = kt * nh + c
                        if not (first and n < 2):
                            pe.wait_ge(v_evac, KT * nh * b + n - 1)
                        pe.matmul(vbank[(KT * nh * k + n) % 2][:, 0:w], ctxb[:, k, kt * P:(kt + 1) * P],
                                  wv[:, at:at + w], start=True, stop=True).then_inc(v_ready, 1)
            pipelined(pe, B, 2, 0, values)

        @block.scalar
        def _(act):
            def queries(v, k):
                m = 2 * v + k
                if not isinstance(v, int) or v > 0:
                    act.wait_ge(qk_stored[k], 16 * v)
                for j in range(per):
                    for c in range(2):
                        act.wait_ge(qk_ready, 2 * per * m + 2 * j + c + 1)
                        act.activation(qk[:, k, j, c * 512:(c + 1) * 512], qkbank[c][:, :], ACT.Copy).then_inc(qk_evac, 1)
            over_blocks(act, queries)

        @block.vector
        def _(dve):
            def queries(v, k):
                m = 2 * v + k
                if not isinstance(v, int) or v > 0:
                    dve.wait_ge(qk_ready, 2 * per * (m - 1))
                for c in range(2):
                    dve.wait_ge(q_ready, 2 * m + c + 1)
                    dve.tensor_scalar(qb[:, k, c * 512:(c + 1) * 512], qbank[c][:, :], bq, scale,
                                      ALU.add, ALU.mult).then_inc(q_evac, 1)
            over_blocks(dve, queries)

            def values(v, k):
                b = 2 * v + k
                if not isinstance(v, int) or v > 0:
                    dve.wait_ge(v_stored[k], 16 * v)
                for kt in range(KT):
                    for c, (at, w) in enumerate(halves):
                        n = kt * nh + c
                        dve.wait_ge(v_ready, KT * nh * b + n + 1)
                        dve.tensor_copy(vb[:, k, at // dh:(at + w) // dh, kt * dh:(kt + 1) * dh],
                                        vbank[(KT * nh * k + n) % 2][:, 0:w].rearrange("p (h d) -> p h d", d=dh)
                                        ).then_inc(v_evac, 1)
            pipelined(dve, B, 2, 0, values)


def ffn0_stage(core, w):
    nc = core.nc
    wc, xc, hc, fc, gc = (core.sem("ffn0_" + s) for s in ("w_chain", "x_chain", "h_chain", "f_chain", "g_chain"))
    names = ("sums_ready", "x_quantized", "x_turned", "x_ready", "gu_ready", "silu_done", "h_quantized", "h_turned",
             "h_ready", "down_ready", "added")
    (sums_ready, x_quantized, x_turned, x_ready, gu_ready, silu_done, h_quantized, h_turned, h_ready, down_ready,
     added) = (core.sem("ffn0_" + s) for s in names)
    with ExitStack() as ctx:
        part = core.sb(ctx, "ffn0_part", [P, 3], F32)
        mean = core.sb(ctx, "ffn0_mean", [P, 3], F32)
        inv = core.sb(ctx, "ffn0_inv", [P, 3], F32)
        wr = core.sb(ctx, "ffn0_wr", [P, 3, FF0], F32)
        wq = core.sb(ctx, "ffn0_wq", [P, 3, FF0], BF16)
        am = core.sb(ctx, "ffn0_am", [P, TT], F32)
        sx = core.sb(ctx, "ffn0_sx", [P, TT], F32)
        fgu = core.sb(ctx, "ffn0_fgu", [P, 2, TT], F32)
        xr = core.sb(ctx, "ffn0_xr", [P, TT, D], F32)
        xq = core.sb(ctx, "ffn0_xq", [P, TT, D], BF16)
        xqT = core.sb(ctx, "ffn0_xqT", [P, B * S], BF16)
        gs = core.sb(ctx, "ffn0_gs", [P, 2, FF0], F32)
        hs = core.sb(ctx, "ffn0_hs", [P, 2, FF0], F32)
        ham = core.sb(ctx, "ffn0_ham", [P, 2], F32)
        hsc = core.sb(ctx, "ffn0_hsc", [P, 2], F32)
        hf = core.sb(ctx, "ffn0_hf", [P, 2], F32)
        hq = core.sb(ctx, "ffn0_hq", [P, 2, FF0], BF16)
        hT = core.sb(ctx, "ffn0_hT", [P, 2, FF0], BF16)
        block = ctx.enter_context(nc.Block())
        g_bank, u_bank, t_bank, d_bank = core.bank[0:2], core.bank[2:4], core.bank[4:6], core.bank[6:8]
        tb = [t_bank[i][:, :].bitcast(BF16) for i in range(2)]

        def live(v, k, lag):
            return not isinstance(v, int) or 0 <= 2 * v + k - lag < TT

        def early(v, k, lag, n):
            return isinstance(v, int) and 2 * v + k - lag < n

        @block.tensor
        def _(pe):
            pe.wait_ge(wc, 1)
            pe.matmul(g_bank[0][:, 0:3], core.ones[:, :], part[:, :], start=True, stop=True).then_inc(sums_ready, 1)
            pe.wait_ge(x_quantized, 1)
            for t in range(TT):
                ins = pe.transpose(tb[t // 4][:, t % 4 * P:(t % 4 + 1) * P], xq[:, t, :], core.identb[:, :])
            ins.then_inc(x_turned, 1)
            pe.wait_ge(x_ready, 2)

            def step(v, k):
                t = 2 * v + k
                if live(v, k, 0):
                    if not early(v, k, 0, 2):
                        pe.wait_ge(h_quantized, t - 1)
                    pe.matmul(g_bank[k][:, :], xqT[:, bass.ts(t, P)], wq[:, 0, :], start=True, stop=True)
                    pe.matmul(u_bank[k][:, :], xqT[:, bass.ts(t, P)], wq[:, 1, :], start=True, stop=True).then_inc(gu_ready, 1)
                if live(v, k, 1):
                    j = 1 - k
                    pe.wait_ge(h_quantized, t)
                    if not early(v, k, 1, 2):
                        pe.wait_ge(h_ready, t - 2)
                    for c in range(4):
                        ins = pe.transpose(tb[j][:, c * P:(c + 1) * P], hq[:, j, c * P:(c + 1) * P], core.identb[:, :])
                    ins.then_inc(h_turned, 1)
                    pe.wait_ge(h_ready, t)
                    if not early(v, k, 1, 2):
                        pe.wait_ge(added, t - 2)
                    for c in range(4):
                        ins = pe.matmul(d_bank[j][:, 0:D], hT[:, j, c * P:(c + 1) * P], wq[:, 2, c * P:(c + 1) * P],
                                        start=(c == 0), stop=(c == 3))
                    ins.then_inc(down_ready, 1)
            pipelined(pe, TT, 2, 1, step, peel=2)

        @block.scalar
        def _(act):
            act.wait_ge(x_turned, 1)
            act.activation(xqT[:, 0:512], tb[0][:, 0:512], ACT.Copy).then_inc(x_ready, 1)
            act.wait_ge(fc, 3)

            def step(v, k):
                t = 2 * v + k
                if live(v, k, 0):
                    act.wait_ge(gu_ready, t + 1)
                    if not early(v, k, 0, 2):
                        act.wait_ge(h_quantized, t - 1)
                    act.activation(gs[:, k, :], g_bank[k][:, :], ACT.Silu, scale=fgu[:, 0, bass.ts(t, 1)]).then_inc(silu_done, 1)
                if live(v, k, 1):
                    j = 1 - k
                    act.wait_ge(h_turned, t)
                    if not early(v, k, 1, 2):
                        act.wait_ge(down_ready, t - 2)
                    act.activation(hT[:, j, :], tb[j][:, 0:FF0], ACT.Copy).then_inc(h_ready, 1)
            pipelined(act, TT, 2, 1, step, peel=2)

        @block.vector
        def _(dve):
            wl, xl, fl = Link(dve, wc), Link(dve, xc), Link(dve, fc)
            wl(dve.tensor_reduce(part[:, :], w[:, :, :], X, ALU.add, apply_absolute_value=True))
            xl(dve.tensor_reduce(am[:, :], core.xn[:, :, :], X, ALU.max, apply_absolute_value=True))
            xl(dve.tensor_scalar(am[:, :], am[:, :], 1e-5, None, ALU.max))
            xl(dve.reciprocal(sx[:, :], am[:, :]))
            xl(dve.tensor_scalar(sx[:, :], sx[:, :], 127.0, None, ALU.mult))
            for t in range(TT):
                ins = dve.tensor_scalar(xr[:, t, :], core.xn[:, t, :], sx[:, t:t + 1], ROUND, ALU.mult, ALU.add)
            xl(ins)
            xl(dve.tensor_scalar(xr[:, :, :], xr[:, :, :], ROUND, 127.0, ALU.subtract, ALU.min))
            dve.tensor_scalar(xq[:, :, :], xr[:, :, :], -128.0, None, ALU.max).then_inc(x_quantized, 1)
            dve.wait_ge(sums_ready, 1)
            wl(dve.tensor_scalar(mean[:, :], g_bank[0][:, 0:3], 1.0 / (FF0 * D), 1e-5, ALU.mult, ALU.max))
            wl(dve.reciprocal(inv[:, :], mean[:, :]))
            for i in range(3):
                ins = dve.tensor_scalar(wr[:, i, :], w[:, i, :], inv[:, i:i + 1], ROUND, ALU.mult, ALU.add)
            wl(ins)
            wl(dve.tensor_scalar(wr[:, :, :], wr[:, :, :], ROUND, 1.0, ALU.subtract, ALU.min))
            wl(dve.tensor_scalar(wq[:, :, :], wr[:, :, :], -1.0, None, ALU.max))
            fl(dve.tensor_scalar(am[:, :], am[:, :], 1.0 / 127.0, None, ALU.mult))
            dve.tensor_scalar(fgu[:, 0, :], am[:, :], mean[:, 0:1], None, ALU.mult)
            fl(dve.tensor_scalar(fgu[:, 1, :], am[:, :], mean[:, 1:2], None, ALU.mult))
            fl(dve.tensor_scalar(mean[:, 2:3], mean[:, 2:3], 1.0 / 127.0, None, ALU.mult))
            dve.wait_ge(x_turned, 1)
            dve.tensor_copy(xqT[:, 512:1024], tb[1][:, 0:512]).then_inc(x_ready, 1)
            hl = Link(dve, hc, 6)

            def step(v, k):
                t = 2 * v + k
                if live(v, k, 0):
                    hl.at(t)
                    dve.wait_ge(silu_done, t + 1)
                    hl(dve.scalar_tensor_tensor(hs[:, k, :], u_bank[k][:, :], fgu[:, 1, bass.ts(t, 1)], gs[:, k, :],
                                                ALU.mult, ALU.mult))
                    hl(dve.tensor_reduce(ham[:, k:k + 1], hs[:, k, :], X, ALU.max, apply_absolute_value=True))
                    hl(dve.tensor_scalar(ham[:, k:k + 1], ham[:, k:k + 1], 1e-5, None, ALU.max))
                    hl(dve.reciprocal(hsc[:, k:k + 1], ham[:, k:k + 1]))
                    if not early(v, k, 0, 2):
                        dve.wait_ge(added, t - 1)
                    dve.tensor_scalar(hf[:, k:k + 1], ham[:, k:k + 1], mean[:, 2:3], None, ALU.mult)
                    hl(dve.tensor_scalar(hsc[:, k:k + 1], hsc[:, k:k + 1], 127.0, None, ALU.mult))
                    hl(dve.tensor_scalar(hs[:, k, :], hs[:, k, :], hsc[:, k:k + 1], ROUND, ALU.mult, ALU.add))
                    if not early(v, k, 0, 2):
                        dve.wait_ge(h_turned, t - 1)
                    dve.tensor_scalar(hq[:, k, :], hs[:, k, :], ROUND, 127.0, ALU.subtract, ALU.min).then_inc(h_quantized, 1)
                if live(v, k, 1):
                    j = 1 - k
                    dve.wait_ge(down_ready, t)
                    tile = core.x[:, t - 1, :]
                    dve.scalar_tensor_tensor(tile, d_bank[j][:, 0:D], hf[:, j:j + 1], tile, ALU.mult, ALU.add).then_inc(added, 1)
            pipelined(dve, TT, 2, 1, step, peel=2)


def moe_stage(core, y, zT, w1, w2, gw, gb, rank):
    nc = core.nc
    gc = core.sem("moe_chain")
    names = ("logits_ready", "up_ready", "gelu_done", "down_ready", "added")
    logits_ready, up_ready, gelu_done, down_ready, added = (core.sem("moe_" + s) for s in names)
    w_in = [core.sem(f"moe_w_in{i}") for i in range(2)]
    steps = 2 * EXPERTS
    with ExitStack() as ctx:
        w1b = core.sb(ctx, "moe_w1b", [P, 2, HID], F32)
        w2b = core.sb(ctx, "moe_w2b", [P, 2, 4, D], F32)
        hid = core.sb(ctx, "moe_hid", [P, 2, 4, 512], F32)
        lg = core.sb(ctx, "moe_lg", [P, TT, EXPERTS], F32)
        best = core.sb(ctx, "moe_best", [P, TT], F32)
        pick = core.sb(ctx, "moe_pick", [P, TT, EXPERTS], F32)
        block = ctx.enter_context(nc.Block())
        up_bank, down_bank, g_bank = core.bank[0:4], core.bank[4:6], core.bank[6]

        def live(v, k, lag):
            return not isinstance(v, int) or 0 <= 4 * v + k - lag < steps

        def early(v, k, lag, n):
            return isinstance(v, int) and 4 * v + k - lag < n

        @block.sync
        def _(sp):
            def step(v, k):
                e = 2 * v + k
                if not isinstance(v, int) or v > 0:
                    sp.wait_ge(down_ready, 2 * (e - 1))
                sp.dma_start(w1b[:, k, :], w1[e]).then_inc(w_in[k], 16)
                sp.dma_start(w2b[:, k, :, :], w2[e]).then_inc(w_in[k], 16)
            pipelined(sp, EXPERTS, 2, 0, step)

        @block.tensor
        def _(pe):
            for t in range(TT):
                ins = pe.matmul(g_bank[:, t * EXPERTS:(t + 1) * EXPERTS], zT[:, t * P:(t + 1) * P], gw,
                                start=True, stop=True)
            ins.then_inc(logits_ready, 1)

            def step(v, k):
                i = 4 * v + k
                if live(v, k, 0):
                    if k % 2 == 0:
                        pe.wait_ge(w_in[k // 2], 32 * (v + 1))
                    for c in range(4):
                        if not early(v, k, 0, 1):
                            pe.wait_ge(gelu_done, 4 * (i - 1) + c + 1)
                        pe.matmul(up_bank[c][:, :], w1b[:, k // 2, c * P:(c + 1) * P],
                                  zT[:, (k % 2) * 512:(k % 2 + 1) * 512], start=True, stop=True).then_inc(up_ready, 1)
                if live(v, k, 1):
                    j = (k - 1) % 4
                    pe.wait_ge(gelu_done, 4 * i)
                    if not early(v, k, 1, 2):
                        pe.wait_ge(added, 4 * (i - 2))
                    for q in range(4):
                        for c in range(4):
                            ins = pe.matmul(down_bank[j % 2][:, q * D:(q + 1) * D], hid[:, j % 2, c, q * P:(q + 1) * P],
                                            w2b[:, j // 2, c, :], start=(c == 0), stop=(c == 3))
                    ins.then_inc(down_ready, 1)
            pipelined(pe, steps, 4, 1, step)

        @block.scalar
        def _(act):
            def step(v, k):
                i = 4 * v + k
                for c in range(4):
                    act.wait_ge(up_ready, 4 * i + c + 1)
                    if c == 0 and not early(v, k, 0, 2):
                        act.wait_ge(down_ready, i - 1)
                    act.activation(hid[:, k % 2, c, :], up_bank[c][:, :], ACT.Gelu_apprx_tanh).then_inc(gelu_done, 1)
            pipelined(act, steps, 4, 0, step)

        @block.vector
        def _(dve):
            link = Link(dve, gc)
            wide = lambda a: a.unsqueeze(1).broadcast_to([P, TT, EXPERTS])
            each = lambda a: a.unsqueeze(2).broadcast_to([P, TT, EXPERTS])
            dve.wait_ge(logits_ready, 1)
            link(dve.tensor_tensor(lg[:, :, :], g_bank[:, 0:TT * EXPERTS].rearrange("p (t e) -> p t e", e=EXPERTS),
                                   wide(gb), ALU.add))
            link(dve.tensor_reduce(best[:, :], lg[:, :, :], X, ALU.max))
            link(dve.tensor_tensor(pick[:, :, :], lg[:, :, :], each(best[:, :]), ALU.is_equal))
            link(dve.tensor_tensor(pick[:, :, :], pick[:, :, :], wide(rank), ALU.mult))
            link(dve.tensor_reduce(best[:, :], pick[:, :, :], X, ALU.max))
            link(dve.tensor_tensor(lg[:, :, :], pick[:, :, :], each(best[:, :]), ALU.is_equal))

            def step(v, k):
                if live(v, k, 1):
                    i = 4 * v + k
                    j = (k - 1) % 4
                    e = 2 * v + (k - 1) // 2
                    dve.wait_ge(down_ready, i)
                    for q in range(4):
                        t = 4 * (j % 2) + q
                        tile = y[:, t, :]
                        if not early(v, k, 1, 2):
                            dve.wait_ge(added, 4 * (i - 3) + q + 1)
                        dve.scalar_tensor_tensor(tile, down_bank[j % 2][:, q * D:(q + 1) * D], lg[:, t, bass.ts(e, 1)],
                                                 tile, ALU.mult, ALU.add).then_inc(added, 1)
            pipelined(dve, steps, 4, 1, step)
            dve.wait_ge(added, 4 * steps)
            link(dve.tensor_tensor(core.x[:, :, :], core.x[:, :, :], y[:, :, :], ALU.add))


def ffn2_stage(core, w_gu, w_down, clips):
    nc = core.nc
    names = ("chain", "w_quantized", "w_turned", "w_ready", "col_ready", "col_turned", "top_ready", "top_spread",
             "exp_done", "gu_ready", "silu_done", "gu_read", "down_ready", "scaled", "out_turned", "w_copied", "xq_ready")
    (chain, w_quantized, w_turned, w_ready, col_ready, col_turned, top_ready, top_spread, exp_done, gu_ready,
     silu_done, gu_read, down_ready, scaled, out_turned, w_copied, xq_ready) = (core.sem("ffn2_" + s) for s in names)
    top_done = core.sem("ffn2_top_done")
    N = B * S
    NC = len(FF2_CHUNKS)
    with ExitStack() as ctx:
        sb = lambda n, shape, dt: core.sb(ctx, "ffn2_" + n, shape, dt)
        am = sb("am", [P, 2 * NC + 1], F32)
        inv = sb("inv", [P, 2 * NC + 1], F32)
        wr = sb("wr", [P, 2 * NC, D], F32)
        wqn = sb("wqn", [P, 2 * NC, D], BF16)
        wdn = sb("wdn", [P, NC * P], F32)
        wdq = sb("wdq", [P, NC * P], BF16)
        wgu = sb("wgu", [P, 2 * NC, P], BF16)
        wd = sb("wd", [P, NC, P], BF16)
        xr = sb("xr", [P, N], F32)
        xq = sb("xq", [P, N], BF16)
        sig = sb("sig", [P, 2], F32)
        col = sb("col", [P, 1], F32)
        top = sb("top", [1, 1], F32)
        sx = sb("sx", [P, 2], F32)
        rx = sb("rx", [P, 2], F32)
        fs = sb("fs", [P, 2 * NC + 1], F32)
        gs = sb("gs", [P, 2, 512], F32)
        h = sb("h", [P, NC, N], F32)
        hq = sb("hq", [P, NC, N], BF16)
        oT = sb("oT", [P, N], F32)
        block = ctx.enter_context(nc.Block())
        bank = core.bank
        tb = bank[0][:, :].bitcast(BF16)
        tb2 = bank[1][:, :].bitcast(BF16)
        work = [(c, i) for i in range(NC) for c in range(2)]

        def pad(i):
            return FF2_CHUNKS[i][1]

        @block.tensor
        def _(pe):
            pe.wait_ge(w_quantized, 2)
            for i in range(2 * NC):
                pe.transpose(tb[:, i * P:(i + 1) * P], wqn[:, i, :], core.identb[:, :])
            for i in range(NC):
                ins = pe.transpose(tb2[:, i * P:(i + 1) * P], wdq[:, i * P:(i + 1) * P], core.identb[:, :])
            ins.then_inc(w_turned, 1)
            for r in range(2):
                pe.wait_ge(col_ready, r + 1)
                pe.transpose(bank[7][0:1, 0:P], col[:, :], core.ident[:, :]).then_inc(col_turned, 1)
                pe.wait_ge(top_ready, r + 1)
                pe.matmul(bank[7][:, 128:129], core.ones[0:1, :], top[:, :], start=True, stop=True).then_inc(top_spread, 1)
                if r == 0:
                    pe.wait_ge(xq_ready, 1)
                    pe.wait_ge(w_ready, 1)
                    for n, (c, i) in enumerate(work):
                        if n >= 2:
                            pe.wait_ge(gu_read, n - 1)
                        rhs = xq[:, c * 512:(c + 1) * 512]
                        pe.matmul(bank[2 + n % 2][0:pad(i), :], wgu[:, i, 0:pad(i)], rhs, start=True, stop=True)
                        pe.matmul(bank[4 + n % 2][0:pad(i), :], wgu[:, NC + i, 0:pad(i)], rhs,
                                  start=True, stop=True).then_inc(gu_ready, 1)
            pe.wait_ge(xq_ready, 2)
            pe.wait_ge(gu_read, 2 * NC)
            for c in range(2):
                for i in range(NC):
                    ins = pe.matmul(bank[2 + c][:, :], wd[:, i, :], hq[:, i, c * 512:(c + 1) * 512],
                                    start=(i == 0), stop=(i == NC - 1))
                ins.then_inc(down_ready, 1)
            for c in range(2):
                pe.wait_ge(scaled, c + 1)
                for t in range(4):
                    ins = pe.transpose(bank[4 + c][:, t * P:(t + 1) * P], oT[:, (4 * c + t) * P:(4 * c + t + 1) * P],
                                       core.ident[:, :])
                ins.then_inc(out_turned, 1)

        @block.scalar
        def _(act):
            act.activation(sig[:, :], clips, ACT.Exp, scale=-1.0).then_inc(exp_done, 1)
            act.wait_ge(w_turned, 1)
            act.activation(wgu[:, :, :], tb[:, 0:2 * NC * P].rearrange("p (i q) -> p i q", q=P), ACT.Copy).then_inc(w_copied, 1)
            act.activation(wd[:, :, :], tb2[:, 0:NC * P].rearrange("p (i q) -> p i q", q=P), ACT.Copy).then_inc(w_copied, 1)
            act.wait_ge(w_copied, 2)
            act.activation(gs[0:1, 0, 0:1], core.ones[0:1, 0:1], ACT.Silu).then_inc(w_ready, 1)
            act.wait_ge(w_ready, 1)
            for n, (c, i) in enumerate(work):
                act.wait_ge(gu_ready, n + 1)
                if n == 0:
                    act.wait_ge(top_done, 1)
                if n >= 2:
                    act.wait_ge(gu_read, n - 1)
                act.activation(gs[0:pad(i), n % 2, :], bank[2 + n % 2][0:pad(i), :], ACT.Silu,
                               scale=fs[0:pad(i), i:i + 1]).then_inc(silu_done, 1)

        @block.vector
        def _(dve):
            link = Link(dve, chain)
            link(dve.tensor_reduce(am[:, 0:2 * NC], w_gu, X, ALU.max, apply_absolute_value=True))
            link(dve.tensor_reduce(am[:, 2 * NC:], w_down, X, ALU.max, apply_absolute_value=True))
            link(dve.tensor_scalar(am[:, :], am[:, :], 1.0 / 127.0, None, ALU.mult))
            link(dve.reciprocal(inv[:, :], am[:, :]))
            for i in range(2 * NC):
                dve.tensor_scalar(wr[:, i, :], w_gu[:, i, :], inv[:, i:i + 1], ROUND, ALU.mult, ALU.add)
            link(dve.tensor_scalar(wdn[:, 0:FF2], w_down, inv[:, 2 * NC:], ROUND, ALU.mult, ALU.add))
            dve.tensor_scalar(wqn[:, :, :], wr[:, :, :], ROUND, 127.0, ALU.subtract, ALU.min).then_inc(w_quantized, 1)
            dve.memset(wdq[:, FF2:], 0.0)
            dve.memset(h[96:P, NC - 1, :], 0.0)
            dve.tensor_scalar(wdq[:, 0:FF2], wdn[:, 0:FF2], ROUND, 127.0, ALU.subtract, ALU.min).then_inc(w_quantized, 1)
            dve.wait_ge(exp_done, 1)
            link(dve.tensor_scalar(sig[:, :], sig[:, :], 1.0, None, ALU.add))
            link(dve.reciprocal(sig[:, :], sig[:, :]))

            def scale_of(r, data):
                dve.tensor_reduce(col[:, :], data, X if r == 0 else mybir.AxisListType.XY, ALU.max,
                                  apply_absolute_value=True).then_inc(col_ready, 1)
                dve.wait_ge(col_turned, r + 1)
                dve.tensor_reduce(top[:, :], bank[7][0:1, 0:P], X, ALU.max).then_inc(top_ready, 1)
                dve.wait_ge(top_spread, r + 1)
                link(dve.tensor_scalar(sx[:, r:r + 1], bank[7][:, 128:129], sig[:, r:r + 1], 1.0 / 127.0, ALU.mult, ALU.mult))
                link(dve.reciprocal(rx[:, r:r + 1], sx[:, r:r + 1]))

            scale_of(0, core.xnT[:, :])
            dve.tensor_scalar(fs[:, :], am[:, :], sx[:, 0:1], None, ALU.mult).then_inc(top_done, 1)
            link(dve.tensor_scalar(xr[:, :], core.xnT[:, :], rx[:, 0:1], ROUND, ALU.mult, ALU.add))
            link(dve.tensor_scalar(xr[:, :], xr[:, :], ROUND, 127.0, ALU.subtract, ALU.min))
            dve.tensor_scalar(xq[:, :], xr[:, :], -128.0, None, ALU.max).then_inc(xq_ready, 1)
            dve.wait_ge(top_done, 1)
            for n, (c, i) in enumerate(work):
                dve.wait_ge(silu_done, n + 1)
                dve.scalar_tensor_tensor(h[0:pad(i), i, c * 512:(c + 1) * 512], bank[4 + n % 2][0:pad(i), :],
                                         fs[0:pad(i), NC + i:NC + i + 1], gs[0:pad(i), n % 2, :],
                                         ALU.mult, ALU.mult).then_inc(gu_read, 1)
            dve.wait_ge(gu_read, 2 * NC)
            scale_of(1, h[:, :, :])
            link(dve.tensor_scalar(h[:, :, :], h[:, :, :], rx[:, 1:2], ROUND, ALU.mult, ALU.add))
            link(dve.tensor_scalar(h[:, :, :], h[:, :, :], ROUND, 127.0, ALU.subtract, ALU.min))
            dve.tensor_scalar(hq[:, :, :], h[:, :, :], -128.0, None, ALU.max).then_inc(xq_ready, 1)
            link(dve.tensor_scalar(fs[:, 2 * NC:], am[:, 2 * NC:], sx[:, 1:2], None, ALU.mult))
            for c in range(2):
                dve.wait_ge(down_ready, c + 1)
                dve.tensor_scalar(oT[:, c * 512:(c + 1) * 512], bank[2 + c][:, :], fs[:, 2 * NC:], None,
                                  ALU.mult).then_inc(scaled, 1)
            for c in range(2):
                dve.wait_ge(out_turned, c + 1)
                link(dve.tensor_tensor(core.x[:, 4 * c:4 * c + 4, :], core.x[:, 4 * c:4 * c + 4, :],
                                       bank[4 + c][:, :].rearrange("p (t d) -> p t d", d=D), ALU.add))


def ffn3_stage(core, u1, v1, b1, u2, v2, b2):
    nc = core.nc
    names = ("p_ready", "p_out", "h_ready", "gelu_done", "q_ready", "q_out", "o_ready", "biased", "added", "stored")
    p_ready, p_out, h_ready, gelu_done, q_ready, q_out, o_ready, biased, added, stored = (core.sem("ffn3_" + s) for s in names)
    NC = FF3 // P
    with ExitStack() as ctx:
        pT = core.sb(ctx, "ffn3_pT", [RANK, B * S], F32)
        hT = core.sb(ctx, "ffn3_hT", [P, 2, NC, 512], F32)
        qT = core.sb(ctx, "ffn3_qT", [RANK, B * S], F32)
        block = ctx.enter_context(nc.Block())
        bank = core.bank
        half = lambda c: slice(c * 512, (c + 1) * 512)

        @block.tensor
        def _(pe):
            for c in range(2):
                pe.matmul(bank[c][0:RANK, :], u1, core.xnT[:, half(c)], start=True, stop=True).then_inc(p_ready, 1)
            for c in range(2):
                pe.wait_ge(p_out, c + 1)
                for i in range(NC):
                    if c:
                        pe.wait_ge(gelu_done, i + 1)
                    pe.matmul(bank[2 + i][:, :], v1[:, i * P:(i + 1) * P], pT[:, half(c)],
                              start=True, stop=True).then_inc(h_ready, 1)
            for c in range(2):
                pe.wait_ge(gelu_done, NC * (c + 1))
                for i in range(NC):
                    ins = pe.matmul(bank[c][0:RANK, :], u2[:, i, :], hT[:, c, i, :], start=(i == 0), stop=(i == NC - 1))
                ins.then_inc(q_ready, 1)
            for c in range(2):
                pe.wait_ge(q_out, c + 1)
                for t in range(4):
                    ins = pe.matmul(bank[6 + c][:, t * D:(t + 1) * D], qT[:, (4 * c + t) * P:(4 * c + t + 1) * P], v2,
                                    start=True, stop=True)
                ins.then_inc(o_ready, 1)

        @block.scalar
        def _(act):
            for c in range(2):
                for i in range(NC):
                    act.wait_ge(h_ready, NC * c + i + 1)
                    act.activation(hT[:, c, i, :], bank[2 + i][:, :], ACT.Gelu_apprx_tanh, bias=b1[:, i:i + 1]).then_inc(gelu_done, 1)

        @block.vector
        def _(dve):
            for c in range(2):
                dve.wait_ge(p_ready, c + 1)
                dve.tensor_copy(pT[:, half(c)], bank[c][0:RANK, :]).then_inc(p_out, 1)
            dve.tensor_tensor(core.x[:, :, :], core.x[:, :, :], b2.unsqueeze(1).broadcast_to([P, TT, D]), ALU.add).then_inc(biased, 1)
            for c in range(2):
                dve.wait_ge(q_ready, c + 1)
                dve.tensor_copy(qT[:, half(c)], bank[c][0:RANK, :]).then_inc(q_out, 1)
            dve.wait_ge(biased, 1)
            for c in range(2):
                dve.wait_ge(o_ready, c + 1)
                dve.tensor_tensor(core.x[:, 4 * c:4 * c + 4, :], core.x[:, 4 * c:4 * c + 4, :],
                                  bank[6 + c][:, :].rearrange("p (t d) -> p t d", d=D), ALU.add).then_inc(added, 1)

        @block.sync
        def _(sp):
            out = core.inp["out"].rearrange("(t p) d -> p t d", p=P)
            for c in range(2):
                sp.wait_ge(added, c + 1)
                sp.dma_start(out[:, 4 * c:4 * c + 4, :], core.x[:, 4 * c:4 * c + 4, :]).then_inc(stored, 16)
            sp.wait_ge(stored, 32)


def small_head_layer(core, name, acc, mask_tile, turned, from_ctx, qkv_w, worep, qk_bias, v_bias, wo_t, bo, late_loads=()):
    nc = core.nc
    nb, cols = (B, SCP) if from_ctx else (1, B * S)
    nk = SC if from_ctx else S
    kts = (nk + P - 1) // P
    k_parts = nc.dram_tensor(name + "_k_parts", (nb, HEADS, 3, 8, cols), BF16, kind="Internal").ap()
    q_stack = nc.dram_tensor(name + "_q_stack", (HEADS, 3, 3, 8, B * S), BF16, kind="Internal").ap()
    v_rows = nc.dram_tensor(name + "_v_rows", (nb, P, HEADS, cols // P * VCOLS), F32, kind="Internal").ap()
    STACK = 72
    share = 1 if from_ctx else B
    ring = 4 if from_ctx else 16
    slots = ring // share
    with ExitStack() as ctx:
        half = (share * nk + 1) // 2
        words = [core.sb(ctx, name + n, [P, slots * w], F32) for n, w in (("_ks", half), ("_qs", share * S // 2),
                                                                          ("_qx", share * S // 2))]
        ks, qs, qx = (w[:, :].bitcast(BF16).rearrange("p (s c) -> p s c", s=slots) for w in words)
        vs = core.sb(ctx, name + "_vs", [P, slots, share * kts, VCOLS], F32)

        def clear(pool, sem):
            blocks = [(words[0][64:MAX_ROW, :], 0.0), (words[0][MAX_ROW:P, :], TWO_ONES), (words[1][64:P, :], 0.0),
                      (words[2][64:P, :], 0.0)]
            for n, (block, value) in enumerate(blocks):
                pool.memset(block, value).then_inc(sem, 1)
                pool.wait_ge(sem, n + 1)

        split_project_stage(core, name + "_proj", qkv_w, qk_bias, 8.0 ** -0.5, from_ctx, k_parts, q_stack, v_rows,
                            clear, late_loads)
        if v_bias is not None:
            bias_stage(core, name + "_bias", acc, v_bias, wo_t, bo)

        def load(sp, b, h, k, sem):
            keys = k_parts[b, h, :, :, 0:nk] if from_ctx else k_parts[0, h, :, :, :]
            queries = q_stack[h, :, :, :, bass.ds(b * S, S)] if from_ctx else q_stack[h, :, :, :, :]
            sp.dma_start(ks[0:STACK, k, 0:share * nk], keys.rearrange("i d c -> (i d) c").unsqueeze(0).broadcast_to([3, 24, share * nk])).then_inc(sem, 16)
            for tile in (qs,) if turned is None else (qs, qx):
                sp.dma_start(tile[0:STACK, k, :], queries.rearrange("j i d c -> (j i d) c")).then_inc(sem, 16)

        def load_values(sp, b, h, k, sem):
            values = v_rows[b, :, h, :] if from_ctx else v_rows[0, :, h, :]
            sp.dma_start(vs[:, k, :, :], values.rearrange("p (t d) -> p t d", d=VCOLS)).then_inc(sem, 16)

        if turned is None:
            attention_stage(core, name + "_attn", acc, worep[:, :, 0:D], HEADS, 8, nk, load, 2, load_values,
                            lambda k, b, at, w: ks[:, k, at:at + w],
                            lambda k, qt: qs[:, k, qt * P:(qt + 1) * P],
                            lambda k, kt: vs[:, k, kt, 0:8], mask_tile)
        else:
            def cut(tile, k, n, start, size):
                return tile[:, k // share, k % share * n + start:k % share * n + start + size]
            turned_attention_stage(core, name + "_attn", acc, worep, nk, ring, share,
                                   (1, 2, 3, 4, 4) if from_ctx else (2, 4, 5, 6, 7), load, 3, load_values,
                                   lambda k, start, size: cut(ks, k, nk, start, size),
                                   lambda k, qt: cut(qs, k, S, qt * P, P), lambda k: cut(qx, k, S, 0, S),
                                   lambda k, kt: vs[:, k // share, k % share * kts + kt, :], mask_tile, turned[0])


def wide_head_layer(core, name, acc, heads, dh, wq_blocks, wk_blocks, bq, wv, worep, zeros):
    nc = core.nc
    blocks = heads * dh // P
    per = heads // blocks
    qk = nc.dram_tensor(name + "_qk", (blocks, P, per, B * S), F32, kind="Internal").ap()
    v_rows = nc.dram_tensor(name + "_v_rows", (B, P, heads, KT * dh), F32, kind="Internal").ap()
    wide_project_stage(core, name + "_proj", heads, dh, wq_blocks, wk_blocks, bq, float(dh) ** -0.5, wv, qk, v_rows)
    with ExitStack() as ctx:
        qs = core.sb(ctx, name + "_qs", [P, 4, S], F32)
        vs = core.sb(ctx, name + "_vs", [P, 4, KT, dh], F32)

        def load(sp, b, h, k, sem):
            m, j = (h // per, h % per) if per > 1 else (h, 0)
            sp.dma_start(qs[:, k, :], qk[m, :, j, bass.ds(b * S, S)]).then_inc(sem, 16)

        def load_values(sp, b, h, k, sem):
            sp.dma_start(vs[:, k, :, :], v_rows[b, :, h, :].rearrange("p (t d) -> p t d", d=dh)).then_inc(sem, 16)

        attention_stage(core, name + "_attn", acc, worep, heads, dh, SC, load, 1, load_values,
                        lambda k, b, at, w: core.ctxT[:, b, at:at + w],
                        lambda k, qt: qs[:, k, qt * P:(qt + 1) * P],
                        lambda k, kt: vs[:, k, kt, :], zeros)


def zero_mask_stage(core, name, tile):
    done = core.sem(name)
    with core.nc.Block() as block:
        @block.vector
        def _(dve):
            dve.memset(tile, 0.0).then_inc(done, 1)
            dve.wait_ge(done, 1)


def build(nc, inp):
    with ExitStack() as top:
        core = Core(nc, top, inp)
        start_stage(core)

        with ExitStack() as ctx:
            sb = lambda n, shape, dt=F32: core.sb(ctx, n, shape, dt)
            w, worep, wot = sb("a0_w", [P, 3, D]), sb("a0_worep", [P, HEADS, D + 1]), sb("a0_wot", [P, D])
            cols, bo = sb("a0_cols", [P, 3]), sb("a0_bo", [P, D])
            mask = sb("a0_mask", [P, 2, SC])
            layernorm_stage(core, "ln0a", core.x, core.xn, core.xnT, loads=[
                (w[:, :, :], inp["a0_w"]), (worep[:, :, :], inp["a0_worep"]), (wot[:, :], inp["a0_wot"]),
                (cols[:, :], inp["a0_cols"]), (bo[:, :], inp["a0_bo"].partition_broadcast(P)),
                (mask[:, :, :], inp["mask0"].rearrange("(t p) k -> p t k", p=P))])
            scaled = core.sem("a0_mask_scaled")
            with nc.Block() as block:
                @block.vector
                def _(dve):
                    dve.tensor_scalar(mask[:, :, :], mask[:, :, :], -1e9, None, ALU.mult).then_inc(scaled, 1)
                    dve.wait_ge(scaled, 1)
            small_head_layer(core, "a0", core.x, lambda qt, at, n: mask[:, qt, at:at + n], None, True,
                             w, worep, cols, cols[:, 2:3], wot[:, :], bo[:, :],
                             late_loads=[(core.ctxT[:, b, :], inp["ctxT"][:, b, :]) for b in range(B)])
        core.end_layer()
        with ExitStack() as ctx:
            w = core.sb(ctx, "f0_w", [P, 3, FF0], F32)
            layernorm_stage(core, "ln0f", core.x, core.xn, loads=[(w[:, :, :], inp["f0_w"])])
            ffn0_stage(core, w)
        core.end_layer()
        with ExitStack() as ctx:
            sb = lambda n, shape, dt=F32: core.sb(ctx, n, shape, dt)
            wv, wot, cols, bo = sb("a1_wv", [P, D]), sb("a1_wot", [P, 1, D]), sb("a1_cols", [P, 2]), sb("a1_bo", [P, D])
            zeros = sb("a1_zeros", [P, 512])
            layernorm_stage(core, "ln1a", core.x, core.xn, core.xnT, loads=[
                (wv[:, :], inp["a1_wv"]), (wot[:, 0, :], inp["a1_wot"]), (cols[:, :], inp["a1_cols"]),
                (bo[:, :], inp["a1_bo"].partition_broadcast(P))])
            zero_mask_stage(core, "a1_zeroed", zeros[:, :])
            bias_stage(core, "a1_bias", core.x, cols[:, 1:2], wot[:, 0, :], bo[:, :])
            wide_head_layer(core, "a1", core.x, 1, D, [inp["a1_wq"]], [inp["a1_wk"].unsqueeze(1)],
                            cols[:, 0:1], wv, wot, lambda qt, at, n: zeros[:, 0:n])
        core.end_layer()
        with ExitStack() as ctx:
            sb = lambda n, shape, dt=F32: core.sb(ctx, n, shape, dt)
            y = sb("f1_y", [P, TT, D])
            layernorm_stage(core, "ln1f", core.x, y)
            with ExitStack() as inner:
                sbi = lambda n, shape, dt=F32: core.sb(inner, n, shape, dt)
                w, worep, zeros = sbi("m1_w", [P, 3, D]), sbi("m1_worep", [P, HEADS, D + 1]), sbi("m1_zeros", [P, 512])
                layernorm_stage(core, "ln1s", y, core.xn, core.xnT, affine=(inp["ln1_w"], inp["ln1_b"]), loads=[
                    (w[:, :, :], inp["m1_w"]), (worep[:, :, :], inp["m1_worep"])])
                zero_mask_stage(core, "m1_zeroed", zeros[:, :])
                small_head_layer(core, "m1", y, None, (None,), False,
                                 w, worep, zeros, None, None, None)
            gw, gb, rank = sb("e1_gw", [P, EXPERTS]), sb("e1_gb", [P, EXPERTS]), sb("e1_rank", [P, EXPERTS])
            layernorm_stage(core, "ln1e", y, core.xn, core.xnT, affine=(inp["ln2_w"], inp["ln2_b"]), loads=[
                (gw[:, :], inp["e1_gw"]), (gb[:, :], inp["e1_gb"].partition_broadcast(P)),
                (rank[:, :], inp["rank"].partition_broadcast(P))])
            moe_stage(core, y, core.xnT, inp["e1_w1"], inp["e1_w2"], gw[:, :], gb[:, :], rank[:, :])
        core.end_layer()
        with ExitStack() as ctx:
            sb = lambda n, shape, dt=F32: core.sb(ctx, n, shape, dt)
            wv, worep, zeros = sb("a2_wv", [P, 1024]), sb("a2_worep", [P, HEADS, D]), sb("a2_zeros", [P, 512])
            layernorm_stage(core, "ln2a", core.x, core.xn, core.xnT, loads=[
                (wv[:, :], inp["a2_wv"]), (worep[:, :, :], inp["a2_worep"])])
            zero_mask_stage(core, "a2_zeroed", zeros[:, :])
            wide_head_layer(core, "a2", core.x, HEADS, 64, inp["a2_wq"], inp["a2_wk"], zeros[:, 0:1], wv, worep,
                            lambda qt, at, n: zeros[:, 0:n])
        core.end_layer()
        with ExitStack() as ctx:
            sb = lambda n, shape, dt=F32: core.sb(ctx, n, shape, dt)
            wgu, wdn, clips = sb("f2_wgu", [P, 6, D]), sb("f2_wdn", [P, FF2]), sb("f2_clips", [P, 2])
            layernorm_stage(core, "ln2f", core.x, core.xn, core.xnT, loads=[
                (wgu[:, :, :], inp["f2_wgu"]), (wdn[:, :], inp["f2_wdn"]),
                (clips[:, 0:1], inp["f2_clip_x"].partition_broadcast(P)),
                (clips[:, 1:2], inp["f2_clip_down"].partition_broadcast(P))])
            ffn2_stage(core, wgu[:, :, :], wdn[:, :], clips[:, :])
        core.end_layer()
        with ExitStack() as ctx:
            sb = lambda n, shape, dt=F32: core.sb(ctx, n, shape, dt)
            w, worep, wot = sb("a3_w", [P, 3, D]), sb("a3_worep", [P, HEADS, D + 1]), sb("a3_wot", [P, D])
            cols, bo = sb("a3_cols", [P, 3]), sb("a3_bo", [P, D])
            mask, maskT = sb("a3_mask", [P, 2, SC]), sb("a3_maskT", [P, KT, S], BF16)
            with ExitStack() as inner:
                seen = core.sb(inner, "a3_seen", [P, 2, SC], I32)
                seenT = core.sb(inner, "a3_seenT", [P, KT, S], I32)
                layernorm_stage(core, "ln3a", core.x, core.xn, core.xnT, loads=[
                    (w[:, :, :], inp["a3_w"]), (worep[:, :, :], inp["a3_worep"]), (wot[:, :], inp["a3_wot"]),
                    (cols[:, :], inp["a3_cols"]), (bo[:, :], inp["a3_bo"].partition_broadcast(P)),
                    (seen[:, :, :], inp["mask3"].rearrange("(t p) k -> p t k", p=P)),
                    (seenT[:, :, :], inp["mask3T"].rearrange("(t p) q -> p t q", p=P))])
                scaled3 = core.sem("a3_mask_scaled")
                with nc.Block() as block:
                    @block.vector
                    def _(dve):
                        dve.tensor_scalar(mask[:, :, :], seen[:, :, :], 0.0, MASKED, ALU.is_equal,
                                          ALU.mult).then_inc(scaled3, 1)
                        dve.tensor_scalar(maskT[:, :, :], seenT[:, :, :], 0.0, MASKED, ALU.is_equal,
                                          ALU.mult).then_inc(scaled3, 1)
                        dve.wait_ge(scaled3, 2)
            small_head_layer(core, "a3", core.x, lambda qt, at, n: mask[:, qt, at:at + n],
                             (lambda kt: maskT[:, kt, :],), True,
                             w, worep, cols, cols[:, 2:3], wot[:, :], bo[:, :])
        core.end_layer()
        with ExitStack() as ctx:
            sb = lambda n, shape, dt=F32: core.sb(ctx, n, shape, dt)
            u1, v1, b1 = sb("f3_u1", [P, RANK]), sb("f3_v1", [RANK, FF3]), sb("f3_b1", [P, FF3 // P])
            u2, v2, b2 = sb("f3_u2", [P, FF3 // P, RANK]), sb("f3_v2", [RANK, D]), sb("f3_b2", [P, D])
            layernorm_stage(core, "ln3f", core.x, core.xn, core.xnT, loads=[
                (u1[:, :], inp["f3_u1"]), (v1[:, :], inp["f3_v1"]), (b1[:, :], inp["f3_b1"]),
                (u2[:, :, :], inp["f3_u2"]), (v2[:, :], inp["f3_v2"]), (b2[:, :], inp["f3_b2"].partition_broadcast(P))])
            ffn3_stage(core, u1[:, :], v1[:, :], b1, u2, v2[:, :], b2[:, :])


def lay_out(inputs):
    g = {k: np.asarray(v) for k, v in inputs.items()}
    a = {"x": g["x"].reshape(B * S, D), "ident": np.eye(P, dtype=np.float32)}
    ctxT = np.zeros((P, B, SCP), np.float32)
    ctxT[:, :, :SC] = g["ctx_1024"].transpose(2, 0, 1)
    a["ctxT"] = ctxT
    a["mask0"] = g["mask_SxS2_fk1"]
    a["mask3"] = g["mask_1x1xSxS2_ik0"].reshape(S, SC)
    a["mask3T"] = np.ones((SCP, S), g["mask_1x1xSxS2_ik0"].dtype)
    a["mask3T"][:SC] = a["mask3"].T
    a["rank"] = np.arange(EXPERTS, 0, -1).astype(np.float32)

    def replicate(wo_rows, dh, sums=0):
        H = wo_rows.shape[0] // dh
        tile = max(dh, 32)
        out = np.zeros((P, H, D + sums), np.float32)
        for j in range(P // tile):
            if sums:
                out[j * tile + dh, :, D] = 1.0
            out[j * tile:j * tile + dh, :, :D] = wo_rows.reshape(H, dh, D).transpose(1, 0, 2)
        return out

    for n, pre in (("a0", "L0_xattn_"), ("a3", "L3_xattn_")):
        a[n + "_w"] = np.stack([g[pre + k].T for k in ("Wq", "Wk", "Wv")], 1)
        a[n + "_worep"] = replicate(g[pre + "Wo"].T, 8, 1)
        a[n + "_wot"] = g[pre + "Wo"].T
        a[n + "_cols"] = np.stack([g[pre + k] for k in ("bq", "bk", "bv")], 1)
        a[n + "_bo"] = g[pre + "bo"]
    a["f0_w"] = np.stack([g["L0_ffn_w_gate"].T, g["L0_ffn_w_up"].T,
                          g["L0_ffn_w_down"].T.reshape(4, P, D).transpose(1, 0, 2).reshape(P, FF0)], 1)
    a["a1_wq"], a["a1_wk"], a["a1_wv"] = g["L1_xattn_Wq"].T, g["L1_xattn_Wk"], g["L1_xattn_Wv"].T
    a["a1_wot"], a["a1_bo"] = g["L1_xattn_Wo"].T, g["L1_xattn_bo"]
    a["a1_cols"] = np.stack([g["L1_xattn_bq"], g["L1_xattn_bv"]], 1)
    a["m1_w"] = g["L1_ffn_w_qkv"].reshape(D, 3, D)
    a["m1_worep"] = replicate(g["L1_ffn_w_proj"], 8, 1)
    for k in ("ln1_w", "ln1_b", "ln2_w", "ln2_b"):
        a[k] = g["L1_ffn_" + k]
    a["e1_gw"], a["e1_gb"] = g["L1_ffn_gate_w"], g["L1_ffn_gate_b"]
    a["e1_w1"] = g["L1_ffn_w1"]
    a["e1_w2"] = g["L1_ffn_w2"].reshape(EXPERTS, 4, P, D).transpose(0, 2, 1, 3)
    a["a2_wq"] = g["L2_xattn_w_q"].reshape(D, 8, P).transpose(1, 0, 2)
    wk = np.zeros((8, P, 2, P), np.float32)
    rows = g["L2_xattn_w_k"].T.reshape(8, 2, 64, D)
    for j in range(2):
        wk[:, 64 * j:64 * (j + 1), j] = rows[:, j]
    a["a2_wk"] = wk
    a["a2_wv"] = g["L2_xattn_w_v"]
    a["a2_worep"] = replicate(g["L2_xattn_w_o"], 64)
    gu = np.ones((2, 3 * P, D), np.float32)
    gu[0, :FF2], gu[1, :FF2] = g["L2_ffn_w_gate"], g["L2_ffn_w_up"]
    a["f2_wgu"] = gu.reshape(6, P, D).transpose(1, 0, 2)
    a["f2_wdn"] = g["L2_ffn_w_down"]
    a["f2_clip_x"], a["f2_clip_down"] = g["L2_ffn_clip_x"], g["L2_ffn_clip_down"]
    a["f3_u1"], a["f3_v1"] = g["L3_ffn_U1"], g["L3_ffn_V1"]
    a["f3_b1"] = g["L3_ffn_b1"].reshape(4, P).T
    a["f3_u2"] = g["L3_ffn_U2"].reshape(4, P, RANK).transpose(1, 0, 2)
    a["f3_v2"], a["f3_b2"] = g["L3_ffn_V2"], g["L3_ffn_b2"]
    return {k: np.ascontiguousarray(v) for k, v in a.items()}


def kernel(**inputs):
    import concourse.bacc as bacc
    from concourse.bass_utils import run_bass_kernel_spmd

    nc = bacc.Bacc("TRN2", target_bir_lowering=False, num_devices=1)
    arrays = lay_out(inputs)
    inp = {n: nc.dram_tensor("in_" + n, a.shape, mybir.dt.from_np(a.dtype), kind="ExternalInput").ap()
           for n, a in arrays.items()}
    inp["out"] = nc.dram_tensor("out_x", (B * S, D), F32, kind="ExternalOutput").ap()
    build(nc, inp)
    r = run_bass_kernel_spmd(nc, [{"in_" + n: a for n, a in arrays.items()}], core_ids=[0])
    return r.results[0]["out_x"].reshape(B, S, D)
```
